# Optimizing a Trainium2 kernel written in Bass

```python
import numpy as np
import jax
import jax.numpy as jnp

def _softmax(x, axis=-1):
    return jax.nn.softmax(x, axis=axis)

def _gelu(x):
    return jax.nn.gelu(x, approximate=True)

def _silu(x):
    return jax.nn.silu(x)

def _sigmoid(x):
    return jax.nn.sigmoid(x)

def _layernorm(x, axis=-1, eps=1e-05):
    m = jnp.mean(x, axis=axis, keepdims=True)
    v = jnp.var(x, axis=axis, keepdims=True)
    return (x - m) / jnp.sqrt(v + eps)

def _scatter_add(tgt, idx, src, axis=0):
    return tgt.at[idx].add(src)

def _segment_sum(src, seg, n):
    return jax.ops.segment_sum(src, seg, n)
kernel_name = 'mk_vit_tower_cls_d2_tok_img1024_r4_31660a'

def setup_inputs(seed: int=0):
    np.random.seed(seed)
    _w = jnp.asarray

    def _rec_inputs():
        import jax
        import jax.numpy as jnp
        _rk = jax.random.key(seed)
        x = -0.00016672 + 0.999947 * jax.random.normal(jax.random.fold_in(_rk, 1), (16, 3, 96, 96), jnp.float32)
        cls_tok = 0.02 * jax.random.normal(jax.random.fold_in(_rk, 5), (1, 1, 256), jnp.float32)
        return (x, cls_tok)
    x, cls_tok = _rec_inputs()

    def _L0_tok_setup():
        import jax, jax.numpy as jnp
        import numpy as np
        DIM = 256
        IMG = 96
        P = 16
        C = 3
        TEMP = 10000.0
        EPS = 1e-05
        PATCH_DIM = C * P * P
        HP = IMG // P

        def layernorm(x, gamma, beta):
            mu = jnp.mean(x, axis=-1, keepdims=True)
            var = jnp.var(x, axis=-1, keepdims=True)
            return (x - mu) * jax.lax.rsqrt(var + EPS) * gamma + beta

        def posemb_sincos_2d(h, w, dim, dtype):
            y, x = jnp.meshgrid(jnp.arange(h), jnp.arange(w), indexing='ij')
            omega = jnp.arange(dim // 4, dtype=jnp.float32) / (dim // 4 - 1)
            omega = 1.0 / TEMP ** omega
            y = y.reshape(-1)[:, None] * omega[None, :]
            x = x.reshape(-1)[:, None] * omega[None, :]
            pe = jnp.concatenate((jnp.sin(x), jnp.cos(x), jnp.sin(y), jnp.cos(y)), axis=1)
            return pe.astype(dtype)
        key = jax.random.key(seed)
        ks = jax.random.split(key, 8)
        B = 64
        img = jax.random.normal(ks[0], (B, C, IMG, IMG), dtype=jnp.float32)
        cls_token = jax.random.normal(ks[1], (1, 1, DIM), dtype=jnp.float32)
        cls_pos_embedding = jax.random.normal(ks[2], (1, 1, DIM), dtype=jnp.float32)
        ln1_g = jnp.ones((PATCH_DIM,), jnp.float32)
        ln1_b = jnp.zeros((PATCH_DIM,), jnp.float32)
        W = jax.random.normal(ks[3], (PATCH_DIM, DIM), dtype=jnp.float32) / np.sqrt(PATCH_DIM)
        bias = jnp.zeros((DIM,), jnp.float32)
        ln2_g = jnp.ones((DIM,), jnp.float32)
        ln2_b = jnp.zeros((DIM,), jnp.float32)
        return {'img': img, 'cls_token': cls_token, 'cls_pos_embedding': cls_pos_embedding, 'ln1_g': ln1_g, 'ln1_b': ln1_b, 'W': W, 'bias': bias, 'ln2_g': ln2_g, 'ln2_b': ln2_b}
    _L0_tok_all = _L0_tok_setup()
    _L0_tok_in = {k: v for k, v in _L0_tok_all.items() if k in ('cls_token', 'cls_pos_embedding', 'ln1_g', 'ln1_b', 'W', 'bias', 'ln2_g', 'ln2_b')}
    del _L0_tok_all

    def _L0_attn_setup():
        import jax, jax.numpy as jnp
        import numpy as np
        import math
        D_MODEL = 256
        NUM_HEADS = 16
        B, L = (2, 512)
        PERIODS = (1.0, 30.0)
        WEIGHTS = (0.8, 0.4)
        SIGMAS = (0.5, 2.0)

        def _gaussian_mask(length):
            idx = jnp.arange(length, dtype=jnp.float32)
            delta = jnp.abs(idx[:, None] - idx[None, :])
            mask = jnp.zeros_like(delta)
            for p, w, sigma in zip(PERIODS, WEIGHTS, SIGMAS):
                if p < 0.2:
                    continue
                mask = mask + w * jnp.exp(-(delta - p) ** 2 / (2.0 * sigma ** 2))
            return mask
        key = jax.random.key(seed)
        ks = jax.random.split(key, 10)
        s = 1.0 / math.sqrt(D_MODEL)
        inp = {'x': jax.random.normal(ks[0], (B, L, D_MODEL), dtype=jnp.float32), 'Wq': jax.random.normal(ks[1], (D_MODEL, D_MODEL), dtype=jnp.float32) * s, 'bq': jax.random.normal(ks[2], (D_MODEL,), dtype=jnp.float32) * 0.01, 'Wk': jax.random.normal(ks[3], (D_MODEL, D_MODEL), dtype=jnp.float32) * s, 'bk': jax.random.normal(ks[4], (D_MODEL,), dtype=jnp.float32) * 0.01, 'Wv': jax.random.normal(ks[5], (D_MODEL, D_MODEL), dtype=jnp.float32) * s, 'bv': jax.random.normal(ks[6], (D_MODEL,), dtype=jnp.float32) * 0.01, 'Wo': jax.random.normal(ks[7], (D_MODEL, D_MODEL), dtype=jnp.float32) * s, 'bo': jax.random.normal(ks[8], (D_MODEL,), dtype=jnp.float32) * 0.01, 'prior_lambda': jnp.asarray(2.0, dtype=jnp.float32)}
        return inp
    _L0_attn_all = _L0_attn_setup()
    _L0_attn_in = {k: v for k, v in _L0_attn_all.items() if k in ('Wq', 'bq', 'Wk', 'bk', 'Wv', 'bv', 'Wo', 'bo', 'prior_lambda')}
    del _L0_attn_all

    def _L0_ffn_setup():
        import jax, jax.numpy as jnp
        import numpy as np
        T, Z, D_DIM = (8, 512, 256)
        N_EXP, P_SLOT, H = (64, 32, 256)
        LN_EPS = 1e-05
        key = jax.random.key(seed)
        k = jax.random.split(key, 5)
        s = 0.02
        return {'x': jax.random.normal(k[0], (T, Z, D_DIM), dtype=jnp.float32), 'phi_w': jax.random.normal(k[1], (N_EXP * P_SLOT, D_DIM), dtype=jnp.float32) * s, 'phi_b': jax.random.normal(k[2], (N_EXP * P_SLOT,), dtype=jnp.float32) * s, 'expert_w': jax.random.normal(k[3], (N_EXP, D_DIM, H), dtype=jnp.float32) * s, 'expert_b': jax.random.normal(k[4], (N_EXP, H), dtype=jnp.float32) * s}
    _L0_ffn_all = _L0_ffn_setup()
    _L0_ffn_in = {k: v for k, v in _L0_ffn_all.items() if k in ('phi_w', 'phi_b', 'expert_w', 'expert_b')}
    del _L0_ffn_all

    def _L1_attn_setup():
        import jax, jax.numpy as jnp
        import numpy as np
        D_MODEL = 256
        EXPAND = 2
        D_INNER = D_MODEL * EXPAND
        C = 8
        B, T = (4, 512)
        key = jax.random.key(seed)
        ks = jax.random.split(key, 8)
        x = jax.random.normal(ks[0], (B, T, D_MODEL), jnp.float32)
        a = np.log(1.0 / np.exp(np.log(0.999) / C) - 1.0)
        b = np.log(1.0 / np.exp(np.log(0.9) / C) - 1.0)
        omega = (a + (b - a) * jax.random.uniform(ks[1], (1, 1, D_INNER))).astype(jnp.float32)
        s = 0.02
        Win = (jax.random.normal(ks[2], (2 * D_INNER, D_MODEL)) * s).astype(jnp.float32)
        Wl = (jax.random.normal(ks[3], (D_INNER, D_INNER)) * s).astype(jnp.float32)
        bl = jnp.zeros((D_INNER,), jnp.float32)
        Wv = (jax.random.normal(ks[4], (D_INNER, D_INNER)) * s).astype(jnp.float32)
        bv = jnp.zeros((D_INNER,), jnp.float32)
        Wout = (jax.random.normal(ks[5], (D_MODEL, D_INNER)) * s).astype(jnp.float32)
        return dict(x=x, omega=omega, Win=Win, Wl=Wl, bl=bl, Wv=Wv, bv=bv, Wout=Wout)
    _L1_attn_all = _L1_attn_setup()
    _L1_attn_in = {k: v for k, v in _L1_attn_all.items() if k in ('omega', 'Win', 'Wl', 'bl', 'Wv', 'bv', 'Wout')}
    del _L1_attn_all

    def _L1_ffn_setup():
        import jax, jax.numpy as jnp
        import numpy as np
        CAPACITY_FACTOR = 1.25
        key = jax.random.key(seed)
        k1, k2, k3, k4 = jax.random.split(key, 4)
        B, T, D, F, E = (4, 1024, 256, 1024, 8)
        s = 0.02
        return {'x': jax.random.normal(k1, (B, T, D), dtype=jnp.float32), 'wg': jax.random.normal(k2, (D, E), dtype=jnp.float32) * s, 'W1': jax.random.normal(k3, (E, D, F), dtype=jnp.float32) * s, 'b1': jnp.zeros((E, F), dtype=jnp.float32), 'W2': jax.random.normal(k4, (E, F, D), dtype=jnp.float32) * s, 'b2': jnp.zeros((E, D), dtype=jnp.float32)}
    _L1_ffn_all = _L1_ffn_setup()
    _L1_ffn_in = {k: v for k, v in _L1_ffn_all.items() if k in ('wg', 'W1', 'b1', 'W2', 'b2')}
    del _L1_ffn_all
    return {'x': x, 'cls_tok': cls_tok, 'L0_tok_cls_token': _L0_tok_in['cls_token'], 'L0_tok_cls_pos_embedding': _L0_tok_in['cls_pos_embedding'], 'L0_tok_ln1_g': _L0_tok_in['ln1_g'], 'L0_tok_ln1_b': _L0_tok_in['ln1_b'], 'L0_tok_W': _L0_tok_in['W'], 'L0_tok_bias': _L0_tok_in['bias'], 'L0_tok_ln2_g': _L0_tok_in['ln2_g'], 'L0_tok_ln2_b': _L0_tok_in['ln2_b'], 'L0_attn_Wq': _L0_attn_in['Wq'], 'L0_attn_bq': _L0_attn_in['bq'], 'L0_attn_Wk': _L0_attn_in['Wk'], 'L0_attn_bk': _L0_attn_in['bk'], 'L0_attn_Wv': _L0_attn_in['Wv'], 'L0_attn_bv': _L0_attn_in['bv'], 'L0_attn_Wo': _L0_attn_in['Wo'], 'L0_attn_bo': _L0_attn_in['bo'], 'L0_attn_prior_lambda': _L0_attn_in['prior_lambda'], 'L0_ffn_phi_w': _L0_ffn_in['phi_w'], 'L0_ffn_phi_b': _L0_ffn_in['phi_b'], 'L0_ffn_expert_w': _L0_ffn_in['expert_w'], 'L0_ffn_expert_b': _L0_ffn_in['expert_b'], 'L1_attn_omega': _L1_attn_in['omega'], 'L1_attn_Win': _L1_attn_in['Win'], 'L1_attn_Wl': _L1_attn_in['Wl'], 'L1_attn_bl': _L1_attn_in['bl'], 'L1_attn_Wv': _L1_attn_in['Wv'], 'L1_attn_bv': _L1_attn_in['bv'], 'L1_attn_Wout': _L1_attn_in['Wout'], 'L1_ffn_wg': _L1_ffn_in['wg'], 'L1_ffn_W1': _L1_ffn_in['W1'], 'L1_ffn_b1': _L1_ffn_in['b1'], 'L1_ffn_W2': _L1_ffn_in['W2'], 'L1_ffn_b2': _L1_ffn_in['b2']}

def reference(x, cls_tok, L0_tok_cls_token, L0_tok_cls_pos_embedding, L0_tok_ln1_g, L0_tok_ln1_b, L0_tok_W, L0_tok_bias, L0_tok_ln2_g, L0_tok_ln2_b, L0_attn_Wq, L0_attn_bq, L0_attn_Wk, L0_attn_bk, L0_attn_Wv, L0_attn_bv, L0_attn_Wo, L0_attn_bo, L0_attn_prior_lambda, L0_ffn_phi_w, L0_ffn_phi_b, L0_ffn_expert_w, L0_ffn_expert_b, L1_attn_omega, L1_attn_Win, L1_attn_Wl, L1_attn_bl, L1_attn_Wv, L1_attn_bv, L1_attn_Wout, L1_ffn_wg, L1_ffn_W1, L1_ffn_b1, L1_ffn_W2, L1_ffn_b2):
    import jax
    import jax.numpy as jnp

    def _L0_tok_ref(img, cls_token, cls_pos_embedding, ln1_g, ln1_b, W, bias, ln2_g, ln2_b):
        import jax, jax.numpy as jnp
        import numpy as np
        DIM = 256
        IMG = 96
        P = 16
        C = 3
        TEMP = 10000.0
        EPS = 1e-05
        PATCH_DIM = C * P * P
        HP = IMG // P

        def layernorm(x, gamma, beta):
            mu = jnp.mean(x, axis=-1, keepdims=True)
            var = jnp.var(x, axis=-1, keepdims=True)
            return (x - mu) * jax.lax.rsqrt(var + EPS) * gamma + beta

        def posemb_sincos_2d(h, w, dim, dtype):
            y, x = jnp.meshgrid(jnp.arange(h), jnp.arange(w), indexing='ij')
            omega = jnp.arange(dim // 4, dtype=jnp.float32) / (dim // 4 - 1)
            omega = 1.0 / TEMP ** omega
            y = y.reshape(-1)[:, None] * omega[None, :]
            x = x.reshape(-1)[:, None] * omega[None, :]
            pe = jnp.concatenate((jnp.sin(x), jnp.cos(x), jnp.sin(y), jnp.cos(y)), axis=1)
            return pe.astype(dtype)
        b = img.shape[0]
        x = img.reshape(b, C, HP, P, HP, P)
        x = jnp.transpose(x, (0, 2, 4, 3, 5, 1))
        x = x.reshape(b, HP, HP, PATCH_DIM)
        x = layernorm(x, ln1_g, ln1_b)
        x = jnp.einsum('bhwp,pd->bhwd', x, W) + bias
        x = layernorm(x, ln2_g, ln2_b)
        pe = posemb_sincos_2d(HP, HP, DIM, x.dtype)
        x = x.reshape(b, HP * HP, DIM) + pe[None]
        cls_tokens = jnp.broadcast_to(cls_token + cls_pos_embedding, (b, 1, DIM))
        return jnp.concatenate((cls_tokens, x), axis=1)

    def _L0_attn_ref(x, Wq, bq, Wk, bk, Wv, bv, Wo, bo, prior_lambda):
        import jax, jax.numpy as jnp
        import numpy as np
        import math
        D_MODEL = 256
        NUM_HEADS = 16
        B, L = (2, 512)
        PERIODS = (1.0, 30.0)
        WEIGHTS = (0.8, 0.4)
        SIGMAS = (0.5, 2.0)

        def _gaussian_mask(length):
            idx = jnp.arange(length, dtype=jnp.float32)
            delta = jnp.abs(idx[:, None] - idx[None, :])
            mask = jnp.zeros_like(delta)
            for p, w, sigma in zip(PERIODS, WEIGHTS, SIGMAS):
                if p < 0.2:
                    continue
                mask = mask + w * jnp.exp(-(delta - p) ** 2 / (2.0 * sigma ** 2))
            return mask
        Bx, Lx, D = x.shape
        H = NUM_HEADS
        hd = D // H

        def split_heads(t):
            return t.reshape(Bx, Lx, H, hd).transpose(0, 2, 1, 3)
        Q = split_heads(x @ Wq.T + bq)
        K = split_heads(x @ Wk.T + bk)
        V = split_heads(x @ Wv.T + bv)
        scores = jnp.einsum('bhqd,bhkd->bhqk', Q, K) / math.sqrt(hd)
        scores = scores + prior_lambda * _gaussian_mask(Lx)[None, None, :, :]
        attn = jax.nn.softmax(scores, axis=-1)
        out = jnp.einsum('bhqk,bhkd->bhqd', attn, V)
        out = out.transpose(0, 2, 1, 3).reshape(Bx, Lx, D)
        return out @ Wo.T + bo

    def _L0_ffn_ref(x, phi_w, phi_b, expert_w, expert_b):
        import jax, jax.numpy as jnp
        import numpy as np
        T, Z, D_DIM = (8, 512, 256)
        N_EXP, P_SLOT, H = (64, 32, 256)
        LN_EPS = 1e-05
        t, z, d = x.shape
        n = expert_w.shape[0]
        p = phi_w.shape[0] // n
        logits = (jnp.einsum('tzd,ed->tze', x, phi_w) + phi_b).reshape(t, z, n, p)
        D = jax.nn.softmax(logits, axis=3)
        C = jax.nn.softmax(logits, axis=2)
        X_tilde = jnp.einsum('tznp,tzd->npd', D, x)
        X_tilde = jnp.clip(X_tilde, -33000.0, 65000.0)
        mu = jnp.mean(X_tilde, axis=-1, keepdims=True)
        var = jnp.mean(jnp.square(X_tilde - mu), axis=-1, keepdims=True)
        X_tilde = (X_tilde - mu) * jax.lax.rsqrt(var + LN_EPS)
        X_tilde = jnp.tanh(X_tilde)
        Y_tilde = jnp.einsum('npd,ndH->npH', X_tilde, expert_w) + expert_b[:, None, :]
        Y = jnp.einsum('tznp,npH->tzH', C, Y_tilde)
        return Y

    def _L1_attn_ref(x, omega, Win, Wl, bl, Wv, bv, Wout):
        import jax, jax.numpy as jnp
        import numpy as np
        D_MODEL = 256
        EXPAND = 2
        D_INNER = D_MODEL * EXPAND
        C = 8
        B, T = (4, 512)
        xz = jnp.einsum('btd,ed->bte', x, Win)
        xi, z = jnp.split(xz, 2, axis=-1)
        log_lam = -C * jax.nn.softplus(omega) * jax.nn.sigmoid(jnp.einsum('bti,ji->btj', xi, Wl) + bl)
        lam = jnp.exp(log_lam)
        v = jnp.einsum('bti,ji->btj', xi, Wv) + bv
        h0 = xi[:, 0]

        def step(h_prev, inp):
            x_t, v_t, lam_t = inp
            vh = jnp.sum(v_t * h_prev, axis=-1, keepdims=True)
            vv = jnp.sum(v_t * v_t, axis=-1, keepdims=True)
            Qh = h_prev - 2.0 * v_t * (vh / vv)
            h = lam_t * Qh + (1.0 - lam_t) * x_t
            return (h, h)
        xs = (jnp.swapaxes(xi[:, 1:], 0, 1), jnp.swapaxes(v[:, 1:], 0, 1), jnp.swapaxes(lam[:, 1:], 0, 1))
        _, hs = jax.lax.scan(step, h0, xs)
        h = jnp.concatenate([h0[:, None], jnp.swapaxes(hs, 0, 1)], axis=1)
        return jnp.einsum('bti,di->btd', jax.nn.silu(z) * h, Wout)

    def _L1_ffn_ref(x, wg, W1, b1, W2, b2):
        import jax, jax.numpy as jnp
        import numpy as np
        CAPACITY_FACTOR = 1.25
        B, T, D = x.shape
        E = wg.shape[1]
        N = B * T
        capacity = int(N / E * CAPACITY_FACTOR) + 1
        xf = x.reshape(N, D)
        logits = xf @ wg
        scores = jax.nn.softmax(logits, axis=-1)
        top1 = jnp.argmax(scores, axis=-1)
        combine_w = jnp.take_along_axis(scores, top1[:, None], axis=1)[:, 0]
        oh = jax.nn.one_hot(top1, E, dtype=jnp.int32)
        rank = jnp.take_along_axis(jnp.cumsum(oh, axis=0), top1[:, None], axis=1)[:, 0] - 1
        valid = rank < capacity
        trash = E * capacity
        slot = jnp.where(valid, top1 * capacity + rank, trash)
        buf = jnp.zeros((E * capacity + 1, D), dtype=x.dtype).at[slot].set(xf)
        eb = buf[:E * capacity].reshape(E, capacity, D)
        h = jax.nn.gelu(jnp.einsum('ecd,edf->ecf', eb, W1) + b1[:, None, :], approximate=False)
        y = jnp.einsum('ecf,efd->ecd', h, W2) + b2[:, None, :]
        yf = y.reshape(E * capacity, D)
        gathered = yf[jnp.minimum(slot, E * capacity - 1)]
        out_flat = jnp.where(valid[:, None], gathered, 0.0) * combine_w[:, None]
        return out_flat.reshape(B, T, D)
    h = _L0_tok_ref(x, L0_tok_cls_token, L0_tok_cls_pos_embedding, L0_tok_ln1_g, L0_tok_ln1_b, L0_tok_W, L0_tok_bias, L0_tok_ln2_g, L0_tok_ln2_b)
    h = jnp.concatenate([jnp.broadcast_to(cls_tok, (h.shape[0], 1, h.shape[2])), h], axis=1)
    h = h + _L0_attn_ref(_layernorm(h, axis=-1), L0_attn_Wq, L0_attn_bq, L0_attn_Wk, L0_attn_bk, L0_attn_Wv, L0_attn_bv, L0_attn_Wo, L0_attn_bo, L0_attn_prior_lambda)
    h = h + _L0_ffn_ref(_layernorm(h, axis=-1), L0_ffn_phi_w, L0_ffn_phi_b, L0_ffn_expert_w, L0_ffn_expert_b)
    h = h + _L1_attn_ref(_layernorm(h, axis=-1), L1_attn_omega, L1_attn_Win, L1_attn_Wl, L1_attn_bl, L1_attn_Wv, L1_attn_bv, L1_attn_Wout)
    h = h + _L1_ffn_ref(_layernorm(h, axis=-1), L1_ffn_wg, L1_ffn_W1, L1_ffn_b1, L1_ffn_W2, L1_ffn_b2)
    return h

_drawn_inputs = setup_inputs


def setup_inputs(seed=0):
    import zlib

    import numpy as np

    out = dict(_drawn_inputs(seed))
    spreads = {'L0_tok_ln1_g': (1.0, 0.2),
     'L0_tok_ln1_b': (0.0, 0.1),
     'L0_tok_bias': (0.0, 0.1),
     'L0_tok_ln2_g': (1.0, 0.2),
     'L0_tok_ln2_b': (0.0, 0.1),
     'L1_attn_bl': (0.0, 0.8),
     'L1_attn_bv': (0.0, 0.8),
     'L1_ffn_b1': (0.0, 0.8),
     'L1_ffn_b2': (0.0, 0.8)}
    factors = {'L0_attn_bq': 8.0,
     'L0_attn_bk': 8.0,
     'L0_attn_bv': 5.308,
     'L0_attn_bo': 5.424,
     'L0_ffn_phi_b': 8.0,
     'L1_attn_omega': 8.0,
     'L1_attn_Win': 3.917,
     'L1_attn_Wl': 8.0,
     'L1_attn_Wv': 8.0,
     'L1_attn_Wout': 3.972,
     'L1_ffn_wg': 4.023,
     'L1_ffn_W1': 5.942,
     'L1_ffn_W2': 5.56}
    for name, (base, spread) in spreads.items():
        noise = np.random.default_rng([zlib.crc32(name.encode()), seed]).standard_normal(out[name].shape)
        drawn = base * np.exp(spread * noise) if base else spread * noise
        out[name] = jnp.asarray(drawn.astype(out[name].dtype))
    for name, factor in factors.items():
        out[name] = (out[name] * factor).astype(out[name].dtype)
    return out
```

```python
from contextlib import ExitStack

import numpy as np

import concourse.bass as bass
from concourse import mybir

F32 = mybir.dt.float32
BF16 = mybir.dt.bfloat16
ALU = mybir.AluOpType
ACT = mybir.ActivationFunctionType
AX = mybir.AxisListType

P = 128
B = 16
T = 38
N = B * T
D = 256
NP = 36
PD = 768
NT = -(-N // P)
KD = D // P
KP = PD // P
ROWS = [min(P, N - P * t) for t in range(NT)]
PROWS = [min(P, B * NP - P * t) for t in range(NT)]
HN = N // 2
HT = T // 2
EPS = 1e-5
H = 16
HD = D // H
G = B // 2
PR = 64 + T
NE0 = 64
SL = 32
NS = NE0 * SL
CH = 4
CS = NS // CH
CE = CS // SL
ST = NS // P
DI = 512
KI = DI // P
E1 = 8
FF = 1024
KF = FF // P
CAP = int(N / E1 * 1.25) + 1


def bc(ap, axis, n):
    a = ap.unsqueeze(axis)
    shape = list(a.shape)
    shape[axis] = n
    return a.broadcast_to(shape)


def tower(nc, A, out, upto):
    ctx = ExitStack()
    with ctx:
        def sb(name, shape, dt=F32):
            return ctx.enter_context(nc.sbuf_tensor(name, shape, dt))

        sems = {}

        def sig(name):
            if name not in sems:
                sems[name] = ctx.enter_context(nc.semaphore(name))
            return sems[name]

        ps = ctx.enter_context(nc.psum_tensor("ps", [P, 8, 512], F32))

        h = sb("h", [P, NT, D])
        hb = sb("hb", [P, NT, D])
        xn = sb("xn", [P, NT, D])
        xnT = sb("xnT", [P, KD, N])
        ident = sb("ident", [P, P])
        ones = sb("ones", [P, P])
        neg_half = sb("neg_half", [P, NT])
        stats = sb("stats", [P, NT, 2, 6])
        mv = sb("mv", [P, NT, 2])
        veps = sb("veps", [P, NT])
        rstd = sb("rstd", [P, NT])
        regA = sb("regA", [P, 20480])
        regB = sb("regB", [P, 13400])

        def carve(reg, at, shape):
            n = int(np.prod(shape))
            ap = reg[:, at:at + n]
            names = [f"d{i}" for i in range(len(shape))]
            if len(shape) > 1:
                ap = ap.rearrange(f"p ({' '.join(names)}) -> p {' '.join(names)}",
                                  **{k: s for k, s in zip(names[1:], shape[1:])})
            return ap, at + n

        at = 0
        patch, at = carve(regA, at, [NT, PD])
        tokW, at = carve(regA, at, [KP, D])
        tokWg, at = carve(regA, at, [KP, D])
        lnb_w, at = carve(regA, at, [KP, P])
        pe2, at = carve(regA, at, [NT, D])
        brow, at = carve(regA, at, [D])
        tok_bias, at = carve(regA, at, [D])
        ln2g, at = carve(regA, at, [D])
        ln2b, at = carve(regA, at, [D])
        lng, at = carve(regA, at, [KP])
        lnb, at = carve(regA, at, [KP])
        clsA, at = carve(regA, at, [D])
        clsB, at = carve(regA, at, [D])
        assert at <= 20480
        patchT, at = carve(regB, 0, [KP, B * NP])

        w_att = sb("w_att", [P, 4, KD, D])
        wq, wk, wv, wo = (w_att[:, i] for i in range(4))
        bq = sb("bq", [P, KD])
        bk = sb("bk", [P, KD])
        bv = sb("bv", [P, KD])
        bo = sb("bo", [P, D])
        lam = sb("lam", [P, 1])
        gmask = sb("gmask", [P, T])
        headmask = sb("headmask", [P, H // KD])
        qb, at = carve(regB, 0, [KD, B, T])
        kb, at = carve(regB, at, [KD, B, T])
        kbd, at = carve(regB, at, [2, KD, 2, H // KD, T])
        soft, at = carve(regB, at, [2, H, T])
        smax, at = carve(regB, at, [2, H])
        ssum, at = carve(regB, at, [2, H])
        assert at <= 13400
        at = 0
        prob, at = carve(regA, at, [2, H, 64])
        probT, at = carve(regA, at, [2, H // 2, PR])
        vbd, at = carve(regA, at, [2, 2, H // 2, 2, HD])
        attT, at = carve(regA, at, [KD, N])

        phi = sb("phi", [P, KD, NS])
        phib = sb("phib", [P, NS])
        yt = sb("yt", [P, ST, D])
        logit, at = carve(regA, 0, [NT, NS])
        combT, at = carve(regA, at, [ST, N])
        disp, at = carve(regB, 0, [2, NT, CS])
        ew, at = carve(regB, at, [4, 4, KD, D])
        assert at <= 13400
        xt = hb[:, 0:2, :]
        xtT = hb[:, 2:4, :].rearrange("p a (k n) -> p a k n", k=KD)
        dmax = sb("dmax", [P, 2, CE])
        dsum = sb("dsum", [P, 2, CE])
        cmax = sb("cmax", [P, NT, SL])
        csum = sb("csum", [P, NT, SL])
        xmv = sb("xmv", [P, 2, 4])
        xstats = sb("xstats", [P, 2, 6])

        w_in = w_att[:].rearrange("p a k n -> p (a k n)").rearrange("p (k n) -> p k n", k=KD)
        w_lam = phi[:].rearrange("p k n -> p (k n)")[:, 0:KI * DI].rearrange("p (k n) -> p k n", k=KI)
        w_v = phi[:].rearrange("p k n -> p (k n)")[:, KI * DI:2 * KI * DI].rearrange("p (k n) -> p k n", k=KI)
        w_out = phib[:, 0:KI * D].rearrange("p (k n) -> p k n", k=KI)
        va, at = carve(regB, 0, [T, 2, KI, B])
        kk, at = carve(regB, at, [T, KI, B])
        hist, at = carve(regB, at, [T, KI, B])
        zs, at = carve(regB, at, [KI, N])
        assert at <= 13400
        xi, at = carve(regA, 16384, [T, KI, B])
        assert at <= 20480
        l1_small = sb("l1_small", [P, 3, KI])
        omega, bl, bv1 = (l1_small[:, i] for i in range(3))
        sp_t = sb("sp_t", [P, 6, KI])
        inv_vv = xn[:].rearrange("p t d -> p (t d)")[:, 0:N]
        prodg = sb("prodg", [P, 2, KI, B])
        dot = sb("dot", [P, B])
        hk = sb("hk", [P, KI, B])

        w_ff, _ = carve(regA, 0, [4, 2 * KD * FF])
        at = 0
        pick, at = carve(regB, at, [NT, E1 * CAP])
        slotT, at = carve(regB, at, [KD, E1 * CAP])
        hid, at = carve(regB, at, [2, KF, CAP])
        ysb, at = carve(regB, at, [2, D])
        diag, at = carve(regB, at, [NT, P])
        sid_row, at = carve(regB, at, [N])
        gate, at = carve(regB, at, [8, NT, E1])
        assert at <= 13400
        phiflat = phi[:].rearrange("p k n -> p (k n)")

        def pickT(e):
            if e < 6:
                return phiflat[0:CAP, e * N:(e + 1) * N]
            return phib[0:CAP, (e - 6) * N:(e - 5) * N]

        yflat = yt[:].rearrange("p s d -> p (s d)")
        slot_iota = yflat[:, 0:E1 * CAP]
        order = yflat[:, E1 * CAP:E1 * CAP + NT * N // 2].bitcast(BF16).rearrange("p (t n) -> p t n", t=NT)
        b2w = w_att[:].rearrange("p a k n -> p (a k n)").rearrange("p (e d) -> p e d", e=E1)
        wg = sb("wg", [P, KD, E1])
        b1c = sb("b1c", [P, E1, KF])
        gconst = sb("gconst", [P, 2, E1])
        oh16 = sb("oh16", [P, NT, E1], BF16)
        tok = sb("tok", [P, 8, NT])

        block = ctx.enter_context(nc.Block())

        @block.sync
        def _(sp):
            def load(name, dst, src):
                sp.dma_start(dst, src).then_inc(sig(name), 16)

            for t in range(NT):
                load(f"patch_loaded{t}", patch[0:PROWS[t], t, :], A["patches"][t * P:t * P + PROWS[t], :])
                if t == 0:
                    load("ident_loaded", ident[:], A["ident"])
                    load("ln1_loaded", lng, A["ln1_g"])
                    load("ln1_loaded", lnb, A["ln1_b"])
                    load("tokw_loaded", tokW, A["tok_w"])
            load("rows_loaded", tok_bias, A["tok_bias"].partition_broadcast(P))
            load("rows_loaded", ln2g, A["ln2_g"].partition_broadcast(P))
            load("rows_loaded", ln2b, A["ln2_b"].partition_broadcast(P))
            load("pe_loaded", pe2, A["pe"])
            load("cls_loaded", clsA[64:96], A["cls_a"])
            load("cls_loaded", clsB[64:96], A["cls_b"])
            for n, w in (("wq", wq), ("wk", wk), ("wv", wv), ("wo", wo)):
                load(n + "_loaded", w[:], A[n])
            for n, w in (("bq", bq), ("bk", bk), ("bv", bv), ("gmask", gmask), ("headmask", headmask)):
                load("att_small_loaded", w[:], A[n])
            load("att_small_loaded", bo[:], A["bo"].partition_broadcast(P))
            load("att_small_loaded", lam[:], A["lam"].partition_broadcast(P))
            if upto >= 2:
                load("l1_small_loaded", l1_small[:], A["l1_small"])
                load("phi_loaded", phi[:], A["phi"])
                load("phib_loaded", phib[:], A["phi_b"].partition_broadcast(P))
                eb = A["expert_b"].rearrange("(s j) h -> j s h", j=4)
                for j in range(4):
                    load("expert_b_loaded", yt[32 * j:32 * j + 32], eb[j].partition_broadcast(32))
                sp.wait_ge(sig("att_ready"), G)
                for s in range(ST):
                    if s == 1:
                        sp.wait_ge(sig("att_out_psum"), NT)
                        load("w_in_loaded", w_in, A["w_in"])
                    if s >= 4:
                        sp.wait_ge(sig("y_psum"), s - 3)
                    load(f"experts_loaded{s % 4}", ew[:, s % 4], A["expert_w"][s])
            if upto >= 3:
                sp.wait_ge(sig("l_psum"), CH * NT)
                load("w_lam_loaded", w_lam, A["w_lam"])
                load("w_v_loaded", w_v, A["w_v"])
                sp.wait_ge(sig("l_read"), CH * NT)
                load("w_out_loaded", w_out, A["w_out"])
            if upto >= 4:
                for n, w in (("wg", wg), ("b1c", b1c), ("gconst", gconst)):
                    load("gate_small_loaded", w[:], A[n])

                def load_expert(e):
                    ring = w_ff[:, e % 4]
                    sp.dma_start(ring[:, 0:KD * FF], A["w1"][e]).then_inc(sig(f"ff_loaded{e % 4}"), 16)
                    sp.dma_start(ring[:, KD * FF:2 * KD * FF], A["w2"][e]).then_inc(sig(f"ff_loaded{e % 4}"), 16)

                sp.wait_ge(sig("moe_psum"), NT)
                load("slot_iota_loaded", slot_iota, A["slot_iota"].partition_broadcast(P))
                load("order_loaded", order, A["order"])
                for e in range(4):
                    load_expert(e)
                sp.wait_ge(sig("z_psum1"), 8)
                load("b2_loaded", b2w, A["b2"].partition_broadcast(P))
                for e in range(4, E1):
                    sp.wait_ge(sig("ff_y_psum"), e - 3)
                    load_expert(e)
            for t in range(NT):
                sp.wait_ge(sig("h_final"), t + 1)
                sp.dma_start(out[t * P:t * P + ROWS[t], :], h[0:ROWS[t], t, :]).then_inc(sig("out_stored"), 16)
            sp.wait_ge(sig("out_stored"), 16 * NT)

        @block.vector
        def _(dve):
            steps = [0]

            def link(ins):
                steps[0] += 1
                ins.then_inc(sig("dve_step"), 1)
                dve.wait_ge(sig("dve_step"), steps[0])

            def row_stats(t, rows, parts, done):
                for i, part in enumerate(parts):
                    ins = dve.bn_stats(stats[0:rows, t, i, :], part)
                link(ins)
                n = len(parts)
                dve.bn_aggr(mv[0:rows, t, :], stats[0:rows, t, 0:n, :].rearrange("p a b -> p (a b)"))\
                    .then_inc(sig(done), 1)

            def layer_norm(k):
                for t in range(NT):
                    r = ROWS[t]
                    row_stats(t, r, [h[0:r, t, :]], "ln_var")
                for t in range(NT):
                    r = ROWS[t]
                    dve.wait_ge(sig("ln_rstd"), NT * (k - 1) + t + 1)
                    dve.tensor_scalar(xn[0:r, t, :], h[0:r, t, :], mv[0:r, t, 0:1], rstd[0:r, t:t + 1],
                                      ALU.subtract, ALU.mult).then_inc(sig("ln_xn"), 1)
                for t in (1, 3):
                    dve.wait_ge(sig("ln_T_psum"), NT * (k - 1) + t + 1)
                    dve.tensor_copy(xnT[:, :, t * P:t * P + ROWS[t]],
                                    ps[:, t, 0:KD * ROWS[t]].rearrange("p (k n) -> p k n", k=KD))\
                        .then_inc(sig("ln_xnT"), 1)

            dve.memset(neg_half[:], -0.5).then_inc(sig("neg_half_set"), 1)
            dve.memset(ones[:], 1.0).then_inc(sig("ones_set"), 1)
            dve.memset(h[64:P, NT - 1, :], 0.0)
            def normalise_patch(t):
                r = PROWS[t]
                dve.wait_ge(sig("patch_rstd"), t + 1)
                dve.tensor_scalar(patch[0:r, t, :], patch[0:r, t, :], mv[0:r, t, 0:1], rstd[0:r, t:t + 1],
                                  ALU.subtract, ALU.mult).then_inc(sig("patch_xhat"), 1)

            def patchT_copy(t):
                r = PROWS[t]
                dve.wait_ge(sig("patchT_psum"), 2 * t + 2)
                dve.tensor_copy(patchT[:, 3:6, t * P:t * P + r],
                                ps[:, (2 * t + 1) % 6, 0:3 * r].rearrange("p (k n) -> p k n", k=3))\
                    .then_inc(sig("patchT_b"), 1)

            for t in range(NT):
                dve.wait_ge(sig(f"patch_loaded{t}"), 16)
                r = PROWS[t]
                row_stats(t, r, [patch[0:r, t, 0:384], patch[0:r, t, 384:768]], "patch_var")
                if t >= 1:
                    normalise_patch(t - 1)
                if t == 2:
                    dve.wait_ge(sig("brow_psum"), 1)
                    dve.wait_ge(sig("rows_loaded"), 48)
                    dve.tensor_tensor(brow, ps[:, 6, 0:D], tok_bias, ALU.add).then_inc(sig("brow_done"), 1)
                if t >= 2:
                    patchT_copy(t - 2)
            normalise_patch(NT - 1)
            patchT_copy(NT - 2)
            dve.wait_ge(sig("brow_done"), 1)
            for t in range(NT):
                r = PROWS[t]
                if t == 1:
                    patchT_copy(NT - 1)
                dve.wait_ge(sig("z_psum"), t + 1)
                dve.tensor_tensor(h[0:r, t, :], ps[0:r, 7 - t % 2, 0:D], brow[0:r], ALU.add)\
                    .then_inc(sig("z_read"), 1)
                dve.wait_ge(sig("z_read"), t + 1)
                row_stats(t, r, [h[0:r, t, :]], "z_var")
            for t in range(NT):
                r = PROWS[t]
                dve.wait_ge(sig("z_rstd"), t + 1)
                ins = dve.tensor_scalar(h[0:r, t, :], h[0:r, t, :], mv[0:r, t, 0:1], rstd[0:r, t:t + 1],
                                        ALU.subtract, ALU.mult)
            link(ins)
            link(dve.tensor_tensor(h[:], h[:], bc(ln2g, 1, NT), ALU.mult))
            dve.wait_ge(sig("pe2_done"), 1)
            link(dve.tensor_tensor(h[:], h[:], pe2, ALU.add))
            dve.wait_ge(sig("cls_loaded"), 32)
            link(dve.tensor_tensor(h[64:96, NT - 1, :], clsA[64:96], clsB[64:96], ALU.add))

            if upto >= 1:
                layer_norm(1)
                dve.wait_ge(sig("att_small_loaded"), 16 * 7)
                dve.tensor_scalar(gmask[:], gmask[:], lam[:, 0:1], None, ALU.mult)
                for m in range(KD):
                    for n in range(2):
                        i = 2 * m + n
                        dve.wait_ge(sig("k_psum"), i + 1)
                        dve.tensor_scalar(kb[:, m, :, n * HT:(n + 1) * HT].rearrange("p b s -> p s b"),
                                          ps[:, 4 + i, 0:HN].rearrange("p (s b) -> p s b", b=B),
                                          bk[:, m:m + 1], None, ALU.add).then_inc(sig("k_ready"), 1)
                dve.wait_ge(sig("q_ready"), 4)
                dve.memset(ps[32:64, 0:4, 0:HN], 0.0).then_inc(sig("score_pad"), 1)

                def scores(g):
                    s = g % 2
                    dve.wait_ge(sig("s_psum"), g + 1)
                    if g >= 2:
                        dve.wait_ge(sig("exp_done"), g - 1)
                    dve.tensor_tensor(soft[0:PR, s].rearrange("p (f h) k -> p f h k", f=KD),
                                      ps[0:PR, 2 * s:2 * s + 2, 0:HN].rearrange("p f (h k) -> p f h k", k=T),
                                      bc(bc(gmask[0:PR], 1, H // KD), 1, KD), ALU.add)\
                        .then_inc(sig("s_read"), 1)
                    dve.wait_ge(sig("s_read"), g + 1)
                    link(dve.tensor_reduce(smax[0:PR, s], soft[0:PR, s], AX.X, ALU.max))
                    dve.tensor_tensor(soft[0:PR, s], soft[0:PR, s], bc(smax[0:PR, s], 2, T), ALU.subtract)\
                        .then_inc(sig("s_shifted"), 1)

                def normalise(g):
                    s = g % 2
                    dve.wait_ge(sig("exp_done"), g + 1)
                    link(dve.tensor_reduce(ssum[0:PR, s], prob[0:PR, s, :, 0:T], AX.X, ALU.add))
                    link(dve.reciprocal(ssum[0:PR, s], ssum[0:PR, s]))
                    dve.tensor_tensor(prob[0:PR, s, :, 0:T], prob[0:PR, s, :, 0:T], bc(ssum[0:PR, s], 2, T),
                                      ALU.mult).then_inc(sig("p_ready"), 1)

                for g in range(G):
                    scores(g)
                    if g >= 1:
                        normalise(g - 1)
                normalise(G - 1)
                for t in range(NT):
                    r = ROWS[t]
                    dve.wait_ge(sig("att_out_psum"), t + 1)
                    if t == 0:
                        dve.wait_ge(sig("hb_done"), 1)
                    ins = dve.tensor_tensor(h[0:r, t, :], ps[0:r, t, 0:D], hb[0:r, t, :], ALU.add)
                link(ins)

            if upto >= 2:
                layer_norm(2)

                def shift_logits(u):
                    c, t, q = u // NT, u % NT, u % 2
                    r = ROWS[t]
                    kept = logit[0:r, t, c * CS:(c + 1) * CS]
                    dve.wait_ge(sig("l_psum"), u + 1)
                    dve.tensor_tensor(kept, ps[0:r, q, :], phib[0:r, c * CS:(c + 1) * CS], ALU.add)\
                        .then_inc(sig("l_read"), 1)
                    dve.wait_ge(sig("l_read"), u + 1)
                    by_expert = kept.rearrange("p (n s) -> p n s", s=SL)
                    link(dve.tensor_reduce(dmax[0:r, q], by_expert, AX.X, ALU.max))
                    if c >= 2:
                        dve.wait_ge(sig("x_psum"), 2 * (c - 1))
                    dve.tensor_tensor(disp[0:r, c % 2, t].rearrange("p (n s) -> p n s", s=SL), by_expert,
                                      bc(dmax[0:r, q], 2, SL), ALU.subtract).then_inc(sig("d_shifted"), 1)

                def normalise_dispatch(u):
                    c, t, q = u // NT, u % NT, u % 2
                    r = ROWS[t]
                    e = disp[0:r, c % 2, t].rearrange("p (n s) -> p n s", s=SL)
                    dve.wait_ge(sig("d_exp"), u + 1)
                    link(dve.tensor_reduce(dsum[0:r, q], e, AX.X, ALU.add))
                    link(dve.reciprocal(dsum[0:r, q], dsum[0:r, q]))
                    dve.tensor_tensor(e, e, bc(dsum[0:r, q], 2, SL), ALU.mult).then_inc(sig("d_ready"), 1)

                def slot_inputs(s):
                    q = s % 2
                    dve.wait_ge(sig("x_psum"), s // 2 + 1)
                    if s >= 2:
                        dve.wait_ge(sig("xT_psum"), s - 1)
                    dve.tensor_scalar(xt[:, q], ps[:, 2 + s % 4 // 2, D * q:D * q + D], -33000.0, 65000.0,
                                      ALU.max, ALU.min).then_inc(sig("x_read"), 1)
                    dve.wait_ge(sig("x_read"), s + 1)
                    link(dve.bn_stats(xstats[:, q], xt[:, q]))
                    dve.bn_aggr(xmv[:, q, 0:2], xstats[:, q]).then_inc(sig("x_var"), 1)

                def slot_scale(s):
                    q = s % 2
                    dve.wait_ge(sig("x_rstd"), s + 1)
                    dve.scalar_tensor_tensor(xmv[:, q, 3:4], xmv[:, q, 0:1], -1.0, xmv[:, q, 2:3], ALU.mult, ALU.mult)\
                        .then_inc(sig("x_scale"), 1)

                def expert_outputs(s):
                    dve.wait_ge(sig("y_psum"), s + 1)
                    dve.tensor_tensor(yt[:, s], ps[:, 5, 0:D], yt[:, s], ALU.add).then_inc(sig("y_read"), 1)

                def slots(c):
                    for i in range(4):
                        s = 4 * c + i
                        slot_inputs(s)
                        slot_scale(s)
                        if i:
                            expert_outputs(s - 1)
                    expert_outputs(4 * c + 3)

                def shift_combine(t):
                    r = ROWS[t]
                    by_place = logit[0:r, t].rearrange("p (n s) -> p s n", s=SL)
                    by_expert = logit[0:r, t].rearrange("p (n s) -> p n s", s=SL)
                    link(dve.tensor_reduce(cmax[0:r, t], by_place, AX.X, ALU.max))
                    dve.tensor_tensor(by_expert, by_expert, bc(cmax[0:r, t], 1, NE0), ALU.subtract)\
                        .then_inc(sig("c_shifted"), 1)

                def normalise_combine(t):
                    r = ROWS[t]
                    by_place = logit[0:r, t].rearrange("p (n s) -> p s n", s=SL)
                    by_expert = logit[0:r, t].rearrange("p (n s) -> p n s", s=SL)
                    dve.wait_ge(sig("c_exp"), t + 1)
                    link(dve.tensor_reduce(csum[0:r, t], by_place, AX.X, ALU.add))
                    link(dve.reciprocal(csum[0:r, t], csum[0:r, t]))
                    dve.tensor_tensor(by_expert, by_expert, bc(csum[0:r, t], 1, NE0), ALU.mult)\
                        .then_inc(sig("c_ready"), 1)

                dve.wait_ge(sig("phib_loaded"), 16)
                dve.wait_ge(sig("expert_b_loaded"), 64)
                for u in range(CH * NT):
                    shift_logits(u)
                    if u >= 1:
                        normalise_dispatch(u - 1)
                    if u % NT == NT - 1 and u // NT >= 1:
                        slots(u // NT - 1)
                normalise_dispatch(CH * NT - 1)
                shift_combine(0)
                slots(CH - 1)
                for t in range(NT):
                    if t + 1 < NT:
                        shift_combine(t + 1)
                    normalise_combine(t)
                for t in range(NT):
                    r = ROWS[t]
                    dve.wait_ge(sig("moe_psum"), t + 1)
                    ins = dve.tensor_tensor(h[0:r, t, :], ps[0:r, t, 0:D], h[0:r, t, :], ALU.add)
                link(ins)

            if upto >= 3:
                layer_norm(3)

                def halves(n, m, whole):
                    return whole[:, n * HT:(n + 1) * HT, m, :]

                def tokens(i):
                    return ps[:, i, 0:HN].rearrange("p (s b) -> p s b", b=B)

                absneg, e, lnw, wm1, inv, sp_out = (sp_t[:, i] for i in range(6))
                dve.wait_ge(sig("l1_small_loaded"), 16)
                link(dve.tensor_scalar(absneg, omega, -1.0, None, ALU.mult))
                dve.tensor_tensor(absneg, absneg, omega, ALU.min).then_inc(sig("sp_abs"), 1)
                dve.wait_ge(sig("sp_exp"), 1)
                dve.tensor_scalar(wm1, e, 1.0, None, ALU.add).then_inc(sig("sp_w"), 1)
                dve.wait_ge(sig("sp_ln"), 1)
                link(dve.tensor_scalar(wm1, wm1, -1.0, None, ALU.add))
                link(dve.tensor_scalar(inv, wm1, 1e-30, None, ALU.max))
                link(dve.reciprocal(inv, inv))
                link(dve.tensor_tensor(lnw, lnw, inv, ALU.mult))
                link(dve.tensor_tensor(lnw, lnw, e, ALU.mult))
                link(dve.tensor_scalar(inv, wm1, 0.0, None, ALU.is_equal))
                link(dve.tensor_tensor(inv, inv, e, ALU.mult))
                link(dve.tensor_scalar(wm1, wm1, 0.0, None, ALU.is_gt))
                link(dve.tensor_tensor(lnw, lnw, wm1, ALU.mult))
                link(dve.tensor_tensor(lnw, lnw, inv, ALU.add))
                link(dve.tensor_scalar(sp_out, omega, 0.0, None, ALU.max))
                link(dve.tensor_tensor(sp_out, sp_out, lnw, ALU.add))
                dve.tensor_scalar(sp_out, sp_out, -8.0, None, ALU.mult).then_inc(sig("decay_ready"), 1)
                for i in range(1, 8, 2):
                    dve.wait_ge(sig("xi_psum"), i + 1)
                    dve.tensor_copy(halves(i % 2, i // 2, xi), tokens(i)).then_inc(sig("xi_odd"), 1)
                for i in range(8):
                    dve.wait_ge(sig("v_psum1"), i + 1)
                    dve.tensor_scalar(halves(i % 2, i // 2, va[:, :, 0]), tokens(i), bv1[:, i // 2:i // 2 + 1], None,
                                      ALU.add).then_inc(sig("v_ready1"), 1)
                for n in range(2):
                    dve.wait_ge(sig("vv_psum"), n + 1)
                    ins = dve.reciprocal(inv_vv[:, n * HN:(n + 1) * HN], ps[:, n, 0:HN])
                ins.then_inc(sig("vv_read"), 1)
                dve.wait_ge(sig("lam_ready"), 8)
                dve.tensor_copy(hist[:, T - 2], xi[:, T - 2]).then_inc(sig("h0_copied"), 1)
                def flat(a):
                    return a.rearrange("p s k b -> p s (k b)")
                link(dve.scalar_tensor_tensor(flat(kk), flat(va[:, :, 0]), -2.0, flat(va[:, :, 1]), ALU.mult, ALU.mult))
                dve.wait_ge(sig("vv_read"), 1)
                link(dve.tensor_tensor(kk, kk, bc(inv_vv.rearrange("p (s b) -> p s b", b=B), 2, KI), ALU.mult))
                dve.wait_ge(sig("h0_copied"), 1)
                link(dve.scalar_tensor_tensor(flat(xi), flat(va[:, :, 1]), -1.0, flat(xi), ALU.add, ALU.mult))
                for i in range(8):
                    dve.wait_ge(sig("z_sig"), i + 1)
                    zh = zs[:, i // 2, (i % 2) * HN:(i % 2 + 1) * HN]
                    ins = dve.tensor_tensor(zh, ps[:, i, 0:HN], zh, ALU.mult)
                ins.then_inc(sig("z_read1"), 1)

                def step(place, before, nth):
                    dve.tensor_tensor(prodg[:], va[:, place], bc(hist[:, before], 1, 2), ALU.mult)\
                        .then_inc(sig("rnn_prod"), 1)
                    dve.wait_ge(sig("rnn_prod"), nth)
                    dve.tensor_reduce(dot[:], prodg[:, 0].rearrange("p k b -> p b k"), AX.X, ALU.add)\
                        .then_inc(sig("rnn_dot"), 1)
                    dve.tensor_tensor(prodg[:, 1], prodg[:, 1], xi[:, place], ALU.subtract).then_inc(sig("rnn_decayed"), 1)
                    dve.wait_ge(sig("rnn_sum"), nth)
                    dve.tensor_tensor(hk[:], kk[:, place], bc(ps[:, 0, 0:B], 1, KI), ALU.mult).then_inc(sig("rnn_turned"), 1)
                    dve.wait_ge(sig("rnn_turned"), nth)
                    dve.tensor_tensor(hist[:, place], hk[:], prodg[:, 1], ALU.add).then_inc(sig("rnn_state"), 1)
                    dve.wait_ge(sig("rnn_state"), nth)

                step(T - 1, T - 2, 1)
                step(0, T - 1, 2)
                for place in range(1, T - 2):
                    step(place, place - 1, place + 2)
                for k in range(KI):
                    zk = zs[:, k].rearrange("p (s b) -> p s b", b=B)
                    ins = dve.tensor_tensor(zk, zk, hist[:, :, k], ALU.mult)
                ins.then_inc(sig("gated"), 1)
                for t in range(NT):
                    r = ROWS[t]
                    dve.wait_ge(sig("rnn_out_psum"), t + 1)
                    ins = dve.tensor_tensor(h[0:r, t, :], ps[0:r, t, 0:D], h[0:r, t, :], ALU.add)
                link(ins)

            if upto >= 4:
                layer_norm(4)
                lg, eq, key, oh, picked, eg = (gate[:, i] for i in range(6))
                top, kmax, sumexp, cw, rank, sid, valid, _ = (tok[:, i] for i in range(8))
                dve.wait_ge(sig("gate_psum"), 1)
                dve.wait_ge(sig("gate_small_loaded"), 48)
                link(dve.tensor_copy(lg, ps[:, 5, 0:NT * E1].rearrange("p (t e) -> p t e", e=E1)))
                link(dve.tensor_reduce(top, lg, AX.X, ALU.max))
                dve.tensor_tensor(lg, lg, bc(top, 2, E1), ALU.subtract).then_inc(sig("gate_shifted"), 1)
                dve.wait_ge(sig("gate_shifted"), 1)
                link(dve.tensor_scalar(eq, lg, 0.0, None, ALU.is_equal))
                link(dve.tensor_tensor(key, eq, bc(gconst[:, 0], 1, NT), ALU.mult))
                link(dve.tensor_reduce(kmax, key, AX.X, ALU.max))
                link(dve.tensor_tensor(oh, key, bc(kmax, 2, E1), ALU.is_equal))
                dve.tensor_copy(oh16[:], oh).then_inc(sig("one_hot"), 1)
                dve.wait_ge(sig("gate_exp"), 1)
                link(dve.tensor_reduce(sumexp, eg, AX.X, ALU.add))
                dve.reciprocal(cw, sumexp)
                dve.wait_ge(sig("rank_psum"), 1)
                link(dve.tensor_tensor(picked, oh, ps[:, 6, 0:NT * E1].rearrange("p (t e) -> p t e", e=E1), ALU.mult))
                link(dve.tensor_reduce(rank, picked, AX.X, ALU.add))
                link(dve.tensor_scalar(valid, rank, float(CAP), None, ALU.is_le))
                link(dve.tensor_scalar(sid, kmax, -float(CAP), float(E1 * CAP), ALU.mult, ALU.add))
                link(dve.tensor_tensor(sid, sid, rank, ALU.add))
                link(dve.tensor_tensor(sid, sid, valid, ALU.mult))
                link(dve.tensor_scalar(sid, sid, -1.0, None, ALU.add))
                dve.wait_ge(sig("slot_iota_loaded"), 16)
                for t in range(NT):
                    dve.tensor_scalar(pick[:, t], slot_iota, sid[:, t:t + 1], None, ALU.is_equal)\
                        .then_inc(sig("pick_ready"), 1)
                for t in range(NT):
                    dve.tensor_scalar(diag[:, t], ident[:], sid[:, t:t + 1], None, ALU.mult)\
                        .then_inc(sig("diag_ready"), 1)
                for i in (1, 3):
                    dve.wait_ge(sig("slots_psum"), i + 1)
                    dve.tensor_copy(slotT[:, i // 2, (i % 2) * 384:(i % 2 + 1) * 384], ps[:, i, 0:384])\
                        .then_inc(sig("slots_odd"), 1)
                dve.wait_ge(sig("sid_row_ready"), 2)
                for e in range(E1):
                    dve.tensor_scalar(pickT(e), sid_row[0:CAP], gconst[0:CAP, 1, e:e + 1], None, ALU.is_equal)\
                        .then_inc(sig("pickT_ready"), 1)
                dve.wait_ge(sig("b2_loaded"), 16)
                for e in range(E1):
                    dve.wait_ge(sig("ff_y_psum"), e + 1)
                    if e >= 2:
                        dve.wait_ge(sig("ff_added"), e - 1)
                    dve.tensor_tensor(ysb[0:CAP, e % 2], ps[0:CAP, 7, 0:D], b2w[0:CAP, e], ALU.add)\
                        .then_inc(sig("ff_y_ready"), 1)
                for t in range(NT):
                    r = ROWS[t]
                    dve.wait_ge(sig("ff_out_psum"), t + 1)
                    dve.scalar_tensor_tensor(h[0:r, t], ps[0:r, t, 0:D], cw[0:r, t:t + 1], h[0:r, t],
                                             ALU.mult, ALU.add).then_inc(sig("h_final"), 1)

            for t in range(NT if upto < 4 else 0):
                dve.memset(ones[:, t:t + 1], 1.0).then_inc(sig("h_final"), 1)

        @block.gpsimd
        def _(pool):
            steps = [0]

            def link(ins):
                steps[0] += 1
                ins.then_inc(sig("pool_step"), 1)
                pool.wait_ge(sig("pool_step"), steps[0])

            def inv_sqrt(t, rows, ready, done, base=0):
                pool.wait_ge(sig(ready), base + t + 1)
                link(pool.tensor_scalar(veps[0:rows, t:t + 1], mv[0:rows, t, 1:2], EPS, None, ALU.add))
                pool.tensor_tensor(rstd[0:rows, t:t + 1], veps[0:rows, t:t + 1], neg_half[0:rows, t:t + 1],
                                   ALU.pow).then_inc(sig(done), 1)

            pool.wait_ge(sig("neg_half_set"), 1)
            for t in range(NT):
                inv_sqrt(t, PROWS[t], "patch_var", "patch_rstd")
            pool.wait_ge(sig("pe_loaded"), 16)
            pool.wait_ge(sig("rows_loaded"), 48)
            pool.tensor_tensor(pe2, pe2, bc(ln2b, 1, NT), ALU.add).then_inc(sig("pe2_done"), 1)
            for t in range(NT):
                inv_sqrt(t, PROWS[t], "z_var", "z_rstd")
            if upto >= 1:
                for t in range(NT):
                    inv_sqrt(t, ROWS[t], "ln_var", "ln_rstd", 0 * NT)
                pool.wait_ge(sig("att_small_loaded"), 16 * 7)
                for t in range(NT):
                    r = ROWS[t]
                    ins = pool.tensor_tensor(hb[0:r, t, :], h[0:r, t, :], bo[0:r], ALU.add)
                ins.then_inc(sig("hb_done"), 1)
                pool.wait_ge(sig("xnT_all"), 1) if False else None
                ins = pool.memset(prob[:, :, :, T:64], 0.0)
                ins = pool.memset(vbd, 0.0)
                ins.then_inc(sig("att_pads"), 1)
                pool.wait_ge(sig("k_ready"), 4)
                for g in range(G):
                    s = g % 2
                    if g >= 2:
                        pool.wait_ge(sig("s_psum"), g - 1)
                    for f in range(KD):
                        for i in range(2):
                            ins = pool.tensor_tensor(kbd[:, s, f, i], bc(kb[:, f, 2 * g + i], 1, H // KD),
                                                     bc(headmask[:], 2, T), ALU.mult)
                    ins.then_inc(sig("kbd_ready"), 1)

            if upto >= 2:
                for t in range(NT):
                    inv_sqrt(t, ROWS[t], "ln_var", "ln_rstd", 1 * NT)
                for s in range(ST):
                    q = s % 2
                    pool.wait_ge(sig("x_var"), s + 1)
                    link(pool.tensor_scalar(veps[:, q:q + 1], xmv[:, q, 1:2], EPS, None, ALU.add))
                    pool.tensor_tensor(xmv[:, q, 2:3], veps[:, q:q + 1], neg_half[:, 0:1], ALU.pow)\
                        .then_inc(sig("x_rstd"), 1)

            if upto >= 3:
                for t in range(NT):
                    inv_sqrt(t, ROWS[t], "ln_var", "ln_rstd", 2 * NT)

            if upto >= 4:
                for t in range(NT):
                    inv_sqrt(t, ROWS[t], "ln_var", "ln_rstd", 3 * NT)

        @block.scalar
        def _(act):
            steps = [0]

            def link(ins):
                steps[0] += 1
                ins.then_inc(sig("act_step"), 1)
                act.wait_ge(sig("act_step"), steps[0])

            def transposed_copies(k):
                for t in (0, 2, 4):
                    act.wait_ge(sig("ln_T_psum"), NT * (k - 1) + t + 1)
                    act.activation(xnT[:, :, t * P:t * P + ROWS[t]],
                                   ps[:, t, 0:KD * ROWS[t]].rearrange("p (k n) -> p k n", k=KD), ACT.Copy)\
                        .then_inc(sig("ln_xnT"), 1)

            act.wait_ge(sig("ln1_loaded"), 32)
            act.wait_ge(sig("tokw_loaded"), 16)
            for k in range(KP):
                ins = act.activation(tokWg[:, k, :], tokW[:, k, :], ACT.Copy, scale=lng[:, k:k + 1])
            ins.then_inc(sig("tokwg_done"), 1)
            act.activation(lnb_w, bc(lnb, 2, P), ACT.Copy).then_inc(sig("lnb_wide"), 1)
            for t in range(NT):
                r = PROWS[t]
                act.wait_ge(sig("patchT_psum"), 2 * t + 1)
                act.activation(patchT[:, 0:3, t * P:t * P + r],
                               ps[:, (2 * t) % 6, 0:3 * r].rearrange("p (k n) -> p k n", k=3), ACT.Copy)\
                    .then_inc(sig("patchT_a"), 1)

            if upto >= 1:
                act.wait_ge(sig("att_small_loaded"), 16 * 7)
                link(act.activation(bq[:], bq[:], ACT.Copy, scale=HD ** -0.5))
                transposed_copies(1)
                for m in range(KD):
                    for n in range(2):
                        i = 2 * m + n
                        act.wait_ge(sig("q_psum"), i + 1)
                        act.activation(qb[:, m, :, n * HT:(n + 1) * HT].rearrange("p b s -> p s b"),
                                       ps[:, i, 0:HN].rearrange("p (s b) -> p s b", b=B),
                                       ACT.Identity, bias=bq[:, m:m + 1], scale=HD ** -0.5)\
                            .then_inc(sig("q_ready"), 1)
                act.wait_ge(sig("att_pads"), 1)

                def values(g):
                    s = g % 2
                    act.wait_ge(sig("v_psum"), g + 1)
                    if g >= 2:
                        act.wait_ge(sig("o_psum"), g - 1)
                    for e in range(2):
                        ins = act.activation(
                            vbd[64 * e:64 * e + T, s, :, :, e, :],
                            ps[64 * e:64 * e + T, 4, 0:D].rearrange("p (i j d) -> p i j d", i=2, d=HD), ACT.Copy)
                    ins.then_inc(sig("v_ready"), 1)

                def exponent(g):
                    s = g % 2
                    act.wait_ge(sig("s_shifted"), g + 1)
                    if g >= 2:
                        act.wait_ge(sig("pT_psum"), 2 * g - 2)
                    act.activation(prob[0:PR, s, :, 0:T], soft[0:PR, s], ACT.Exp).then_inc(sig("exp_done"), 1)

                def probs(g):
                    s = g % 2
                    for f in range(2):
                        act.wait_ge(sig("pT_psum"), 2 * g + f + 1)
                        if g >= 2:
                            act.wait_ge(sig("o_psum"), g - 1)
                        act.activation(probT[:, s, 4 * f:4 * f + 4, :],
                                       ps[:, 5 + f, 0:4 * PR].rearrange("p (j q) -> p j q", q=PR), ACT.Copy)\
                            .then_inc(sig("pT_ready"), 1)

                def heads_out(g):
                    act.wait_ge(sig("o_psum"), g + 1)
                    for f in range(KD):
                        ins = act.activation(
                            attT[:, f, :].rearrange("p (s b) -> p b s", b=B)[:, 2 * g:2 * g + 2, :],
                            ps[:, 7, 2 * T * f:2 * T * (f + 1)].rearrange("p (i s) -> p i s", i=2),
                            ACT.Identity, bias=bv[:, f:f + 1])
                    ins.then_inc(sig("att_ready"), 1)

                values(0)
                exponent(0)
                for g in range(G):
                    if g + 1 < G:
                        values(g + 1)
                        exponent(g + 1)
                    probs(g)
                    heads_out(g)

            if upto >= 2:
                transposed_copies(2)

                def exp_dispatch(u):
                    c, t = u // NT, u % NT
                    r = ROWS[t]
                    act.wait_ge(sig("d_shifted"), u + 1)
                    act.activation(disp[0:r, c % 2, t], disp[0:r, c % 2, t], ACT.Exp).then_inc(sig("d_exp"), 1)

                def slots(c):
                    for i in range(4):
                        s = 4 * c + i
                        q = s % 2
                        act.wait_ge(sig("x_scale"), s + 1)
                        act.activation(xt[:, q], xt[:, q], ACT.Tanh, bias=xmv[:, q, 3:4], scale=xmv[:, q, 2:3])\
                            .then_inc(sig("x_hat"), 1)
                        act.wait_ge(sig("xT_psum"), s + 1)
                        if s >= 2:
                            act.wait_ge(sig("y_psum"), s - 1)
                        act.activation(xtT[:, q], ps[:, 4, 0:KD * P].rearrange("p (k n) -> p k n", k=KD), ACT.Copy)\
                            .then_inc(sig("xT_ready"), 1)

                def exp_combine(t):
                    r = ROWS[t]
                    act.wait_ge(sig("c_shifted"), t + 1)
                    act.activation(logit[0:r, t], logit[0:r, t], ACT.Exp).then_inc(sig("c_exp"), 1)

                def combine_copies(t):
                    r = ROWS[t]
                    for f in range(4):
                        act.wait_ge(sig("cT_psum"), 4 * t + f + 1)
                        act.activation(combT[:, 4 * f:4 * f + 4, t * P:t * P + r],
                                       ps[:, 6 + f % 2, 0:4 * r].rearrange("p (s n) -> p s n", n=r), ACT.Copy)\
                            .then_inc(sig("cT_ready"), 1)

                for u in range(CH * NT):
                    exp_dispatch(u)
                    if u % NT == NT - 1 and u // NT >= 1:
                        slots(u // NT - 1)
                exp_combine(0)
                slots(CH - 1)
                for t in range(NT):
                    if t + 1 < NT:
                        exp_combine(t + 1)
                    combine_copies(t)

            if upto >= 3:
                transposed_copies(3)

                def halves(n, m, whole):
                    return whole[:, n * HT:(n + 1) * HT, m, :]

                def tokens(i):
                    return ps[:, i, 0:HN].rearrange("p (s b) -> p s b", b=B)

                act.wait_ge(sig("sp_abs"), 1)
                act.activation(sp_t[:, 1], sp_t[:, 0], ACT.Exp).then_inc(sig("sp_exp"), 1)
                act.wait_ge(sig("sp_w"), 1)
                act.activation(sp_t[:, 2], sp_t[:, 3], ACT.Ln).then_inc(sig("sp_ln"), 1)
                for i in range(0, 8, 2):
                    act.wait_ge(sig("xi_psum"), i + 1)
                    act.activation(halves(i % 2, i // 2, xi), tokens(i), ACT.Copy).then_inc(sig("xi_even"), 1)
                for k in range(KI):
                    act.wait_ge(sig("v_ready1"), 2 * k + 2)
                    act.activation(hist[:, :, k], va[:, :, 0, k], ACT.Square).then_inc(sig("v_squared"), 1)
                for i in range(8):
                    act.wait_ge(sig("lam_psum"), i + 1)
                    act.activation(halves(i % 2, i // 2, va[:, :, 1]), tokens(i), ACT.Sigmoid,
                                   bias=bl[:, i // 2:i // 2 + 1]).then_inc(sig("lam_sig"), 1)
                for i in range(8):
                    act.wait_ge(sig("z_psum1"), i + 1)
                    act.activation(zs[:, i // 2, (i % 2) * HN:(i % 2 + 1) * HN], ps[:, i, 0:HN], ACT.Sigmoid)\
                        .then_inc(sig("z_sig"), 1)
                act.wait_ge(sig("decay_ready"), 1)
                act.wait_ge(sig("lam_sig"), 8)
                for i in range(8):
                    act.activation(halves(i % 2, i // 2, va[:, :, 1]), halves(i % 2, i // 2, va[:, :, 1]), ACT.Exp,
                                   scale=sp_t[:, 5, i // 2:i // 2 + 1]).then_inc(sig("lam_ready"), 1)

            if upto >= 4:
                transposed_copies(4)
                act.wait_ge(sig("gate_shifted"), 1)
                act.activation(gate[:, 5], gate[:, 0], ACT.Exp).then_inc(sig("gate_exp"), 1)
                for i in (0, 2):
                    act.wait_ge(sig("slots_psum"), i + 1)
                    act.activation(slotT[:, i // 2, 0:384], ps[:, i, 0:384], ACT.Copy).then_inc(sig("slots_even"), 1)
                for i, (at, n) in enumerate(((0, 4 * P), (4 * P, N - 4 * P))):
                    act.wait_ge(sig("sid_psum"), i + 1)
                    act.activation(sid_row[:, at:at + n], ps[:, 4 + i, 0:n], ACT.Copy).then_inc(sig("sid_row_ready"), 1)
                for e in range(E1):
                    if e >= 2:
                        act.wait_ge(sig("ff_y_psum"), e - 1)
                    for f in range(KF):
                        if f % 4 == 0:
                            act.wait_ge(sig("ff_h_psum"), 2 * e + f // 4 + 1)
                        ins = act.activation(hid[:, e % 2, f], ps[:, 5 + f // 4, (f % 4) * CAP:(f % 4 + 1) * CAP],
                                             ACT.Gelu, bias=b1c[:, e, f:f + 1])
                        if f % 4 == 3:
                            ins.then_inc(sig("ff_h_ready"), 1)

        @block.tensor
        def _(pe):
            def transposes(k):
                for t in range(NT):
                    r = ROWS[t]
                    pe.wait_ge(sig("ln_xn"), NT * (k - 1) + t + 1)
                    for c in range(KD):
                        ins = pe.transpose(ps[:, t, c * r:(c + 1) * r], xn[0:r, t, c * P:(c + 1) * P],
                                           ident[0:r, 0:r])
                    ins.then_inc(sig("ln_T_psum"), 1)
                pe.wait_ge(sig("ln_xnT"), NT * k)

            pe.wait_ge(sig("lnb_wide"), 1)
            pe.wait_ge(sig("tokw_loaded"), 16)
            for k in range(KP):
                ins = pe.matmul(ps[:, 6, 0:D], lnb_w[:, k, :], tokW[:, k, :], start=(k == 0), stop=(k == KP - 1))
            ins.then_inc(sig("brow_psum"), 1)
            pe.wait_ge(sig("ident_loaded"), 16)

            def patch_product(t):
                r = PROWS[t]
                pe.wait_ge(sig("patchT_a"), t + 1)
                pe.wait_ge(sig("patchT_b"), t + 1)
                if t == 0:
                    pe.wait_ge(sig("tokwg_done"), 1)
                if t == 1:
                    pe.wait_ge(sig("brow_done"), 1)
                if t >= 2:
                    pe.wait_ge(sig("z_read"), t - 1)
                for k in range(KP):
                    ins = pe.matmul(ps[0:r, 7 - t % 2, 0:D], patchT[:, k, t * P:t * P + r], tokWg[:, k, :],
                                    start=(k == 0), stop=(k == KP - 1))
                ins.then_inc(sig("z_psum"), 1)

            for t in range(NT):
                r = PROWS[t]
                pe.wait_ge(sig("patch_xhat"), t + 1)
                for f in range(2):
                    if t >= 3:
                        pe.wait_ge(sig("patchT_b" if f else "patchT_a"), t - 2)
                    for k in range(3):
                        ins = pe.transpose(ps[:, (2 * t + f) % 6, k * r:(k + 1) * r],
                                           patch[0:r, t, (3 * f + k) * P:(3 * f + k + 1) * P], ident[0:r, 0:r])
                    ins.then_inc(sig("patchT_psum"), 1)
                if t >= 1:
                    patch_product(t - 1)
            patch_product(NT - 1)

            if upto >= 1:
                transposes(1)
                for w, name, base in ((wq, "q", 0), (wk, "k", 4)):
                    pe.wait_ge(sig(f"w{name}_loaded"), 16)
                    for m in range(KD):
                        for n in range(2):
                            for k in range(KD):
                                ins = pe.matmul(ps[:, base + 2 * m + n, 0:HN], w[:, k, m * P:(m + 1) * P],
                                                xnT[:, k, n * HN:(n + 1) * HN], start=(k == 0), stop=(k == KD - 1))
                            ins.then_inc(sig(f"{name}_psum"), 1)

                def image(ap, b):
                    return ap.rearrange("p (s b) -> p b s", b=B)[:, b, :]

                def scores(g):
                    s = g % 2
                    pe.wait_ge(sig("kbd_ready"), g + 1)
                    if g >= 2:
                        pe.wait_ge(sig("s_read"), g - 1)
                    for f in range(KD):
                        for i in range(2):
                            ins = pe.matmul(ps[64 * i:64 * i + T, 2 * s + f, 0:HN], qb[:, f, 2 * g + i, :],
                                            kbd[:, s, f, i].rearrange("p h k -> p (h k)"), start=True, stop=True)
                    ins.then_inc(sig("s_psum"), 1)

                def values(g):
                    if g >= 1:
                        pe.wait_ge(sig("v_ready"), g)
                    for i in range(2):
                        for e in range(2):
                            for k in range(KD):
                                ins = pe.matmul(
                                    ps[64 * e:64 * e + T, 4, i * P:(i + 1) * P],
                                    image(xnT[:, k, :], 2 * g + i),
                                    wv[:, k, :].rearrange("p (j e d) -> p e j d", e=2, d=HD)[:, e],
                                    start=(k == 0), stop=(k == KD - 1))
                    ins.then_inc(sig("v_psum"), 1)

                def attend(g):
                    s = g % 2
                    pe.wait_ge(sig("p_ready"), g + 1)
                    for f in range(2):
                        if g >= 1:
                            pe.wait_ge(sig("pT_ready"), 2 * g - 1 + f)
                        for j in range(4):
                            hh = 2 * (4 * f + j)
                            ins = pe.transpose(ps[:, 5 + f, j * PR:(j + 1) * PR],
                                               prob[0:PR, s, hh:hh + 2, :].rearrange("p a k -> p (a k)"),
                                               ident[0:PR, 0:PR])
                        ins.then_inc(sig("pT_psum"), 1)
                    pe.wait_ge(sig("pT_ready"), 2 * g + 2)
                    pe.wait_ge(sig("v_ready"), g + 1)
                    if g >= 1:
                        pe.wait_ge(sig("att_ready"), g)
                    for f in range(2):
                        for i in range(2):
                            for j in range(4):
                                ins = pe.matmul(
                                    ps[32 * j:32 * j + 32, 7, (2 * f + i) * T:(2 * f + i + 1) * T],
                                    vbd[0:PR, s, i, 4 * f + j].rearrange("p e d -> p (e d)"),
                                    probT[0:PR, s, 4 * f + j, 64 * i:64 * i + T], start=True, stop=True)
                    ins.then_inc(sig("o_psum"), 1)

                pe.wait_ge(sig("k_ready"), 4)
                pe.wait_ge(sig("score_pad"), 1)
                pe.wait_ge(sig("wv_loaded"), 16)
                scores(0)
                values(0)
                for g in range(G):
                    if g + 1 < G:
                        scores(g + 1)
                        values(g + 1)
                    attend(g)
                pe.wait_ge(sig("att_ready"), G)
                pe.wait_ge(sig("wo_loaded"), 16)
                for t in range(NT):
                    r = ROWS[t]
                    for k in range(KD):
                        ins = pe.matmul(ps[0:r, t, 0:D], attT[:, k, t * P:t * P + r], wo[:, k, :],
                                        start=(k == 0), stop=(k == KD - 1))
                    ins.then_inc(sig("att_out_psum"), 1)

            if upto >= 2:
                transposes(2)

                def logits(u):
                    c, t, q = u // NT, u % NT, u % 2
                    r = ROWS[t]
                    if u >= 2:
                        pe.wait_ge(sig("l_read"), u - 1)
                    for k in range(KD):
                        ins = pe.matmul(ps[0:r, q, :], xnT[:, k, t * P:t * P + r], phi[:, k, c * CS:(c + 1) * CS],
                                        start=(k == 0), stop=(k == KD - 1))
                    ins.then_inc(sig("l_psum"), 1)

                def slot_inputs(c):
                    pe.wait_ge(sig("d_ready"), NT * (c + 1))
                    for i in range(4):
                        if c >= 1 and i % 2 == 0:
                            pe.wait_ge(sig("x_read"), 4 * c - 2 + i)
                        for t in range(NT):
                            r = ROWS[t]
                            ins = pe.matmul(ps[:, 2 + i // 2, D * (i % 2):D * (i % 2) + D],
                                            disp[0:r, c % 2, t, i * P:(i + 1) * P], xn[0:r, t, :],
                                            start=(t == 0), stop=(t == NT - 1))
                        if i % 2:
                            ins.then_inc(sig("x_psum"), 1)

                def experts(c):
                    for i in range(4):
                        s = 4 * c + i
                        q = s % 2
                        pe.wait_ge(sig("x_hat"), s + 1)
                        if s:
                            pe.wait_ge(sig("xT_ready"), s)
                        for k in range(KD):
                            ins = pe.transpose(ps[:, 4, k * P:(k + 1) * P], xt[:, q, k * P:(k + 1) * P], ident[:])
                        ins.then_inc(sig("xT_psum"), 1)
                        pe.wait_ge(sig("xT_ready"), s + 1)
                        pe.wait_ge(sig(f"experts_loaded{s % 4}"), 16 * (s // 4 + 1))
                        if s:
                            pe.wait_ge(sig("y_read"), s)
                        for j in range(4):
                            for k in range(KD):
                                ins = pe.matmul(ps[32 * j:32 * j + 32, 5, 0:D], xtT[:, q, k, 32 * j:32 * j + 32],
                                                ew[:, s % 4, j, k, :], start=(k == 0), stop=(k == KD - 1))
                        ins.then_inc(sig("y_psum"), 1)

                def combine_transposes(t):
                    r = ROWS[t]
                    pe.wait_ge(sig("c_ready"), t + 1)
                    for f in range(4):
                        if 4 * t + f >= 2:
                            pe.wait_ge(sig("cT_ready"), 4 * t + f - 1)
                        for i in range(4):
                            s = 4 * f + i
                            ins = pe.transpose(ps[:, 6 + f % 2, i * r:(i + 1) * r],
                                               logit[0:r, t, s * P:(s + 1) * P], ident[0:r, 0:r])
                        ins.then_inc(sig("cT_psum"), 1)

                def combine(t):
                    r = ROWS[t]
                    pe.wait_ge(sig("cT_ready"), 4 * t + 4)
                    for s in range(ST):
                        ins = pe.matmul(ps[0:r, t, 0:D], combT[:, s, t * P:t * P + r], yt[:, s, :],
                                        start=(s == 0), stop=(s == ST - 1))
                    ins.then_inc(sig("moe_psum"), 1)

                pe.wait_ge(sig("phi_loaded"), 16)
                for u in range(CH * NT):
                    logits(u)
                    if u % NT == NT - 1 and u // NT >= 1:
                        slot_inputs(u // NT - 1)
                        experts(u // NT - 1)
                slot_inputs(CH - 1)
                experts(CH - 1)
                pe.wait_ge(sig("y_read"), ST)
                for t in range(NT):
                    combine_transposes(t)
                    if t >= 1:
                        combine(t - 1)
                combine(NT - 1)

            if upto >= 3:
                transposes(3)

                def product(w, col, src, kt, bank, n, name):
                    for k in range(kt):
                        ins = pe.matmul(ps[:, bank, 0:HN], w[:, k, col:col + P], src(k, n),
                                        start=(k == 0), stop=(k == kt - 1))
                    ins.then_inc(sig(name), 1)

                def from_x(k, n):
                    return xnT[:, k, n * HN:(n + 1) * HN]

                def from_xi(k, n):
                    return xi[:, n * HT:(n + 1) * HT, k, :]

                def from_vv(k, n):
                    return hist[:, n * HT:(n + 1) * HT, k, :]

                pe.wait_ge(sig("w_in_loaded"), 16)
                for i in range(8):
                    product(w_in, (i // 2) * P, from_x, KD, i, i % 2, "xi_psum")
                pe.wait_ge(sig("xi_even"), 4)
                pe.wait_ge(sig("xi_odd"), 4)
                pe.wait_ge(sig("w_v_loaded"), 16)
                for i in range(8):
                    product(w_v, (i // 2) * P, from_xi, KI, i, i % 2, "v_psum1")
                pe.wait_ge(sig("w_lam_loaded"), 16)
                for i in range(8):
                    pe.wait_ge(sig("v_ready1"), i + 1)
                    product(w_lam, (i // 2) * P, from_xi, KI, i, i % 2, "lam_psum")
                pe.wait_ge(sig("v_squared"), KI)
                for n in range(2):
                    pe.wait_ge(sig("lam_sig"), n + 1)
                    for k in range(KI):
                        ins = pe.matmul(ps[:, n, 0:HN], ones[:], from_vv(k, n), start=(k == 0), stop=(k == KI - 1))
                    ins.then_inc(sig("vv_psum"), 1)
                for i in (2, 3, 4, 5, 6, 7, 0, 1):
                    pass
                for i in range(8):
                    pe.wait_ge(sig("lam_sig"), i + 1)
                    if i == 0:
                        pe.wait_ge(sig("vv_read"), 1)
                    product(w_in, DI + (i // 2) * P, from_x, KD, i, i % 2, "z_psum1")

                def total(nth):
                    pe.wait_ge(sig("rnn_dot"), nth)
                    pe.matmul(ps[:, 0, 0:B], ones[:], dot[:], start=True, stop=True).then_inc(sig("rnn_sum"), 1)

                pe.wait_ge(sig("z_read1"), 1)
                total(1)
                total(2)
                for place in range(1, T - 2):
                    total(place + 2)
                pe.wait_ge(sig("gated"), 1)
                pe.wait_ge(sig("w_out_loaded"), 16)
                for t in range(NT):
                    r = ROWS[t]
                    for k in range(KI):
                        ins = pe.matmul(ps[0:r, t, 0:D], zs[:, k, t * P:t * P + r], w_out[:, k, :],
                                        start=(k == 0), stop=(k == KI - 1))
                    ins.then_inc(sig("rnn_out_psum"), 1)

            if upto >= 4:
                transposes(4)
                pe.wait_ge(sig("gate_small_loaded"), 48)
                for t in range(NT):
                    r = ROWS[t]
                    for k in range(KD):
                        ins = pe.matmul(ps[0:r, 5, t * E1:(t + 1) * E1], xnT[:, k, t * P:t * P + r], wg[:, k, :],
                                        start=(k == 0), stop=(k == KD - 1))
                ins.then_inc(sig("gate_psum"), 1)
                pe.wait_ge(sig("one_hot"), 1)
                pe.wait_ge(sig("order_loaded"), 16)
                for t in range(NT):
                    r = ROWS[t]
                    for j in range(NT):
                        ins = pe.matmul(ps[0:r, 6, t * E1:(t + 1) * E1], order[0:ROWS[j], j, t * P:t * P + r],
                                        oh16[0:ROWS[j], j, :], start=(j == 0), stop=(j == NT - 1))
                ins.then_inc(sig("rank_psum"), 1)
                pe.wait_ge(sig("pick_ready"), NT)
                for i in range(4):
                    m, n = i // 2, i % 2
                    for t in range(NT):
                        r = ROWS[t]
                        ins = pe.matmul(ps[:, i, 0:384], xn[0:r, t, m * P:(m + 1) * P],
                                        pick[0:r, t, n * 384:(n + 1) * 384], start=(t == 0), stop=(t == NT - 1))
                    ins.then_inc(sig("slots_psum"), 1)
                pe.wait_ge(sig("diag_ready"), NT)
                for t in range(NT):
                    r = ROWS[t]
                    ins = pe.matmul(ps[:, 4 + t // 4, (t % 4) * P:(t % 4) * P + r], ones[0:r, :], diag[0:r, t, 0:r],
                                    start=True, stop=True)
                    if t >= 3:
                        ins.then_inc(sig("sid_psum"), 1)

                def hidden(e):
                    w1 = w_ff[:, e % 4, 0:KD * FF].rearrange("p (k f) -> p k f", k=KD)
                    pe.wait_ge(sig(f"ff_loaded{e % 4}"), 32 * (e // 4 + 1))
                    for f in range(KF):
                        if e and f % 4 == 0:
                            pe.wait_ge(sig("ff_h_ready"), 2 * e - 1 + f // 4)
                        for k in range(KD):
                            ins = pe.matmul(ps[:, 5 + f // 4, (f % 4) * CAP:(f % 4 + 1) * CAP], w1[:, k, f * P:(f + 1) * P],
                                            slotT[:, k, e * CAP:(e + 1) * CAP], start=(k == 0), stop=(k == KD - 1))
                        if f % 4 == 3:
                            ins.then_inc(sig("ff_h_psum"), 1)

                def outputs(e):
                    w2 = w_ff[:, e % 4, KD * FF:].rearrange("p (k d) -> p k d", k=KF)
                    pe.wait_ge(sig("ff_h_ready"), 2 * e + 2)
                    if e:
                        pe.wait_ge(sig("ff_y_ready"), e)
                    for f in range(KF):
                        ins = pe.matmul(ps[0:CAP, 7, 0:D], hid[:, e % 2, f], w2[:, f, :],
                                        start=(f == 0), stop=(f == KF - 1))
                    ins.then_inc(sig("ff_y_psum"), 1)

                def add_back(e):
                    pe.wait_ge(sig("ff_y_ready"), e + 1)
                    for t in range(NT):
                        r = ROWS[t]
                        ins = pe.matmul(ps[0:r, t, 0:D], pickT(e)[:, t * P:t * P + r], ysb[0:CAP, e % 2],
                                        start=(e == 0), stop=(e == E1 - 1))
                        if e == E1 - 1:
                            ins.then_inc(sig("ff_out_psum"), 1)
                    if e < E1 - 1:
                        ins.then_inc(sig("ff_added"), 1)

                pe.wait_ge(sig("slots_even"), 2)
                pe.wait_ge(sig("slots_odd"), 2)
                pe.wait_ge(sig("sid_row_ready"), 2)
                hidden(0)
                pe.wait_ge(sig("pickT_ready"), E1)
                for e in range(E1):
                    if e + 1 < E1:
                        hidden(e + 1)
                    outputs(e)
                    if e:
                        add_back(e - 1)
                add_back(E1 - 1)


def kernel(x, cls_tok, L0_tok_cls_token, L0_tok_cls_pos_embedding, L0_tok_ln1_g, L0_tok_ln1_b, L0_tok_W,
           L0_tok_bias, L0_tok_ln2_g, L0_tok_ln2_b, L0_attn_Wq, L0_attn_bq, L0_attn_Wk, L0_attn_bk, L0_attn_Wv,
           L0_attn_bv, L0_attn_Wo, L0_attn_bo, L0_attn_prior_lambda, L0_ffn_phi_w, L0_ffn_phi_b,
           L0_ffn_expert_w, L0_ffn_expert_b, L1_attn_omega, L1_attn_Win, L1_attn_Wl, L1_attn_bl, L1_attn_Wv,
           L1_attn_bv, L1_attn_Wout, L1_ffn_wg, L1_ffn_W1, L1_ffn_b1, L1_ffn_W2, L1_ffn_b2, upto=9):
    import concourse.bacc as bacc
    from concourse.bass_utils import run_bass_kernel_spmd

    def arr(a):
        return np.asarray(a)

    def tiled(w):
        w = arr(w)
        return w.reshape(w.shape[0] // P, P, w.shape[1]).transpose(1, 0, 2)

    def col(v):
        return arr(v).reshape(-1, P).T

    patches = arr(x).reshape(B, 3, 6, 16, 6, 16).transpose(2, 4, 0, 1, 3, 5).reshape(B * NP, PD)

    def by_channel(w):
        return arr(w).reshape(16 * 16, 3, -1).transpose(1, 0, 2).reshape(PD, -1)

    omega = (1.0 / 10000.0 ** (np.arange(D // 4, dtype=np.float32) / (D // 4 - 1))).astype(np.float32)
    gy, gx = np.meshgrid(np.arange(6), np.arange(6), indexing="ij")
    ya = gy.reshape(-1)[:, None] * omega[None, :]
    xa = gx.reshape(-1)[:, None] * omega[None, :]
    pe = np.concatenate((np.sin(xa), np.cos(xa), np.sin(ya), np.cos(ya)), axis=1).astype(np.float32)
    pe_rows = np.zeros((NT * P, D), np.float32)
    pe_rows[:B * NP] = np.repeat(pe, B, axis=0)
    time = (np.arange(T) + 2) % T
    delta = np.abs(time[:, None] - time[None, :]).astype(np.float32)
    gauss = np.zeros((T, T), np.float32)
    for period, weight, sigma in ((1.0, 0.8, 0.5), (30.0, 0.4, 2.0)):
        gauss = gauss + np.float32(weight) * np.exp(-(delta - np.float32(period)) ** 2 / np.float32(2.0 * sigma ** 2))
    gmask = np.zeros((P, T), np.float32)
    gmask[0:T] = gauss
    gmask[64:64 + T] = gauss
    headmask = (np.arange(P)[:, None] // HD == np.arange(H // KD)[None, :]).astype(np.float32)

    ins = {
        "patches": patches,
        "ident": np.eye(P, dtype=np.float32),
        "ln1_g": by_channel(L0_tok_ln1_g)[:, 0].reshape(KP, P).T,
        "ln1_b": by_channel(L0_tok_ln1_b)[:, 0].reshape(KP, P).T,
        "tok_w": tiled(by_channel(L0_tok_W)),
        "tok_bias": arr(L0_tok_bias), "ln2_g": arr(L0_tok_ln2_g), "ln2_b": arr(L0_tok_ln2_b),
        "pe": pe_rows.reshape(NT, P, D).transpose(1, 0, 2),
        "cls_a": np.repeat(np.concatenate([arr(cls_tok)[0], arr(L0_tok_cls_token)[0]]), B, axis=0),
        "cls_b": np.repeat(np.concatenate([np.zeros((1, D), np.float32), arr(L0_tok_cls_pos_embedding)[0]]), B, axis=0),
        "wq": tiled(arr(L0_attn_Wq).T), "wk": tiled(arr(L0_attn_Wk).T),
        "wv": tiled(arr(L0_attn_Wv).T), "wo": tiled(arr(L0_attn_Wo).T),
        "bq": col(L0_attn_bq), "bk": col(L0_attn_bk), "bv": col(L0_attn_bv), "bo": arr(L0_attn_bo),
        "lam": arr(L0_attn_prior_lambda).reshape(1), "gmask": gmask, "headmask": headmask,
    }
    ew = arr(L0_ffn_expert_w).reshape(ST, 4, KD, P, D).transpose(0, 3, 1, 2, 4)
    ins |= {"phi": tiled(arr(L0_ffn_phi_w).T), "phi_b": arr(L0_ffn_phi_b), "expert_b": arr(L0_ffn_expert_b),
            "expert_w": ew,
            "l1_small": np.stack([col(arr(L1_attn_omega).reshape(-1)), col(L1_attn_bl), col(L1_attn_bv)], axis=1),
            "w_in": tiled(arr(L1_attn_Win).T), "w_lam": tiled(arr(L1_attn_Wl).T), "w_v": tiled(arr(L1_attn_Wv).T),
            "w_out": tiled(arr(L1_attn_Wout).T)}
    rank_of = (np.arange(B)[None, :] * T + time[:, None]).reshape(-1)
    before = np.zeros((NT * P, N), np.float32)
    before[:N] = rank_of[:, None] <= rank_of[None, :]
    e8 = np.arange(E1, dtype=np.float32)
    gconst = np.zeros((P, 2, E1), np.float32)
    gconst[:, 0] = E1 - e8
    gconst[:, 1] = np.arange(P, dtype=np.float32)[:, None] + CAP * e8
    ins |= {
        "wg": tiled(L1_ffn_wg), "gconst": gconst, "slot_iota": np.arange(E1 * CAP, dtype=np.float32),
        "order": before.reshape(NT, P, N).transpose(1, 0, 2).astype(mybir.dt.np(BF16)),
        "w1": arr(L1_ffn_W1).reshape(E1, KD, P, FF).transpose(0, 2, 1, 3).reshape(E1, P, KD * FF),
        "w2": arr(L1_ffn_W2).reshape(E1, KF, P, D).transpose(0, 2, 1, 3).reshape(E1, P, KF * D),
        "b1c": arr(L1_ffn_b1).reshape(E1, KF, P).transpose(2, 0, 1), "b2": arr(L1_ffn_b2),
    }
    nc = bacc.Bacc("TRN2", target_bir_lowering=False, num_devices=1)
    arrays, A = {}, {}
    for name, a in ins.items():
        a = np.ascontiguousarray(a)
        arrays["in_" + name] = a
        A[name] = nc.dram_tensor("in_" + name, a.shape, mybir.dt.from_np(a.dtype), kind="ExternalInput").ap()
    out = nc.dram_tensor("out_rows", (N, D), F32, kind="ExternalOutput").ap()
    tower(nc, A, out, upto)
    r = run_bass_kernel_spmd(nc, [arrays], core_ids=[0])
    rows = r.results[0]["out_rows"]
    return np.ascontiguousarray(np.roll(rows.reshape(T, B, D).transpose(1, 0, 2), 2, axis=1))
```

```python
from contextlib import ExitStack

import numpy as np

import concourse.bass as bass
from concourse import mybir

F32 = mybir.dt.float32
BF16 = mybir.dt.bfloat16
ALU = mybir.AluOpType
ACT = mybir.ActivationFunctionType
AX = mybir.AxisListType

P = 128
B = 16
T = 38
N = B * T
D = 256
NP = 36
PD = 768
NT = -(-N // P)
KD = D // P
KP = PD // P
ROWS = [min(P, N - P * t) for t in range(NT)]
CLS = 2 * B
HN = N // 2
HT = T // 2
OUT_STEPS = (24, 25, 26, 27, 28, 29, 34, 35)
PIECES = (T - 1) // 4
SIDE_BANKS = [3 + q % 5 for q in range(21)]
REC = (0, 21, T)
LN_BANKS = {k: (5, 0, 1, 6, 7) if k == 3 else (5, 6, 7, 5, 6) for k in (1, 2, 3, 4)}
EPS = 1e-5
H = 16
HD = D // H
G = B // 2
PR = 64 + T
NE0 = 64
SL = 32
NS = NE0 * SL
CH = 4
CS = NS // CH
CE = CS // SL
ST = NS // P
DI = 512
KI = DI // P
E1 = 8
FF = 1024
KF = FF // P
CAP = int(N / E1 * 1.25) + 1


LOGIT_BANKS = (0, 1, 6, 7)


def slot_tile(unit):
    c, i = unit // NT - 1, unit % NT
    return 4 * c + i if 0 <= c < CH and i < 4 else None


def bc(ap, axis, n):
    a = ap.unsqueeze(axis)
    shape = list(a.shape)
    shape[axis] = n
    return a.broadcast_to(shape)


def tower(nc, A, out, upto):
    ctx = ExitStack()
    with ctx:
        def sb(name, shape, dt=F32):
            return ctx.enter_context(nc.sbuf_tensor(name, shape, dt))

        sems = {}

        def sig(name):
            if name not in sems:
                sems[name] = ctx.enter_context(nc.semaphore(name))
            return sems[name]

        ps = ctx.enter_context(nc.psum_tensor("ps", [P, 8, 512], F32))

        h = sb("h", [P, NT, D])
        hb = sb("hb", [P, NT, D])
        xn = sb("xn", [P, NT, D])
        xnT = sb("xnT", [P, KD, N])
        ident = sb("ident", [P, P])
        ones = sb("ones", [P, P])
        neg_half = sb("neg_half", [P, NT])
        stats = sb("stats", [P, NT, 2, 6])
        mv = sb("mv", [P, NT, 2])
        veps = sb("veps", [P, NT])
        rstd = sb("rstd", [P, NT])
        regA = sb("regA", [P, 20480])
        regB = sb("regB", [P, 13400])

        def carve(reg, at, shape):
            n = int(np.prod(shape))
            ap = reg[:, at:at + n]
            names = [f"d{i}" for i in range(len(shape))]
            if len(shape) > 1:
                ap = ap.rearrange(f"p ({' '.join(names)}) -> p {' '.join(names)}",
                                  **{k: s for k, s in zip(names[1:], shape[1:])})
            return ap, at + n

        at = 0
        patch, at = carve(regA, at, [NT, PD])
        tokW, at = carve(regA, at, [KP, D])
        tokWg, at = carve(regA, at, [KP, D])
        lnb_w, at = carve(regA, at, [KP, P])
        pe2, at = carve(regA, at, [NT, D])
        brow, at = carve(regA, at, [D])
        tok_bias, at = carve(regA, at, [D])
        ln2g, at = carve(regA, at, [D])
        ln2b, at = carve(regA, at, [D])
        lng, at = carve(regA, at, [KP])
        lnb, at = carve(regA, at, [KP])
        clsA, at = carve(regA, at, [D])
        clsB, at = carve(regA, at, [D])
        assert at <= 20480
        patchT, at = carve(regB, 0, [KP, N])

        w_att = sb("w_att", [P, 4, KD, D])
        wq, wk, wv, wo = (w_att[:, i] for i in range(4))
        bq = sb("bq", [P, KD])
        bk = sb("bk", [P, KD])
        bv = sb("bv", [P, KD])
        bo = sb("bo", [P, D])
        lam = sb("lam", [P, 1])
        gmask = sb("gmask", [P, T])
        headmask = sb("headmask", [P, H // KD])
        qb, at = carve(regB, 0, [KD, B, T])
        kb, at = carve(regB, at, [KD, B, T])
        kbd, at = carve(regB, at, [2, KD, 2, H // KD, T])
        soft, at = carve(regB, at, [2, H, T])
        smax, at = carve(regB, at, [2, H])
        ssum, at = carve(regB, at, [2, H])
        assert at <= 13400
        at = 0
        prob, at = carve(regA, at, [2, H, 64])
        probT, at = carve(regA, at, [2, H // 2, PR])
        vbd, at = carve(regA, at, [2, 2, H // 2, 2, HD])
        attT, at = carve(regA, at, [KD, N])

        phi = sb("phi", [P, KD, NS])
        phib = sb("phib", [P, NS])
        yt = sb("yt", [P, ST, D])
        logit, at = carve(regA, 0, [NT, NS])
        combT, at = carve(regA, at, [ST, N])
        disp, at = carve(regB, 0, [2, NT, CS])
        ew, at = carve(regB, at, [4, 4, KD, D])
        assert at <= 13400
        xt = hb[:, 0:2, :]
        xtT = hb[:, 2:4, :].rearrange("p a (k n) -> p a k n", k=KD)
        dmax = sb("dmax", [P, 2, CE])
        dsum = sb("dsum", [P, 2, CE])
        cmax = sb("cmax", [P, NT, SL])
        csum = sb("csum", [P, NT, SL])
        xmv = sb("xmv", [P, 2, 4])
        xstats = sb("xstats", [P, 2, 6])

        w_in = w_att[:].rearrange("p a k n -> p (a k n)").rearrange("p (k n) -> p k n", k=KD)
        w_lam = phi[:].rearrange("p k n -> p (k n)")[:, 0:KI * DI].rearrange("p (k n) -> p k n", k=KI)
        w_v = phi[:].rearrange("p k n -> p (k n)")[:, KI * DI:2 * KI * DI].rearrange("p (k n) -> p k n", k=KI)
        w_out = phib[:, 0:KI * D].rearrange("p (k n) -> p k n", k=KI)
        va, at = carve(regB, 0, [T, 2, KI, B])
        kk, at = carve(regB, at, [T, KI, B])
        hist, at = carve(regB, at, [T, KI, B])
        zs, at = carve(regB, at, [KI, N])
        assert at <= 13400
        xi, at = carve(regA, 16384, [T, KI, B])
        assert at <= 20480
        l1_small = sb("l1_small", [P, 3, KI])
        omega, bl, bv1 = (l1_small[:, i] for i in range(3))
        sp_t = sb("sp_t", [P, 6, KI])
        inv_vv = xn[:].rearrange("p t d -> p (t d)")[:, 0:N]
        prodg = sb("prodg", [P, 2, KI, B])
        dot = sb("dot", [P, B])
        hk = sb("hk", [P, KI, B])

        w_ff, _ = carve(regA, 0, [4, 2 * KD * FF])
        at = 0
        pick, at = carve(regB, at, [NT, E1 * CAP])
        slotT, at = carve(regB, at, [KD, E1 * CAP])
        hid, at = carve(regB, at, [2, KF, CAP])
        ysb, at = carve(regB, at, [2, D])
        diag, at = carve(regB, at, [NT, P])
        sid_row, at = carve(regB, at, [N])
        gate, at = carve(regB, at, [8, NT, E1])
        assert at <= 13400
        phiflat = phi[:].rearrange("p k n -> p (k n)")

        def pickT(e):
            if e < 6:
                return phiflat[0:CAP, e * N:(e + 1) * N]
            return phib[0:CAP, (e - 6) * N:(e - 5) * N]

        yflat = yt[:].rearrange("p s d -> p (s d)")
        slot_iota = yflat[:, 0:E1 * CAP]
        order = yflat[:, E1 * CAP:E1 * CAP + NT * N // 2].bitcast(BF16).rearrange("p (t n) -> p t n", t=NT)
        b2w = w_att[:].rearrange("p a k n -> p (a k n)").rearrange("p (e d) -> p e d", e=E1)
        wg = sb("wg", [P, KD, E1])
        b1c = sb("b1c", [P, E1, KF])
        gconst = sb("gconst", [P, 2, E1])
        oh16 = sb("oh16", [P, NT, E1], BF16)
        tok = sb("tok", [P, 8, NT])

        block = ctx.enter_context(nc.Block())

        @block.sync
        def _(sp):
            def load(name, dst, src):
                sp.dma_start(dst, src).then_inc(sig(name), 16)

            for t in range(NT):
                lo = CLS if t == 0 else 0
                load(f"patch_loaded{t}", patch[lo:ROWS[t], t, :],
                     A["patches"][t * P + lo - CLS:t * P + ROWS[t] - CLS, :])
                if t == 0:
                    load("ident_loaded", ident[:], A["ident"])
                    load("ln1_loaded", lng, A["ln1_g"])
                    load("ln1_loaded", lnb, A["ln1_b"])
                    load("tokw_loaded", tokW, A["tok_w"])
            load("rows_loaded", tok_bias, A["tok_bias"].partition_broadcast(P))
            load("rows_loaded", ln2g, A["ln2_g"].partition_broadcast(P))
            load("rows_loaded", ln2b, A["ln2_b"].partition_broadcast(P))
            load("pe_loaded", pe2, A["pe"])
            load("cls_loaded", clsA[0:CLS], A["cls_a"])
            load("cls_loaded", clsB[0:CLS], A["cls_b"])
            for n, w in (("wq", wq), ("wk", wk), ("wv", wv), ("wo", wo)):
                load(n + "_loaded", w[:], A[n])
            for n, w in (("bq", bq), ("bk", bk), ("bv", bv), ("gmask", gmask), ("headmask", headmask)):
                load("att_small_loaded", w[:], A[n])
            load("att_small_loaded", bo[:], A["bo"].partition_broadcast(P))
            load("att_small_loaded", lam[:], A["lam"].partition_broadcast(P))
            if upto >= 2:
                load("l1_small_loaded", l1_small[:], A["l1_small"])
                load("phi_loaded", phi[:], A["phi"])
                load("phib_loaded", phib[:], A["phi_b"].partition_broadcast(P))
                eb = A["expert_b"].rearrange("(s j) h -> j s h", j=4)
                for j in range(4):
                    load("expert_b_loaded", yt[32 * j:32 * j + 32], eb[j].partition_broadcast(32))
                sp.wait_ge(sig("att_ready"), G)
                for s in range(ST):
                    if s == 1:
                        sp.wait_ge(sig("att_out_psum"), NT)
                        load("w_in_loaded", w_in, A["w_in"])
                    if s >= 4:
                        sp.wait_ge(sig("y_psum"), s - 3)
                    load(f"experts_loaded{s % 4}", ew[:, s % 4], A["expert_w"][s])
            if upto >= 3:
                sp.wait_ge(sig("l_psum"), CH * NT)
                load("w_lam_loaded", w_lam, A["w_lam"])
                load("w_v_loaded", w_v, A["w_v"])
                sp.wait_ge(sig("l_read"), CH * NT)
                load("w_out_loaded", w_out, A["w_out"])
            if upto >= 4:
                for n, w in (("wg", wg), ("b1c", b1c), ("gconst", gconst)):
                    load("gate_small_loaded", w[:], A[n])

                def load_expert(e):
                    ring = w_ff[:, e % 4]
                    sp.dma_start(ring[:, 0:KD * FF], A["w1"][e]).then_inc(sig(f"ff_loaded{e % 4}"), 16)
                    sp.dma_start(ring[:, KD * FF:2 * KD * FF], A["w2"][e]).then_inc(sig(f"ff_loaded{e % 4}"), 16)

                sp.wait_ge(sig("moe_psum"), NT)
                load("slot_iota_loaded", slot_iota, A["slot_iota"].partition_broadcast(P))
                load("order_loaded", order, A["order"])
                for e in range(4):
                    load_expert(e)
                sp.wait_ge(sig("side_psum"), 16)
                load("b2_loaded", b2w, A["b2"].partition_broadcast(P))
                for e in range(4, E1):
                    sp.wait_ge(sig("ff_y_psum"), e - 3)
                    load_expert(e)
            for t in range(NT):
                sp.wait_ge(sig("h_final"), t + 1)
                sp.dma_start(out[t * P:t * P + ROWS[t], :], h[0:ROWS[t], t, :]).then_inc(sig("out_stored"), 16)
            sp.wait_ge(sig("out_stored"), 16 * NT)

        @block.vector
        def _(dve):
            steps = [0]

            def link(ins):
                steps[0] += 1
                ins.then_inc(sig("dve_step"), 1)
                dve.wait_ge(sig("dve_step"), steps[0])

            def mark(ins):
                steps[0] += 1
                ins.then_inc(sig("dve_step"), 1)
                return steps[0]

            def after(value):
                dve.wait_ge(sig("dve_step"), value)

            def row_stats(t, rows, parts, done):
                for i, part in enumerate(parts):
                    ins = dve.bn_stats(stats[0:rows, t, i, :], part)
                link(ins)
                n = len(parts)
                dve.bn_aggr(mv[0:rows, t, :], stats[0:rows, t, 0:n, :].rearrange("p a b -> p (a b)"))\
                    .then_inc(sig(done), 1)

            def ln_stats(t):
                row_stats(t, ROWS[t], [h[0:ROWS[t], t, :]], "ln_var")

            def ln_norm(k, t):
                r = ROWS[t]
                dve.wait_ge(sig("ln_rstd"), NT * (k - 1) + t + 1)
                dve.tensor_scalar(xn[0:r, t, :], h[0:r, t, :], mv[0:r, t, 0:1], rstd[0:r, t:t + 1],
                                  ALU.subtract, ALU.mult).then_inc(sig("ln_xn"), 1)

            def finish_tile(k, t, finish):
                link(finish(t))
                ln_stats(t)
                if t:
                    ln_norm(k, t - 1)

            def finish_tiles(k, finish):
                for t in range(NT):
                    finish_tile(k, t, finish)
                ln_norm(k, NT - 1)

            dve.memset(neg_half[:], -0.5).then_inc(sig("neg_half_set"), 1)
            dve.memset(ones[:], 1.0).then_inc(sig("ones_set"), 1)
            link(dve.memset(patch[0:CLS, 0, :], 0.0))
            def normalise_patch(t):
                r = ROWS[t]
                dve.wait_ge(sig("patch_rstd"), t + 1)
                dve.tensor_scalar(patch[0:r, t, :], patch[0:r, t, :], mv[0:r, t, 0:1], rstd[0:r, t:t + 1],
                                  ALU.subtract, ALU.mult).then_inc(sig("patch_xhat"), 1)

            def patchT_copy(t):
                r = ROWS[t]
                dve.wait_ge(sig("patchT_psum"), 2 * t + 2)
                dve.tensor_copy(patchT[:, 3:6, t * P:t * P + r],
                                ps[:, (2 * t + 1) % 6, 0:3 * r].rearrange("p (k n) -> p k n", k=3))\
                    .then_inc(sig("patchT_b"), 1)

            for t in range(NT):
                dve.wait_ge(sig(f"patch_loaded{t}"), 16)
                r = ROWS[t]
                row_stats(t, r, [patch[0:r, t, 0:384], patch[0:r, t, 384:768]], "patch_var")
                if t >= 1:
                    normalise_patch(t - 1)
                if t == 2:
                    dve.wait_ge(sig("brow_psum"), 1)
                    dve.wait_ge(sig("rows_loaded"), 48)
                    dve.tensor_tensor(brow, ps[:, 6, 0:D], tok_bias, ALU.add).then_inc(sig("brow_done"), 1)
                if t >= 2:
                    patchT_copy(t - 2)
            normalise_patch(NT - 1)
            patchT_copy(NT - 2)
            dve.wait_ge(sig("brow_done"), 1)
            def z_stats(t):
                r = ROWS[t]
                dve.wait_ge(sig("z_psum"), t + 1)
                dve.tensor_tensor(h[0:r, t, :], ps[0:r, 7 - t % 2, 0:D], brow[0:r], ALU.add)\
                    .then_inc(sig("z_read"), 1)
                dve.wait_ge(sig("z_read"), t + 1)
                row_stats(t, r, [h[0:r, t, :]], "z_var")

            def z_finish(t):
                r = ROWS[t]
                dve.wait_ge(sig("z_rstd"), t + 1)
                link(dve.tensor_scalar(h[0:r, t, :], h[0:r, t, :], mv[0:r, t, 0:1], rstd[0:r, t:t + 1],
                                       ALU.subtract, ALU.mult))
                link(dve.tensor_tensor(h[0:r, t, :], h[0:r, t, :], ln2g[0:r], ALU.mult))
                if t == 0:
                    dve.wait_ge(sig("pe2_done"), 1)
                ins = dve.tensor_tensor(h[0:r, t, :], h[0:r, t, :], pe2[0:r, t], ALU.add)
                if t == 0:
                    link(ins)
                    dve.wait_ge(sig("cls_loaded"), 32)
                    ins = dve.tensor_tensor(h[0:CLS, 0, :], clsA[0:CLS], clsB[0:CLS], ALU.add)
                return ins

            z_stats(0)
            patchT_copy(NT - 1)
            z_stats(1)

            for t in range(NT):
                link(z_finish(t))
                ln_stats(t)
                if t + 2 < NT:
                    z_stats(t + 2)
                ln_norm(1, t)

            if upto >= 1:
                dve.wait_ge(sig("att_small_loaded"), 16 * 7)
                dve.tensor_scalar(gmask[:], gmask[:], lam[:, 0:1], None, ALU.mult)
                for m in range(KD):
                    for n in range(2):
                        i = 2 * m + n
                        dve.wait_ge(sig("k_psum"), i + 1)
                        dve.tensor_scalar(kb[:, m, :, n * HT:(n + 1) * HT].rearrange("p b s -> p s b"),
                                          ps[:, 4 + i, 0:HN].rearrange("p (s b) -> p s b", b=B),
                                          bk[:, m:m + 1], None, ALU.add).then_inc(sig("k_ready"), 1)
                dve.wait_ge(sig("q_ready"), 4)
                dve.memset(ps[32:64, 0:4, 0:HN], 0.0).then_inc(sig("score_pad"), 1)

                def scores(g):
                    s = g % 2
                    dve.wait_ge(sig("s_psum"), g + 1)
                    if g >= 2:
                        dve.wait_ge(sig("exp_done"), g - 1)
                    dve.tensor_tensor(soft[0:PR, s].rearrange("p (f h) k -> p f h k", f=KD),
                                      ps[0:PR, 2 * s:2 * s + 2, 0:HN].rearrange("p f (h k) -> p f h k", k=T),
                                      bc(bc(gmask[0:PR], 1, H // KD), 1, KD), ALU.add)\
                        .then_inc(sig("s_read"), 1)
                    dve.wait_ge(sig("s_read"), g + 1)
                    link(dve.tensor_reduce(smax[0:PR, s], soft[0:PR, s], AX.X, ALU.max))
                    dve.tensor_tensor(soft[0:PR, s], soft[0:PR, s], bc(smax[0:PR, s], 2, T), ALU.subtract)\
                        .then_inc(sig("s_shifted"), 1)

                def normalise(g):
                    s = g % 2
                    dve.wait_ge(sig("exp_done"), g + 1)
                    link(dve.tensor_reduce(ssum[0:PR, s], prob[0:PR, s, :, 0:T], AX.X, ALU.add))
                    link(dve.reciprocal(ssum[0:PR, s], ssum[0:PR, s]))
                    dve.tensor_tensor(prob[0:PR, s, :, 0:T], prob[0:PR, s, :, 0:T], bc(ssum[0:PR, s], 2, T),
                                      ALU.mult).then_inc(sig("p_ready"), 1)

                for g in range(G):
                    scores(g)
                    if g >= 1:
                        normalise(g - 1)
                normalise(G - 1)
                def attention_out(t):
                    r = ROWS[t]
                    dve.wait_ge(sig("att_out_psum"), t + 1)
                    return dve.tensor_tensor(h[0:r, t, :], ps[0:r, t, 0:D], hb[0:r, t, :], ALU.add)

                dve.wait_ge(sig("hb_done"), NT)
                finish_tiles(2, attention_out)

            if upto >= 2:

                def unit(u):
                    c, t, q = u // NT, u % NT, u % 2
                    r = ROWS[t]
                    if u < CH * NT:
                        kept = logit[0:r, t, c * CS:(c + 1) * CS]
                        by_expert = kept.rearrange("p (n s) -> p n s", s=SL)
                        dve.wait_ge(sig("l_psum"), u + 1)
                        dve.tensor_tensor(kept, ps[0:r, LOGIT_BANKS[u % 4], :], phib[0:r, c * CS:(c + 1) * CS], ALU.add)\
                            .then_inc(sig("l_read"), 1)
                    slot_variance(slot_tile(u - 2))
                    if u >= 1:
                        pc, pt = (u - 1) // NT, (u - 1) % NT
                        pr = ROWS[pt]
                        e = disp[0:pr, pc % 2, pt].rearrange("p (n s) -> p n s", s=SL)
                        dve.wait_ge(sig("d_exp"), u)
                        summed = mark(dve.tensor_reduce(dsum[0:pr, 1 - q], e, AX.X, ALU.add))
                    if u < CH * NT:
                        dve.wait_ge(sig("l_read"), u + 1)
                        top = mark(dve.tensor_reduce(dmax[0:r, q], by_expert, AX.X, ALU.max))
                    slot_scale(slot_tile(u - 2))
                    expert_outputs(slot_tile(u - 3))
                    if u >= 1:
                        after(summed)
                        inverse = mark(dve.reciprocal(dsum[0:pr, 1 - q], dsum[0:pr, 1 - q]))
                    if u < CH * NT:
                        after(top)
                        if c >= 2:
                            dve.wait_ge(sig("x_psum"), 4 * (c - 1))
                        dve.tensor_tensor(disp[0:r, c % 2, t].rearrange("p (n s) -> p n s", s=SL), by_expert,
                                          bc(dmax[0:r, q], 2, SL), ALU.subtract).then_inc(sig("d_shifted"), 1)
                        slot_clip(slot_tile(u - 1))
                    if u >= 1:
                        after(inverse)
                        dve.tensor_tensor(e, e, bc(dsum[0:pr, 1 - q], 2, SL), ALU.mult).then_inc(sig("d_ready"), 1)
                    if u < CH * NT:
                        slot_stats(slot_tile(u - 1))

                def slot_clip(s):
                    if s is None:
                        return
                    q = s % 2
                    dve.wait_ge(sig("x_psum"), s + 1)
                    if s >= 2:
                        dve.wait_ge(sig("xT_psum"), s - 1)
                    dve.tensor_scalar(xt[:, q], ps[:, 2 + q, 0:D], -33000.0, 65000.0, ALU.max, ALU.min)\
                        .then_inc(sig("x_read"), 1)

                def slot_stats(s):
                    if s is None:
                        return
                    dve.wait_ge(sig("x_read"), s + 1)
                    dve.bn_stats(xstats[:, s % 2], xt[:, s % 2]).then_inc(sig("x_stats"), 1)

                def slot_variance(s):
                    if s is None:
                        return
                    dve.wait_ge(sig("x_stats"), s + 1)
                    dve.bn_aggr(xmv[:, s % 2, 0:2], xstats[:, s % 2]).then_inc(sig("x_var"), 1)

                def slot_inputs(s):
                    slot_clip(s)
                    slot_stats(s)
                    slot_variance(s)

                def slot_scale(s):
                    if s is None:
                        return
                    q = s % 2
                    dve.wait_ge(sig("x_rstd"), s + 1)
                    dve.scalar_tensor_tensor(xmv[:, q, 3:4], xmv[:, q, 0:1], -1.0, xmv[:, q, 2:3], ALU.mult, ALU.mult)\
                        .then_inc(sig("x_scale"), 1)

                def expert_outputs(s):
                    if s is None:
                        return
                    dve.wait_ge(sig("y_psum"), s + 1)
                    dve.tensor_tensor(yt[:, s], ps[:, 5, 0:D], yt[:, s], ALU.add).then_inc(sig("y_read"), 1)

                def combine_views(t):
                    r = ROWS[t]
                    return (logit[0:r, t].rearrange("p (n s) -> p s n", s=SL),
                            logit[0:r, t].rearrange("p (n s) -> p n s", s=SL))

                def combine_max(t):
                    by_place, _ = combine_views(t)
                    dve.tensor_reduce(cmax[0:ROWS[t], t], by_place, AX.X, ALU.max).then_inc(sig("c_max"), 1)

                def combine_shift(t):
                    _, by_expert = combine_views(t)
                    dve.wait_ge(sig("c_max"), t + 1)
                    dve.tensor_tensor(by_expert, by_expert, bc(cmax[0:ROWS[t], t], 1, NE0), ALU.subtract)\
                        .then_inc(sig("c_shifted"), 1)

                def combine_sum(t):
                    r = ROWS[t]
                    by_place, _ = combine_views(t)
                    dve.wait_ge(sig("c_exp"), t + 1)
                    link(dve.tensor_reduce(csum[0:r, t], by_place, AX.X, ALU.add))
                    dve.reciprocal(csum[0:r, t], csum[0:r, t]).then_inc(sig("c_inverse"), 1)

                def combine_divide(t):
                    _, by_expert = combine_views(t)
                    dve.wait_ge(sig("c_inverse"), t + 1)
                    dve.tensor_tensor(by_expert, by_expert, bc(csum[0:ROWS[t], t], 1, NE0), ALU.mult)\
                        .then_inc(sig("c_ready"), 1)

                dve.wait_ge(sig("phib_loaded"), 16)
                dve.wait_ge(sig("expert_b_loaded"), 64)
                for u in range(CH * NT + 1):
                    unit(u)
                s = ST - 4
                combine_max(0)
                combine_shift(0)
                expert_outputs(s - 1)
                slot_inputs(s)
                combine_max(1)
                slot_scale(s)
                slot_inputs(s + 1)
                combine_shift(1)
                slot_scale(s + 1)
                expert_outputs(s)
                slot_inputs(s + 2)
                combine_sum(0)
                slot_scale(s + 2)
                slot_inputs(s + 3)
                expert_outputs(s + 1)
                combine_divide(0)
                slot_scale(s + 3)
                expert_outputs(s + 2)
                combine_max(2)
                expert_outputs(s + 3)
                combine_shift(2)
                for t in range(1, NT):
                    combine_sum(t)
                    combine_divide(t)
                    if t + 2 < NT:
                        combine_max(t + 2)
                        combine_shift(t + 2)

                def moe_out(t):
                    r = ROWS[t]
                    dve.wait_ge(sig("moe_psum"), t + 1)
                    return dve.tensor_tensor(h[0:r, t, :], ps[0:r, t, 0:D], h[0:r, t, :], ALU.add)

                finish_tiles(3, moe_out)

            if upto >= 3:

                def part(n, m, whole):
                    return whole[:, REC[n]:REC[n + 1], m, :]

                def times(bank, n):
                    return ps[:, bank, 0:B * (REC[n + 1] - REC[n])].rearrange("p (s b) -> p s b", b=B)

                absneg, e, lnw, wm1, inv, sp_out = (sp_t[:, i] for i in range(6))
                dve.wait_ge(sig("l1_small_loaded"), 16)
                link(dve.tensor_scalar(absneg, omega, -1.0, None, ALU.mult))
                dve.tensor_tensor(absneg, absneg, omega, ALU.min).then_inc(sig("sp_abs"), 1)
                dve.wait_ge(sig("sp_exp"), 1)
                dve.tensor_scalar(wm1, e, 1.0, None, ALU.add).then_inc(sig("sp_w"), 1)
                dve.wait_ge(sig("sp_ln"), 1)
                link(dve.tensor_scalar(wm1, wm1, -1.0, None, ALU.add))
                link(dve.tensor_scalar(inv, wm1, 1e-30, None, ALU.max))
                link(dve.reciprocal(inv, inv))
                link(dve.tensor_tensor(lnw, lnw, inv, ALU.mult))
                link(dve.tensor_tensor(lnw, lnw, e, ALU.mult))
                link(dve.tensor_scalar(inv, wm1, 0.0, None, ALU.is_equal))
                link(dve.tensor_tensor(inv, inv, e, ALU.mult))
                link(dve.tensor_scalar(wm1, wm1, 0.0, None, ALU.is_gt))
                link(dve.tensor_tensor(lnw, lnw, wm1, ALU.mult))
                link(dve.tensor_tensor(lnw, lnw, inv, ALU.add))
                link(dve.tensor_scalar(sp_out, omega, 0.0, None, ALU.max))
                link(dve.tensor_tensor(sp_out, sp_out, lnw, ALU.add))
                dve.tensor_scalar(sp_out, sp_out, -8.0, None, ALU.mult).then_inc(sig("decay_ready"), 1)
                for i in range(1, 8, 2):
                    dve.wait_ge(sig("xi_psum"), i + 1)
                    dve.tensor_copy(part(i // KI, i % KI, xi), times(i, i // KI)).then_inc(sig("xi_odd"), 1)

                def flat(a):
                    return a.rearrange("p s k b -> p s (k b)")

                def coefficients(piece, i):
                    t0 = 4 * piece + 1
                    t1 = t0 + 4 if piece < PIECES - 1 else T
                    n = int(t0 >= REC[1])
                    if i == 0:
                        dve.wait_ge(sig("vv_psum"), n + 1)
                        lo = B * (t0 - REC[n])
                        ins = dve.reciprocal(inv_vv[:, B * t0:B * t1], ps[:, 1 + n, lo:lo + B * (t1 - t0)])
                    if i == 1:
                        dve.wait_ge(sig("lam_ready"), KI * (n + 1))
                        ins = dve.scalar_tensor_tensor(flat(kk[:, t0:t1]), flat(va[:, t0:t1, 0]), -2.0,
                                                       flat(va[:, t0:t1, 1]), ALU.mult, ALU.mult)
                    if i == 2:
                        dve.wait_ge(sig("coefficients_done"), 4 * piece + 2)
                        ins = dve.tensor_tensor(kk[:, t0:t1], kk[:, t0:t1],
                                                bc(inv_vv[:, B * t0:B * t1].rearrange("p (s b) -> p s b", b=B), 2, KI),
                                                ALU.mult)
                    if i == 3:
                        ins = dve.scalar_tensor_tensor(flat(xi[:, t0:t1]), flat(va[:, t0:t1, 1]), -1.0,
                                                       flat(xi[:, t0:t1]), ALU.add, ALU.mult)
                    ins.then_inc(sig("coefficients_done"), 1)

                def gate_states(t):
                    s0, s1 = 8 * t, min(8 * t + 8, T)
                    dve.wait_ge(sig("side_read"), 2 * KI + 2 * KI)
                    zt = zs[:, :, B * s0:B * s1].rearrange("p k (s b) -> p k s b", b=B)
                    dve.tensor_tensor(zt, zt, hist[:, s0:s1].rearrange("p s k b -> p k s b"), ALU.mult)\
                        .then_inc(sig("gated"), 1)

                def recurrence_out(t):
                    r = ROWS[t]
                    dve.wait_ge(sig("rnn_out_psum"), t + 1)
                    return dve.tensor_tensor(h[0:r, t, :], ps[0:r, SIDE_BANKS[16 + t], 0:D], h[0:r, t, :], ALU.add)

                def beside(t):
                    if t <= 4 * (PIECES - 1):
                        coefficients((t + 3) // 4, (t - 1) % 4)
                    if t in (23, 25, 27, 33):
                        gate_states((23, 25, 27, 33).index(t))
                    if t >= T - 3:
                        finish_tile(4, t - (T - 3), recurrence_out)

                dve.wait_ge(sig("xi_even"), 4)
                for i in range(4):
                    coefficients(0, i)
                dve.tensor_copy(hist[:, 0], xi[:, 0]).then_inc(sig("rnn_state"), 1)
                for t in range(1, T):
                    dve.wait_ge(sig("rnn_state"), t)
                    dve.tensor_tensor(prodg[:], va[:, t], bc(hist[:, t - 1], 1, 2), ALU.mult)\
                        .then_inc(sig("rnn_prod"), 1)
                    dve.wait_ge(sig("rnn_prod"), t)
                    dve.tensor_reduce(dot[:], prodg[:, 0].rearrange("p k b -> p b k"), AX.X, ALU.add)\
                        .then_inc(sig("rnn_dot"), 1)
                    if t % 4 == 1:
                        dve.wait_ge(sig("coefficients_done"), 4 * min((t + 3) // 4, PIECES))
                    dve.tensor_tensor(prodg[:, 1], prodg[:, 1], xi[:, t], ALU.subtract).then_inc(sig("rnn_decayed"), 1)
                    beside(t)
                    dve.wait_ge(sig("rnn_sum"), t)
                    dve.tensor_tensor(hk[:], kk[:, t], bc(ps[:, 0, 0:B], 1, KI), ALU.mult).then_inc(sig("rnn_turned"), 1)
                    dve.wait_ge(sig("rnn_turned"), t)
                    dve.tensor_tensor(hist[:, t], hk[:], prodg[:, 1], ALU.add).then_inc(sig("rnn_state"), 1)
                dve.wait_ge(sig("rnn_state"), T)
                gate_states(NT - 1)
                finish_tile(4, 3, recurrence_out)
                finish_tile(4, 4, recurrence_out)
                ln_norm(4, NT - 1)

            if upto >= 4:
                lg, eq, key, oh, picked, eg = (gate[:, i] for i in range(6))
                top, kmax, sumexp, cw, rank, sid, valid, _ = (tok[:, i] for i in range(8))
                dve.wait_ge(sig("gate_psum"), 1)
                dve.wait_ge(sig("gate_small_loaded"), 48)
                link(dve.tensor_copy(lg, ps[:, 5, 0:NT * E1].rearrange("p (t e) -> p t e", e=E1)))
                link(dve.tensor_reduce(top, lg, AX.X, ALU.max))
                dve.tensor_tensor(lg, lg, bc(top, 2, E1), ALU.subtract).then_inc(sig("gate_shifted"), 1)
                dve.wait_ge(sig("gate_shifted"), 1)
                link(dve.tensor_scalar(eq, lg, 0.0, None, ALU.is_equal))
                link(dve.tensor_tensor(key, eq, bc(gconst[:, 0], 1, NT), ALU.mult))
                link(dve.tensor_reduce(kmax, key, AX.X, ALU.max))
                link(dve.tensor_tensor(oh, key, bc(kmax, 2, E1), ALU.is_equal))
                dve.tensor_copy(oh16[:], oh).then_inc(sig("one_hot"), 1)
                dve.wait_ge(sig("gate_exp"), 1)
                link(dve.tensor_reduce(sumexp, eg, AX.X, ALU.add))
                dve.reciprocal(cw, sumexp)
                dve.wait_ge(sig("rank_psum"), 1)
                link(dve.tensor_tensor(picked, oh, ps[:, 6, 0:NT * E1].rearrange("p (t e) -> p t e", e=E1), ALU.mult))
                link(dve.tensor_reduce(rank, picked, AX.X, ALU.add))
                link(dve.tensor_scalar(valid, rank, float(CAP), None, ALU.is_le))
                link(dve.tensor_scalar(sid, kmax, -float(CAP), float(E1 * CAP), ALU.mult, ALU.add))
                link(dve.tensor_tensor(sid, sid, rank, ALU.add))
                link(dve.tensor_tensor(sid, sid, valid, ALU.mult))
                link(dve.tensor_scalar(sid, sid, -1.0, None, ALU.add))
                dve.wait_ge(sig("slot_iota_loaded"), 16)
                for t in range(NT):
                    dve.tensor_scalar(pick[:, t], slot_iota, sid[:, t:t + 1], None, ALU.is_equal)\
                        .then_inc(sig("pick_ready"), 1)
                for t in range(NT):
                    dve.tensor_scalar(diag[:, t], ident[:], sid[:, t:t + 1], None, ALU.mult)\
                        .then_inc(sig("diag_ready"), 1)
                for i in (1, 3):
                    dve.wait_ge(sig("slots_psum"), i + 1)
                    dve.tensor_copy(slotT[:, i // 2, (i % 2) * 384:(i % 2 + 1) * 384], ps[:, i, 0:384])\
                        .then_inc(sig("slots_odd"), 1)
                dve.wait_ge(sig("sid_row_ready"), 2)
                for e in range(E1):
                    dve.tensor_scalar(pickT(e), sid_row[0:CAP], gconst[0:CAP, 1, e:e + 1], None, ALU.is_equal)\
                        .then_inc(sig("pickT_ready"), 1)
                dve.wait_ge(sig("b2_loaded"), 16)
                for e in range(E1):
                    dve.wait_ge(sig("ff_y_psum"), e + 1)
                    if e >= 2:
                        dve.wait_ge(sig("ff_added"), e - 1)
                    dve.tensor_tensor(ysb[0:CAP, e % 2], ps[0:CAP, 7, 0:D], b2w[0:CAP, e], ALU.add)\
                        .then_inc(sig("ff_y_ready"), 1)
                for t in range(NT):
                    r = ROWS[t]
                    dve.wait_ge(sig("ff_out_psum"), t + 1)
                    dve.scalar_tensor_tensor(h[0:r, t], ps[0:r, t, 0:D], cw[0:r, t:t + 1], h[0:r, t],
                                             ALU.mult, ALU.add).then_inc(sig("h_final"), 1)

            for t in range(NT if upto < 4 else 0):
                dve.memset(ones[:, t:t + 1], 1.0).then_inc(sig("h_final"), 1)

        @block.gpsimd
        def _(pool):
            steps = [0]

            def link(ins):
                steps[0] += 1
                ins.then_inc(sig("pool_step"), 1)
                pool.wait_ge(sig("pool_step"), steps[0])

            def inv_sqrt(t, rows, ready, done, base=0):
                pool.wait_ge(sig(ready), base + t + 1)
                link(pool.tensor_scalar(veps[0:rows, t:t + 1], mv[0:rows, t, 1:2], EPS, None, ALU.add))
                pool.tensor_tensor(rstd[0:rows, t:t + 1], veps[0:rows, t:t + 1], neg_half[0:rows, t:t + 1],
                                   ALU.pow).then_inc(sig(done), 1)

            pool.wait_ge(sig("neg_half_set"), 1)
            for t in range(NT):
                inv_sqrt(t, ROWS[t], "patch_var", "patch_rstd")
            pool.wait_ge(sig("pe_loaded"), 16)
            pool.wait_ge(sig("rows_loaded"), 48)
            pool.tensor_tensor(pe2, pe2, bc(ln2b, 1, NT), ALU.add).then_inc(sig("pe2_done"), 1)
            for t in range(2):
                inv_sqrt(t, ROWS[t], "z_var", "z_rstd")
            for t in range(NT):
                inv_sqrt(t, ROWS[t], "ln_var", "ln_rstd", 0 * NT)
                if t + 2 < NT:
                    inv_sqrt(t + 2, ROWS[t + 2], "z_var", "z_rstd")
            if upto >= 1:
                pool.memset(prob, 0.0)
                pool.memset(vbd, 0.0).then_inc(sig("att_pads"), 1)
                pool.wait_ge(sig("att_small_loaded"), 16 * 7)
                pool.wait_ge(sig("k_ready"), 4)
                for g in range(G):
                    s = g % 2
                    if g >= 2:
                        pool.wait_ge(sig("s_psum"), g - 1)
                    for f in range(KD):
                        for i in range(2):
                            ins = pool.tensor_tensor(kbd[:, s, f, i], bc(kb[:, f, 2 * g + i], 1, H // KD),
                                                     bc(headmask[:], 2, T), ALU.mult)
                    ins.then_inc(sig("kbd_ready"), 1)
                    if g < NT:
                        pool.tensor_tensor(hb[0:ROWS[g], g, :], h[0:ROWS[g], g, :], bo[0:ROWS[g]], ALU.add)\
                            .then_inc(sig("hb_done"), 1)

                for t in range(NT):
                    inv_sqrt(t, ROWS[t], "ln_var", "ln_rstd", 1 * NT)

            if upto >= 2:
                for s in range(ST):
                    q = s % 2
                    pool.wait_ge(sig("x_var"), s + 1)
                    link(pool.tensor_scalar(veps[:, q:q + 1], xmv[:, q, 1:2], EPS, None, ALU.add))
                    pool.tensor_tensor(xmv[:, q, 2:3], veps[:, q:q + 1], neg_half[:, 0:1], ALU.pow)\
                        .then_inc(sig("x_rstd"), 1)

                for t in range(NT):
                    inv_sqrt(t, ROWS[t], "ln_var", "ln_rstd", 2 * NT)

            if upto >= 3:
                for t in range(NT):
                    inv_sqrt(t, ROWS[t], "ln_var", "ln_rstd", 3 * NT)

        @block.scalar
        def _(act):
            steps = [0]

            def link(ins):
                steps[0] += 1
                ins.then_inc(sig("act_step"), 1)
                act.wait_ge(sig("act_step"), steps[0])

            def transposed_copies(k):
                for t in range(NT):
                    act.wait_ge(sig("ln_T_psum"), NT * (k - 1) + t + 1)
                    act.activation(xnT[:, :, t * P:t * P + ROWS[t]],
                                   ps[:, LN_BANKS[k][t], 0:KD * ROWS[t]].rearrange("p (k n) -> p k n", k=KD), ACT.Copy)\
                        .then_inc(sig("ln_xnT"), 1)

            act.wait_ge(sig("ln1_loaded"), 32)
            act.wait_ge(sig("tokw_loaded"), 16)
            for k in range(KP):
                ins = act.activation(tokWg[:, k, :], tokW[:, k, :], ACT.Copy, scale=lng[:, k:k + 1])
            ins.then_inc(sig("tokwg_done"), 1)
            act.activation(lnb_w, bc(lnb, 2, P), ACT.Copy).then_inc(sig("lnb_wide"), 1)
            for t in range(NT):
                r = ROWS[t]
                act.wait_ge(sig("patchT_psum"), 2 * t + 1)
                act.activation(patchT[:, 0:3, t * P:t * P + r],
                               ps[:, (2 * t) % 6, 0:3 * r].rearrange("p (k n) -> p k n", k=3), ACT.Copy)\
                    .then_inc(sig("patchT_a"), 1)

            if upto >= 1:
                act.wait_ge(sig("att_small_loaded"), 16 * 7)
                link(act.activation(bq[:], bq[:], ACT.Copy, scale=HD ** -0.5))
                transposed_copies(1)
                for m in range(KD):
                    for n in range(2):
                        i = 2 * m + n
                        act.wait_ge(sig("q_psum"), i + 1)
                        act.activation(qb[:, m, :, n * HT:(n + 1) * HT].rearrange("p b s -> p s b"),
                                       ps[:, i, 0:HN].rearrange("p (s b) -> p s b", b=B),
                                       ACT.Identity, bias=bq[:, m:m + 1], scale=HD ** -0.5)\
                            .then_inc(sig("q_ready"), 1)
                act.wait_ge(sig("att_pads"), 1)

                def values(g):
                    s = g % 2
                    act.wait_ge(sig("v_psum"), g + 1)
                    if g >= 2:
                        act.wait_ge(sig("o_psum"), g - 1)
                    for e in range(2):
                        ins = act.activation(
                            vbd[64 * e:64 * e + T, s, :, :, e, :],
                            ps[64 * e:64 * e + T, 4, 0:D].rearrange("p (i j d) -> p i j d", i=2, d=HD), ACT.Copy)
                    ins.then_inc(sig("v_ready"), 1)

                def exponent(g):
                    s = g % 2
                    act.wait_ge(sig("s_shifted"), g + 1)
                    if g >= 2:
                        act.wait_ge(sig("pT_psum"), 2 * g - 2)
                    act.activation(prob[0:PR, s, :, 0:T], soft[0:PR, s], ACT.Exp).then_inc(sig("exp_done"), 1)

                def probs(g):
                    s = g % 2
                    for f in range(2):
                        act.wait_ge(sig("pT_psum"), 2 * g + f + 1)
                        if g >= 2:
                            act.wait_ge(sig("o_psum"), g - 1)
                        act.activation(probT[:, s, 4 * f:4 * f + 4, :],
                                       ps[:, 5 + f, :].rearrange("p (j q) -> p j q", q=P)[:, :, 0:PR], ACT.Copy)\
                            .then_inc(sig("pT_ready"), 1)

                def heads_out(g):
                    act.wait_ge(sig("o_psum"), g + 1)
                    for f in range(KD):
                        ins = act.activation(
                            attT[:, f, :].rearrange("p (s b) -> p b s", b=B)[:, 2 * g:2 * g + 2, :],
                            ps[:, 7, 2 * T * f:2 * T * (f + 1)].rearrange("p (i s) -> p i s", i=2),
                            ACT.Identity, bias=bv[:, f:f + 1])
                    ins.then_inc(sig("att_ready"), 1)

                values(0)
                exponent(0)
                for g in range(G):
                    if g + 1 < G:
                        values(g + 1)
                        exponent(g + 1)
                    probs(g)
                    heads_out(g)

                transposed_copies(2)

            if upto >= 2:

                def exp_dispatch(u):
                    c, t = u // NT, u % NT
                    r = ROWS[t]
                    act.wait_ge(sig("d_shifted"), u + 1)
                    act.activation(disp[0:r, c % 2, t], disp[0:r, c % 2, t], ACT.Exp).then_inc(sig("d_exp"), 1)

                def slot_tanh(s):
                    if s is None:
                        return
                    q = s % 2
                    act.wait_ge(sig("x_scale"), s + 1)
                    act.activation(xt[:, q], xt[:, q], ACT.Tanh, bias=xmv[:, q, 3:4], scale=xmv[:, q, 2:3])\
                        .then_inc(sig("x_hat"), 1)

                def slot_copy(s):
                    if s is None:
                        return
                    q = s % 2
                    act.wait_ge(sig("xT_psum"), s + 1)
                    if s >= 2:
                        act.wait_ge(sig("y_psum"), s - 1)
                    act.activation(xtT[:, q], ps[:, 4, 0:KD * P].rearrange("p (k n) -> p k n", k=KD), ACT.Copy)\
                        .then_inc(sig("xT_ready"), 1)

                def exp_combine(t):
                    r = ROWS[t]
                    act.wait_ge(sig("c_shifted"), t + 1)
                    act.activation(logit[0:r, t], logit[0:r, t], ACT.Exp).then_inc(sig("c_exp"), 1)

                def combine_copies(t):
                    r = ROWS[t]
                    for f in range(4):
                        act.wait_ge(sig("cT_psum"), 4 * t + f + 1)
                        act.activation(combT[:, 4 * f:4 * f + 4, t * P:t * P + r],
                                       ps[:, 6 + f % 2, 0:4 * r].rearrange("p (s n) -> p s n", n=r), ACT.Copy)\
                            .then_inc(sig("cT_ready"), 1)

                for u in range(CH * NT):
                    slot_tanh(slot_tile(u - 2))
                    slot_copy(slot_tile(u - 2))
                    exp_dispatch(u)
                s = ST - 4
                slot_tanh(s - 1)
                slot_copy(s - 1)
                exp_combine(0)
                slot_tanh(s)
                slot_copy(s)
                slot_tanh(s + 1)
                exp_combine(1)
                slot_copy(s + 1)
                slot_tanh(s + 2)
                slot_copy(s + 2)
                slot_tanh(s + 3)
                slot_copy(s + 3)
                combine_copies(0)
                for t in range(1, NT):
                    if t + 1 < NT:
                        exp_combine(t + 1)
                    combine_copies(t)
                transposed_copies(3)

            if upto >= 3:

                def part(n, m, whole):
                    return whole[:, REC[n]:REC[n + 1], m, :]

                def times(bank, n):
                    return ps[:, bank, 0:B * (REC[n + 1] - REC[n])].rearrange("p (s b) -> p s b", b=B)

                def v_read(m, n, bank, name):
                    act.activation(part(n, m, va[:, :, 0]), times(bank, n), ACT.Identity, bias=bv1[:, m:m + 1])\
                        .then_inc(sig(name), 1)
                    act.wait_ge(sig(name), m + 1)
                    act.activation(part(n, m, hist), part(n, m, va[:, :, 0]), ACT.Square).then_inc(sig("v_squared"), 1)

                def lam_read(m, n, bank, name):
                    act.activation(part(n, m, va[:, :, 1]), times(bank, n), ACT.Sigmoid, bias=bl[:, m:m + 1])\
                        .then_inc(sig(name), 1)

                def decays(n):
                    for m in range(KI):
                        act.activation(part(n, m, va[:, :, 1]), part(n, m, va[:, :, 1]), ACT.Exp,
                                       scale=sp_t[:, 5, m:m + 1]).then_inc(sig("lam_ready"), 1)

                act.wait_ge(sig("sp_abs"), 1)
                act.activation(sp_t[:, 1], sp_t[:, 0], ACT.Exp).then_inc(sig("sp_exp"), 1)
                act.wait_ge(sig("sp_w"), 1)
                act.activation(sp_t[:, 2], sp_t[:, 3], ACT.Ln).then_inc(sig("sp_ln"), 1)
                for i in range(0, 8, 2):
                    act.wait_ge(sig("xi_psum"), i + 1)
                    act.activation(part(i // KI, i % KI, xi), times(i, i // KI), ACT.Copy).then_inc(sig("xi_even"), 1)
                for m in range(KI):
                    act.wait_ge(sig("v0_psum"), m + 1)
                    v_read(m, 0, m, "v0_read")
                for m in range(KI):
                    act.wait_ge(sig("lam0_psum"), m + 1)
                    lam_read(m, 0, 4 + m, "lam0_read")
                act.wait_ge(sig("decay_ready"), 1)
                act.wait_ge(sig("lam0_read"), KI)
                decays(0)
                for q in range(16):
                    act.wait_ge(sig("side_psum"), q + 1)
                    if q < KI:
                        v_read(q, 1, SIDE_BANKS[q], "side_read")
                    elif q < 2 * KI:
                        lam_read(q - KI, 1, SIDE_BANKS[q], "side_read")
                        if q == 2 * KI - 1:
                            act.wait_ge(sig("side_read"), 2 * KI)
                            decays(1)
                    else:
                        m, n = (q - 2 * KI) // 2, q % 2
                        act.activation(zs[:, m, n * HN:(n + 1) * HN], ps[:, SIDE_BANKS[q], 0:HN], ACT.Silu)\
                            .then_inc(sig("side_read"), 1)

                transposed_copies(4)

            if upto >= 4:
                act.wait_ge(sig("gate_shifted"), 1)
                act.activation(gate[:, 5], gate[:, 0], ACT.Exp).then_inc(sig("gate_exp"), 1)
                for i in (0, 2):
                    act.wait_ge(sig("slots_psum"), i + 1)
                    act.activation(slotT[:, i // 2, 0:384], ps[:, i, 0:384], ACT.Copy).then_inc(sig("slots_even"), 1)
                for i, (at, n) in enumerate(((0, 4 * P), (4 * P, N - 4 * P))):
                    act.wait_ge(sig("sid_psum"), i + 1)
                    act.activation(sid_row[:, at:at + n], ps[:, 4 + i, 0:n], ACT.Copy).then_inc(sig("sid_row_ready"), 1)
                for e in range(E1):
                    if e >= 2:
                        act.wait_ge(sig("ff_y_psum"), e - 1)
                    for f in range(KF):
                        if f % 4 == 0:
                            act.wait_ge(sig("ff_h_psum"), 2 * e + f // 4 + 1)
                        ins = act.activation(hid[:, e % 2, f], ps[:, 5 + f // 4, (f % 4) * CAP:(f % 4 + 1) * CAP],
                                             ACT.Gelu, bias=b1c[:, e, f:f + 1])
                        if f % 4 == 3:
                            ins.then_inc(sig("ff_h_ready"), 1)

        @block.tensor
        def _(pe):
            def transpose_tile(k, t):
                r = ROWS[t]
                pe.wait_ge(sig("ln_xn"), NT * (k - 1) + t + 1)
                bank = LN_BANKS[k][t]
                if bank in LN_BANKS[k][:t]:
                    pe.wait_ge(sig("ln_xnT"), NT * (k - 1) + t - LN_BANKS[k][:t][::-1].index(bank))
                for c in range(KD):
                    ins = pe.transpose(ps[:, bank, c * r:(c + 1) * r], xn[0:r, t, c * P:(c + 1) * P],
                                       ident[0:r, 0:r])
                ins.then_inc(sig("ln_T_psum"), 1)

            def product_tiles(k, product):
                for t in range(NT):
                    product(t)
                    if t >= 2:
                        transpose_tile(k, t - 2)
                transpose_tile(k, NT - 2)
                transpose_tile(k, NT - 1)
                pe.wait_ge(sig("ln_xnT"), NT * k)

            pe.wait_ge(sig("lnb_wide"), 1)
            pe.wait_ge(sig("tokw_loaded"), 16)
            for k in range(KP):
                ins = pe.matmul(ps[:, 6, 0:D], lnb_w[:, k, :], tokW[:, k, :], start=(k == 0), stop=(k == KP - 1))
            ins.then_inc(sig("brow_psum"), 1)
            pe.wait_ge(sig("ident_loaded"), 16)

            def patch_product(t):
                r = ROWS[t]
                pe.wait_ge(sig("patchT_a"), t + 1)
                pe.wait_ge(sig("patchT_b"), t + 1)
                if t == 0:
                    pe.wait_ge(sig("tokwg_done"), 1)
                if t == 1:
                    pe.wait_ge(sig("brow_done"), 1)
                if t >= 2:
                    pe.wait_ge(sig("z_read"), t - 1)
                for k in range(KP):
                    ins = pe.matmul(ps[0:r, 7 - t % 2, 0:D], patchT[:, k, t * P:t * P + r], tokWg[:, k, :],
                                    start=(k == 0), stop=(k == KP - 1))
                ins.then_inc(sig("z_psum"), 1)

            for t in range(NT):
                r = ROWS[t]
                pe.wait_ge(sig("patch_xhat"), t + 1)
                for f in range(2):
                    if t >= 3:
                        pe.wait_ge(sig("patchT_b" if f else "patchT_a"), t - 2)
                    for k in range(3):
                        ins = pe.transpose(ps[:, (2 * t + f) % 6, k * r:(k + 1) * r],
                                           patch[0:r, t, (3 * f + k) * P:(3 * f + k + 1) * P], ident[0:r, 0:r])
                    ins.then_inc(sig("patchT_psum"), 1)
                if t >= 1:
                    patch_product(t - 1)
            patch_product(NT - 1)
            for t in range(NT):
                transpose_tile(1, t)
            pe.wait_ge(sig("ln_xnT"), NT)

            if upto >= 1:
                for w, name, base in ((wq, "q", 0), (wk, "k", 4)):
                    pe.wait_ge(sig(f"w{name}_loaded"), 16)
                    for m in range(KD):
                        for n in range(2):
                            for k in range(KD):
                                ins = pe.matmul(ps[:, base + 2 * m + n, 0:HN], w[:, k, m * P:(m + 1) * P],
                                                xnT[:, k, n * HN:(n + 1) * HN], start=(k == 0), stop=(k == KD - 1))
                            ins.then_inc(sig(f"{name}_psum"), 1)

                def image(ap, b):
                    return ap.rearrange("p (s b) -> p b s", b=B)[:, b, :]

                def scores(g):
                    s = g % 2
                    pe.wait_ge(sig("kbd_ready"), g + 1)
                    if g >= 2:
                        pe.wait_ge(sig("s_read"), g - 1)
                    for f in range(KD):
                        for i in range(2):
                            ins = pe.matmul(ps[64 * i:64 * i + T, 2 * s + f, 0:HN], qb[:, f, 2 * g + i, :],
                                            kbd[:, s, f, i].rearrange("p h k -> p (h k)"), start=True, stop=True)
                    ins.then_inc(sig("s_psum"), 1)

                def values(g):
                    if g >= 1:
                        pe.wait_ge(sig("v_ready"), g)
                    for i in range(2):
                        for k in range(KD):
                            for e in range(2):
                                ins = pe.matmul(
                                    ps[64 * e:64 * e + T, 4, i * P:(i + 1) * P],
                                    image(xnT[:, k, :], 2 * g + i),
                                    wv[:, k, :].rearrange("p (j e d) -> p e j d", e=2, d=HD)[:, e],
                                    start=(k == 0), stop=(k == KD - 1))
                    ins.then_inc(sig("v_psum"), 1)

                def attend(g):
                    s = g % 2
                    pe.wait_ge(sig("p_ready"), g + 1)
                    for f in range(2):
                        if g >= 1:
                            pe.wait_ge(sig("pT_ready"), 2 * g - 1 + f)
                        for j in range(4):
                            hh = 2 * (4 * f + j)
                            ins = pe.transpose(ps[:, 5 + f, j * P:(j + 1) * P],
                                               prob[:, s, hh:hh + 2, :].rearrange("p a k -> p (a k)"), ident[:])
                        ins.then_inc(sig("pT_psum"), 1)
                    pe.wait_ge(sig("pT_ready"), 2 * g + 2)
                    pe.wait_ge(sig("v_ready"), g + 1)
                    if g >= 1:
                        pe.wait_ge(sig("att_ready"), g)
                    for f in range(2):
                        for i in range(2):
                            for j in range(4):
                                ins = pe.matmul(
                                    ps[32 * j:32 * j + 32, 7, (2 * f + i) * T:(2 * f + i + 1) * T],
                                    vbd[0:PR, s, i, 4 * f + j].rearrange("p e d -> p (e d)"),
                                    probT[0:PR, s, 4 * f + j, 64 * i:64 * i + T], start=True, stop=True)
                    ins.then_inc(sig("o_psum"), 1)

                pe.wait_ge(sig("k_ready"), 4)
                pe.wait_ge(sig("score_pad"), 1)
                pe.wait_ge(sig("wv_loaded"), 16)
                scores(0)
                values(0)
                scores(1)
                for g in range(G):
                    if g + 1 < G:
                        values(g + 1)
                    if g + 2 < G:
                        scores(g + 2)
                    attend(g)
                pe.wait_ge(sig("att_ready"), G)
                pe.wait_ge(sig("wo_loaded"), 16)

                def project(t):
                    r = ROWS[t]
                    for k in range(KD):
                        ins = pe.matmul(ps[0:r, t, 0:D], attT[:, k, t * P:t * P + r], wo[:, k, :],
                                        start=(k == 0), stop=(k == KD - 1))
                    ins.then_inc(sig("att_out_psum"), 1)

                product_tiles(2, project)

            if upto >= 2:

                def logits(u):
                    c, t, q = u // NT, u % NT, LOGIT_BANKS[u % 4]
                    r = ROWS[t]
                    if u >= 4:
                        pe.wait_ge(sig("l_read"), u - 3)
                    for k in range(KD):
                        ins = pe.matmul(ps[0:r, q, :], xnT[:, k, t * P:t * P + r], phi[:, k, c * CS:(c + 1) * CS],
                                        start=(k == 0), stop=(k == KD - 1))
                    ins.then_inc(sig("l_psum"), 1)

                def slot_inputs(s):
                    if s is None:
                        return
                    c, i = s // 4, s % 4
                    pe.wait_ge(sig("d_ready"), NT * (c + 1))
                    if s >= 2:
                        pe.wait_ge(sig("x_read"), s - 1)
                    for t in range(NT):
                        r = ROWS[t]
                        ins = pe.matmul(ps[:, 2 + s % 2, 0:D], disp[0:r, c % 2, t, i * P:(i + 1) * P], xn[0:r, t, :],
                                        start=(t == 0), stop=(t == NT - 1))
                    ins.then_inc(sig("x_psum"), 1)

                def slot_transposes(s):
                    if s is None:
                        return
                    pe.wait_ge(sig("x_hat"), s + 1)
                    if s:
                        pe.wait_ge(sig("xT_ready"), s)
                    for k in range(KD):
                        ins = pe.transpose(ps[:, 4, k * P:(k + 1) * P], xt[:, s % 2, k * P:(k + 1) * P], ident[:])
                    ins.then_inc(sig("xT_psum"), 1)

                def experts(s):
                    if s is None:
                        return
                    pe.wait_ge(sig("xT_ready"), s + 1)
                    pe.wait_ge(sig(f"experts_loaded{s % 4}"), 16 * (s // 4 + 1))
                    if s:
                        pe.wait_ge(sig("y_read"), s)
                    for k in range(KD):
                        for j in range(4):
                            ins = pe.matmul(ps[32 * j:32 * j + 32, 5, 0:D], xtT[:, s % 2, k, 32 * j:32 * j + 32],
                                            ew[:, s % 4, j, k, :], start=(k == 0), stop=(k == KD - 1))
                    ins.then_inc(sig("y_psum"), 1)

                def combine_transposes(t):
                    r = ROWS[t]
                    pe.wait_ge(sig("c_ready"), t + 1)
                    for f in range(4):
                        if 4 * t + f >= 2:
                            pe.wait_ge(sig("cT_ready"), 4 * t + f - 1)
                        for i in range(4):
                            s = 4 * f + i
                            ins = pe.transpose(ps[:, 6 + f % 2, i * r:(i + 1) * r],
                                               logit[0:r, t, s * P:(s + 1) * P], ident[0:r, 0:r])
                        ins.then_inc(sig("cT_psum"), 1)

                def combine(t):
                    r = ROWS[t]
                    for s in range(ST):
                        if s % 4 == 0:
                            pe.wait_ge(sig("cT_ready"), 4 * t + s // 4 + 1)
                        if t == NT - 1 and s == ST // 2:
                            for done in range(NT - 2):
                                transpose_tile(3, done)
                        ins = pe.matmul(ps[0:r, t, 0:D], combT[:, s, t * P:t * P + r], yt[:, s, :],
                                        start=(s == 0), stop=(s == ST - 1))
                    ins.then_inc(sig("moe_psum"), 1)

                pe.wait_ge(sig("phi_loaded"), 16)
                logits(0)
                logits(1)
                logits(2)
                for u in range(CH * NT):
                    if u + 3 < CH * NT:
                        logits(u + 3)
                    slot_transposes(slot_tile(u - 2))
                    if u % NT:
                        slot_inputs(slot_tile(u))
                    experts(slot_tile(u - 2))
                    if u % NT == 0:
                        slot_inputs(slot_tile(u))
                s = ST - 4
                slot_transposes(s - 1)
                slot_inputs(s)
                experts(s - 1)
                slot_inputs(s + 1)
                slot_inputs(s + 2)
                for i in range(4):
                    slot_transposes(s + i)
                    experts(s + i)
                    if i == 0:
                        slot_inputs(s + 3)
                pe.wait_ge(sig("y_read"), ST)

                for t in range(NT):
                    combine_transposes(t)
                    combine(t)
                transpose_tile(3, NT - 2)
                transpose_tile(3, NT - 1)
                pe.wait_ge(sig("ln_xnT"), NT * 3)

            if upto >= 3:
                def cols(n):
                    return B * (REC[n + 1] - REC[n])

                def x_product(m, n, bank, k):
                    return pe.matmul(ps[:, bank, 0:cols(n)], w_in[:, k, m * P:(m + 1) * P],
                                     xnT[:, k, B * REC[n]:B * REC[n + 1]], start=(k == 0), stop=(k == KD - 1))

                def xi_product(w, m, n, bank, k):
                    return pe.matmul(ps[:, bank, 0:cols(n)], w[:, k, m * P:(m + 1) * P],
                                     xi[:, REC[n]:REC[n + 1], k, :], start=(k == 0), stop=(k == KI - 1))

                def vv_product(n, k):
                    ins = pe.matmul(ps[:, 1 + n, 0:cols(n)], ones[:], hist[:, REC[n]:REC[n + 1], k, :],
                                    start=(k == 0), stop=(k == KI - 1))
                    if k == KI - 1:
                        ins.then_inc(sig("vv_psum"), 1)

                def z_product(m, n, bank, k):
                    return pe.matmul(ps[:, bank, 0:HN], w_in[:, k, DI + m * P:DI + (m + 1) * P],
                                     xnT[:, k, n * HN:(n + 1) * HN], start=(k == 0), stop=(k == KD - 1))

                pe.wait_ge(sig("w_in_loaded"), 16)
                for i in range(8):
                    for k in range(KD):
                        ins = x_product(i % KI, i // KI, i, k)
                    ins.then_inc(sig("xi_psum"), 1)
                pe.wait_ge(sig("xi_even"), 2)
                pe.wait_ge(sig("xi_odd"), 2)
                pe.wait_ge(sig("w_v_loaded"), 16)
                for m in range(KI):
                    for k in range(KI):
                        ins = xi_product(w_v, m, 0, m, k)
                    ins.then_inc(sig("v0_psum"), 1)
                pe.wait_ge(sig("xi_even"), 4)
                pe.wait_ge(sig("xi_odd"), 4)
                pe.wait_ge(sig("w_lam_loaded"), 16)
                for m in range(KI):
                    if m == KI - 1:
                        pe.wait_ge(sig("v_squared"), KI)
                        for k in range(KI):
                            vv_product(0, k)
                    for k in range(KI):
                        ins = xi_product(w_lam, m, 0, 4 + m, k)
                    ins.then_inc(sig("lam0_psum"), 1)

                def side(i):
                    if i < 8 * KI:
                        q, k, last = i // KI, i % KI, KI - 1
                    elif i < 9 * KI:
                        if i == 8 * KI:
                            pe.wait_ge(sig("v_squared"), 2 * KI)
                        vv_product(1, i - 8 * KI)
                        return
                    else:
                        q, k, last = 2 * KI + (i - 9 * KI) // KD, (i - 9 * KI) % KD, KD - 1
                    bank = SIDE_BANKS[q]
                    if k == 0:
                        if q == 0:
                            pe.wait_ge(sig("v0_read"), KI)
                        elif q < 5:
                            pe.wait_ge(sig("lam0_read"), q)
                        else:
                            pe.wait_ge(sig("side_read"), q - 4)
                    if q < KI:
                        ins = xi_product(w_v, q, 1, bank, k)
                    elif q < 2 * KI:
                        ins = xi_product(w_lam, q - KI, 1, bank, k)
                    else:
                        ins = z_product((q - 2 * KI) // 2, q % 2, bank, k)
                    if k == last:
                        ins.then_inc(sig("side_psum"), 1)

                def recurrence_out(t, k):
                    r = ROWS[t]
                    if k == 0:
                        pe.wait_ge(sig("gated"), t + 1)
                        if t == 0:
                            pe.wait_ge(sig("w_out_loaded"), 16)
                            pe.wait_ge(sig("side_read"), 16)
                    ins = pe.matmul(ps[0:r, SIDE_BANKS[16 + t], 0:D], zs[:, k, t * P:t * P + r], w_out[:, k, :],
                                    start=(k == 0), stop=(k == KI - 1))
                    if k == KI - 1:
                        ins.then_inc(sig("rnn_out_psum"), 1)

                pe.wait_ge(sig("v0_read"), 1)
                for t in range(1, T):
                    pe.wait_ge(sig("rnn_dot"), t)
                    pe.matmul(ps[:, 0, 0:B], ones[:], dot[:], start=True, stop=True).then_inc(sig("rnn_sum"), 1)
                    if t <= 12:
                        for i in range(3 * t - 3, 3 * t):
                            side(i)
                    elif t <= 20:
                        side(36 + 2 * (t - 13))
                        side(37 + 2 * (t - 13))
                    if t in OUT_STEPS:
                        i = OUT_STEPS.index(t)
                        for k in (0, 1) if i % 2 == 0 else (2, 3):
                            recurrence_out(i // 2, k)
                for k in range(KI):
                    recurrence_out(4, k)
                for t in range(NT):
                    transpose_tile(4, t)
                pe.wait_ge(sig("ln_xnT"), NT * 4)

            if upto >= 4:
                pe.wait_ge(sig("gate_small_loaded"), 48)
                for t in range(NT):
                    r = ROWS[t]
                    for k in range(KD):
                        ins = pe.matmul(ps[0:r, 5, t * E1:(t + 1) * E1], xnT[:, k, t * P:t * P + r], wg[:, k, :],
                                        start=(k == 0), stop=(k == KD - 1))
                ins.then_inc(sig("gate_psum"), 1)
                pe.wait_ge(sig("one_hot"), 1)
                pe.wait_ge(sig("order_loaded"), 16)
                for t in range(NT):
                    r = ROWS[t]
                    for j in range(NT):
                        ins = pe.matmul(ps[0:r, 6, t * E1:(t + 1) * E1], order[0:ROWS[j], j, t * P:t * P + r],
                                        oh16[0:ROWS[j], j, :], start=(j == 0), stop=(j == NT - 1))
                ins.then_inc(sig("rank_psum"), 1)
                pe.wait_ge(sig("pick_ready"), NT)
                for i in range(4):
                    m, n = i // 2, i % 2
                    for t in range(NT):
                        r = ROWS[t]
                        ins = pe.matmul(ps[:, i, 0:384], xn[0:r, t, m * P:(m + 1) * P],
                                        pick[0:r, t, n * 384:(n + 1) * 384], start=(t == 0), stop=(t == NT - 1))
                    ins.then_inc(sig("slots_psum"), 1)
                pe.wait_ge(sig("diag_ready"), NT)
                for t in range(NT):
                    r = ROWS[t]
                    ins = pe.matmul(ps[:, 4 + t // 4, (t % 4) * P:(t % 4) * P + r], ones[0:r, :], diag[0:r, t, 0:r],
                                    start=True, stop=True)
                    if t >= 3:
                        ins.then_inc(sig("sid_psum"), 1)

                def hidden(e):
                    w1 = w_ff[:, e % 4, 0:KD * FF].rearrange("p (k f) -> p k f", k=KD)
                    pe.wait_ge(sig(f"ff_loaded{e % 4}"), 32 * (e // 4 + 1))
                    for f in range(KF):
                        if e and f % 4 == 0:
                            pe.wait_ge(sig("ff_h_ready"), 2 * e - 1 + f // 4)
                        for k in range(KD):
                            ins = pe.matmul(ps[:, 5 + f // 4, (f % 4) * CAP:(f % 4 + 1) * CAP], w1[:, k, f * P:(f + 1) * P],
                                            slotT[:, k, e * CAP:(e + 1) * CAP], start=(k == 0), stop=(k == KD - 1))
                        if f % 4 == 3:
                            ins.then_inc(sig("ff_h_psum"), 1)

                def outputs(e):
                    w2 = w_ff[:, e % 4, KD * FF:].rearrange("p (k d) -> p k d", k=KF)
                    pe.wait_ge(sig("ff_h_ready"), 2 * e + 2)
                    if e:
                        pe.wait_ge(sig("ff_y_ready"), e)
                    for f in range(KF):
                        ins = pe.matmul(ps[0:CAP, 7, 0:D], hid[:, e % 2, f], w2[:, f, :],
                                        start=(f == 0), stop=(f == KF - 1))
                    ins.then_inc(sig("ff_y_psum"), 1)

                def add_back(e):
                    pe.wait_ge(sig("ff_y_ready"), e + 1)
                    for t in range(NT):
                        r = ROWS[t]
                        ins = pe.matmul(ps[0:r, t, 0:D], pickT(e)[:, t * P:t * P + r], ysb[0:CAP, e % 2],
                                        start=(e == 0), stop=(e == E1 - 1))
                        if e == E1 - 1:
                            ins.then_inc(sig("ff_out_psum"), 1)
                    if e < E1 - 1:
                        ins.then_inc(sig("ff_added"), 1)

                pe.wait_ge(sig("slots_even"), 2)
                pe.wait_ge(sig("slots_odd"), 2)
                pe.wait_ge(sig("sid_row_ready"), 2)
                hidden(0)
                pe.wait_ge(sig("pickT_ready"), E1)
                for e in range(E1):
                    if e + 1 < E1:
                        hidden(e + 1)
                    outputs(e)
                    if e:
                        add_back(e - 1)
                add_back(E1 - 1)


def kernel(x, cls_tok, L0_tok_cls_token, L0_tok_cls_pos_embedding, L0_tok_ln1_g, L0_tok_ln1_b, L0_tok_W,
           L0_tok_bias, L0_tok_ln2_g, L0_tok_ln2_b, L0_attn_Wq, L0_attn_bq, L0_attn_Wk, L0_attn_bk, L0_attn_Wv,
           L0_attn_bv, L0_attn_Wo, L0_attn_bo, L0_attn_prior_lambda, L0_ffn_phi_w, L0_ffn_phi_b,
           L0_ffn_expert_w, L0_ffn_expert_b, L1_attn_omega, L1_attn_Win, L1_attn_Wl, L1_attn_bl, L1_attn_Wv,
           L1_attn_bv, L1_attn_Wout, L1_ffn_wg, L1_ffn_W1, L1_ffn_b1, L1_ffn_W2, L1_ffn_b2, upto=9):
    import concourse.bacc as bacc
    from concourse.bass_utils import run_bass_kernel_spmd

    def arr(a):
        return np.asarray(a)

    def tiled(w):
        w = arr(w)
        return w.reshape(w.shape[0] // P, P, w.shape[1]).transpose(1, 0, 2)

    def col(v):
        return arr(v).reshape(-1, P).T

    patches = arr(x).reshape(B, 3, 6, 16, 6, 16).transpose(2, 4, 0, 1, 3, 5).reshape(B * NP, PD)

    def by_channel(w):
        return arr(w).reshape(16 * 16, 3, -1).transpose(1, 0, 2).reshape(PD, -1)

    omega = (1.0 / 10000.0 ** (np.arange(D // 4, dtype=np.float32) / (D // 4 - 1))).astype(np.float32)
    gy, gx = np.meshgrid(np.arange(6), np.arange(6), indexing="ij")
    ya = gy.reshape(-1)[:, None] * omega[None, :]
    xa = gx.reshape(-1)[:, None] * omega[None, :]
    pe = np.concatenate((np.sin(xa), np.cos(xa), np.sin(ya), np.cos(ya)), axis=1).astype(np.float32)
    pe_rows = np.zeros((NT * P, D), np.float32)
    pe_rows[CLS:N] = np.repeat(pe, B, axis=0)
    time = np.arange(T)
    delta = np.abs(time[:, None] - time[None, :]).astype(np.float32)
    gauss = np.zeros((T, T), np.float32)
    for period, weight, sigma in ((1.0, 0.8, 0.5), (30.0, 0.4, 2.0)):
        gauss = gauss + np.float32(weight) * np.exp(-(delta - np.float32(period)) ** 2 / np.float32(2.0 * sigma ** 2))
    gmask = np.zeros((P, T), np.float32)
    gmask[0:T] = gauss
    gmask[64:64 + T] = gauss
    headmask = (np.arange(P)[:, None] // HD == np.arange(H // KD)[None, :]).astype(np.float32)

    ins = {
        "patches": patches,
        "ident": np.eye(P, dtype=np.float32),
        "ln1_g": by_channel(L0_tok_ln1_g)[:, 0].reshape(KP, P).T,
        "ln1_b": by_channel(L0_tok_ln1_b)[:, 0].reshape(KP, P).T,
        "tok_w": tiled(by_channel(L0_tok_W)),
        "tok_bias": arr(L0_tok_bias), "ln2_g": arr(L0_tok_ln2_g), "ln2_b": arr(L0_tok_ln2_b),
        "pe": pe_rows.reshape(NT, P, D).transpose(1, 0, 2),
        "cls_a": np.repeat(np.concatenate([arr(cls_tok)[0], arr(L0_tok_cls_token)[0]]), B, axis=0),
        "cls_b": np.repeat(np.concatenate([np.zeros((1, D), np.float32), arr(L0_tok_cls_pos_embedding)[0]]), B, axis=0),
        "wq": tiled(arr(L0_attn_Wq).T), "wk": tiled(arr(L0_attn_Wk).T),
        "wv": tiled(arr(L0_attn_Wv).T), "wo": tiled(arr(L0_attn_Wo).T),
        "bq": col(L0_attn_bq), "bk": col(L0_attn_bk), "bv": col(L0_attn_bv), "bo": arr(L0_attn_bo),
        "lam": arr(L0_attn_prior_lambda).reshape(1), "gmask": gmask, "headmask": headmask,
    }
    ew = arr(L0_ffn_expert_w).reshape(ST, 4, KD, P, D).transpose(0, 3, 1, 2, 4)
    ins |= {"phi": tiled(arr(L0_ffn_phi_w).T), "phi_b": arr(L0_ffn_phi_b), "expert_b": arr(L0_ffn_expert_b),
            "expert_w": ew,
            "l1_small": np.stack([col(arr(L1_attn_omega).reshape(-1)), col(L1_attn_bl), col(L1_attn_bv)], axis=1),
            "w_in": tiled(arr(L1_attn_Win).T), "w_lam": tiled(arr(L1_attn_Wl).T), "w_v": tiled(arr(L1_attn_Wv).T),
            "w_out": tiled(arr(L1_attn_Wout).T)}
    rank_of = (np.arange(B)[None, :] * T + time[:, None]).reshape(-1)
    before = np.zeros((NT * P, N), np.float32)
    before[:N] = rank_of[:, None] <= rank_of[None, :]
    e8 = np.arange(E1, dtype=np.float32)
    gconst = np.zeros((P, 2, E1), np.float32)
    gconst[:, 0] = E1 - e8
    gconst[:, 1] = np.arange(P, dtype=np.float32)[:, None] + CAP * e8
    ins |= {
        "wg": tiled(L1_ffn_wg), "gconst": gconst, "slot_iota": np.arange(E1 * CAP, dtype=np.float32),
        "order": before.reshape(NT, P, N).transpose(1, 0, 2).astype(mybir.dt.np(BF16)),
        "w1": arr(L1_ffn_W1).reshape(E1, KD, P, FF).transpose(0, 2, 1, 3).reshape(E1, P, KD * FF),
        "w2": arr(L1_ffn_W2).reshape(E1, KF, P, D).transpose(0, 2, 1, 3).reshape(E1, P, KF * D),
        "b1c": arr(L1_ffn_b1).reshape(E1, KF, P).transpose(2, 0, 1), "b2": arr(L1_ffn_b2),
    }
    nc = bacc.Bacc("TRN2", target_bir_lowering=False, num_devices=1)
    arrays, A = {}, {}
    for name, a in ins.items():
        a = np.ascontiguousarray(a)
        arrays["in_" + name] = a
        A[name] = nc.dram_tensor("in_" + name, a.shape, mybir.dt.from_np(a.dtype), kind="ExternalInput").ap()
    out = nc.dram_tensor("out_rows", (N, D), F32, kind="ExternalOutput").ap()
    tower(nc, A, out, upto)
    r = run_bass_kernel_spmd(nc, [arrays], core_ids=[0])
    rows = r.results[0]["out_rows"]
    return np.ascontiguousarray(rows.reshape(T, B, D).transpose(1, 0, 2))
```

```python
from contextlib import ExitStack

import numpy as np

import concourse.bass as bass
from concourse import mybir

F32 = mybir.dt.float32
BF16 = mybir.dt.bfloat16
ALU = mybir.AluOpType
ACT = mybir.ActivationFunctionType
AX = mybir.AxisListType

P = 128
B = 16
T = 38
N = B * T
D = 256
NP = 36
PD = 768
NT = -(-N // P)
KD = D // P
KP = PD // P
ROWS = [min(P, N - P * t) for t in range(NT)]
CLS = 2 * B
HN = N // 2
HT = T // 2
EPS = 1e-5
H = 16
HD = D // H
G = B // 2
PR = 64 + T
NE0 = 64
SL = 32
NS = NE0 * SL
CH = 4
CS = NS // CH
CE = CS // SL
ST = NS // P
DI = 512
KI = DI // P
E1 = 8
FF = 1024
KF = FF // P
CAP = int(N / E1 * 1.25) + 1


REC = (0, 17, 29, T)
PIECES = (T - 1) // 4
OUT_STEPS = (28, 29, 30, 31, 32, 33, 34, 35)
VV_BANKS = (1, 2, 1)
Z_BANKS = (3, 2, 0)
SIDE_BANKS = [3 + q % 5 for q in range(26)]
LN_BANKS = {1: (5, 6, 7, 5, 7), 2: (0, 1, 2, 3, 4), 3: (5, 0, 1, 6, 7), 4: (5, 6, 7, 5, 6)}
LOGIT_BANKS = (0, 1, 6, 7)
WARM_START, WARM_NORM1, WARM_NORM2, WARM_SCORES, WARM_SOFTMAX, WARM_LAST = 2, 4, 2, 2, 2, 3
WARM_STEP, WARM_GATE, WARM_PICK = 2, 8, 6


def slot_tile(unit):
    c, i = unit // NT - 1, unit % NT
    return 4 * c + i if 0 <= c < CH and i < 4 else None


def bc(ap, axis, n):
    a = ap.unsqueeze(axis)
    shape = list(a.shape)
    shape[axis] = n
    return a.broadcast_to(shape)


def tower(nc, A, out):
    ctx = ExitStack()
    with ctx:
        def sb(name, shape, dt=F32):
            return ctx.enter_context(nc.sbuf_tensor(name, shape, dt))

        sems = {}

        def sig(name):
            if name not in sems:
                sems[name] = ctx.enter_context(nc.semaphore(name))
            return sems[name]

        ps = ctx.enter_context(nc.psum_tensor("ps", [P, 8, 512], F32))

        h = sb("h", [P, NT, D])
        hb = sb("hb", [P, NT, D])
        xn = sb("xn", [P, NT, D])
        xnT = sb("xnT", [P, KD, N])
        ident = sb("ident", [P, P])
        ones = sb("ones", [P, P])
        neg_half = sb("neg_half", [P, NT])
        stats = sb("stats", [P, NT, 2, 6])
        mv = sb("mv", [P, NT, 2])
        veps = sb("veps", [P, NT])
        rstd = sb("rstd", [P, NT])
        regA = sb("regA", [P, 20480])
        regB = sb("regB", [P, 13400])

        def carve(reg, at, shape):
            n = int(np.prod(shape))
            ap = reg[:, at:at + n]
            names = [f"d{i}" for i in range(len(shape))]
            if len(shape) > 1:
                ap = ap.rearrange(f"p ({' '.join(names)}) -> p {' '.join(names)}",
                                  **{k: s for k, s in zip(names[1:], shape[1:])})
            return ap, at + n

        at = 0
        patch, at = carve(regA, at, [NT, PD])
        tokW, at = carve(regA, at, [KP, D])
        tokWg, at = carve(regA, at, [KP, D])
        lnb_w, at = carve(regA, at, [KP, P])
        pe2, at = carve(regA, at, [NT, D])
        brow, at = carve(regA, at, [D])
        tok_bias, at = carve(regA, at, [D])
        ln2g, at = carve(regA, at, [D])
        ln2b, at = carve(regA, at, [D])
        lng, at = carve(regA, at, [KP])
        lnb, at = carve(regA, at, [KP])
        clsA, at = carve(regA, at, [D])
        clsB, at = carve(regA, at, [D])
        assert at <= 20480
        patchT, at = carve(regB, 0, [KP, N])

        w_att = sb("w_att", [P, 4, KD, D])
        wq, wk, wv, wo = (w_att[:, i] for i in range(4))
        bq = sb("bq", [P, KD])
        bk = sb("bk", [P, KD])
        bv = sb("bv", [P, KD])
        bo = sb("bo", [P, D])
        lam = sb("lam", [P, 1])
        gmask = sb("gmask", [P, 2, T])
        parity = sb("parity", [P, 2])
        qb, at = carve(regB, 0, [KD, B, T])
        kbd, at = carve(regB, at, [KD, B, 2, T])
        soft, at = carve(regB, at, [2, H, T])
        smax, at = carve(regB, at, [2, H])
        ssum, at = carve(regB, at, [2, H])
        assert at <= 13400
        at = 0
        prob, at = carve(regA, at, [2, H, 64])
        probT, at = carve(regA, at, [2, H // 2, PR])
        vbd, at = carve(regA, at, [2, 2, H // 2, 2, HD])
        attT, at = carve(regA, at, [KD, N])

        phi = sb("phi", [P, KD, NS])
        phib = sb("phib", [P, NS])
        yt = sb("yt", [P, ST, D])
        logit, at = carve(regA, 0, [NT, NS])
        combT, at = carve(regA, at, [ST, N])
        disp, at = carve(regB, 0, [2, NT, CS])
        ew, at = carve(regB, at, [4, 4, KD, D])
        assert at <= 13400
        xt = hb[:, 0:2, :]
        xtT = hb[:, 2:4, :].rearrange("p a (k n) -> p a k n", k=KD)
        dmax = sb("dmax", [P, 2, CE])
        dsum = sb("dsum", [P, 2, CE])
        cmax = sb("cmax", [P, NT, SL])
        csum = sb("csum", [P, NT, SL])
        xmv = sb("xmv", [P, 2, 4])
        xstats = sb("xstats", [P, 2, 6])

        w_in = w_att[:].rearrange("p a k n -> p (a k n)").rearrange("p (k n) -> p k n", k=KD)
        w_lam = phi[:].rearrange("p k n -> p (k n)")[:, 0:KI * DI].rearrange("p (k n) -> p k n", k=KI)
        w_v = phi[:].rearrange("p k n -> p (k n)")[:, KI * DI:2 * KI * DI].rearrange("p (k n) -> p k n", k=KI)
        w_out = phib[:, 0:KI * D].rearrange("p (k n) -> p k n", k=KI)
        va, at = carve(regB, 0, [T, 2, KI, B])
        kk, at = carve(regB, at, [T, KI, B])
        hist, at = carve(regB, at, [T, KI, B])
        zs, at = carve(regB, at, [KI, N])
        assert at <= 13400
        xi, at = carve(regA, 16384, [T, KI, B])
        assert at <= 20480
        l1_small = sb("l1_small", [P, 3, KI])
        omega, bl, bv1 = (l1_small[:, i] for i in range(3))
        sp_t = sb("sp_t", [P, 6, KI])
        bl_half = sb("bl_half", [P, KI])
        inv_vv = xn[:].rearrange("p t d -> p (t d)")[:, 0:N]
        prodg = sb("prodg", [P, 2, KI, B])
        dot = sb("dot", [P, B])
        hk = sb("hk", [P, KI, B])

        w_ff, _ = carve(regA, 0, [4, 2 * KD * FF])
        at = 0
        pick, at = carve(regB, at, [NT, E1 * CAP])
        slotT, at = carve(regB, at, [KD, E1 * CAP])
        hid, at = carve(regB, at, [2, KF, CAP])
        ysb, at = carve(regB, at, [2, D])
        diag, at = carve(regB, at, [NT, P])
        sid_row, at = carve(regB, at, [N])
        gate, at = carve(regB, at, [8, NT, E1])
        assert at <= 13400
        phiflat = phi[:].rearrange("p k n -> p (k n)")

        def pickT(e):
            if e < 6:
                return phiflat[0:CAP, e * N:(e + 1) * N]
            return phib[0:CAP, (e - 6) * N:(e - 5) * N]

        yflat = yt[:].rearrange("p s d -> p (s d)")
        slot_iota = yflat[:, 0:E1 * CAP]
        order = yflat[:, E1 * CAP:E1 * CAP + NT * N // 2].bitcast(BF16).rearrange("p (t n) -> p t n", t=NT)
        b2w = w_att[:].rearrange("p a k n -> p (a k n)").rearrange("p (e d) -> p e d", e=E1)
        wg = sb("wg", [P, KD, E1])
        b1c = sb("b1c", [P, E1, KF])
        gconst = sb("gconst", [P, 2, E1])
        oh16 = sb("oh16", [P, NT, E1], BF16)
        tok = sb("tok", [P, 8, NT])

        block = ctx.enter_context(nc.Block())

        @block.sync
        def _(sp):
            def load(name, dst, src):
                sp.dma_start(dst, src).then_inc(sig(name), 16)

            for t in range(NT):
                lo = CLS if t == 0 else 0
                load(f"patch_loaded{t}", patch[lo:ROWS[t], t, :],
                     A["patches"][t * P + lo - CLS:t * P + ROWS[t] - CLS, :])
                if t == 0:
                    load("ident_loaded", ident[:], A["ident"])
                    load("ln1_loaded", lng, A["ln1_g"])
                    load("ln1_loaded", lnb, A["ln1_b"])
                    load("tokw_loaded", tokW, A["tok_w"])
            load("rows_loaded", tok_bias, A["tok_bias"].partition_broadcast(P))
            load("rows_loaded", ln2g, A["ln2_g"].partition_broadcast(P))
            load("rows_loaded", ln2b, A["ln2_b"].partition_broadcast(P))
            load("pe_loaded", pe2, A["pe"])
            load("cls_loaded", clsA[0:CLS], A["cls_a"])
            load("cls_loaded", clsB[0:CLS], A["cls_b"])
            for n, w in (("wq", wq), ("wk", wk), ("wv", wv), ("wo", wo)):
                load(n + "_loaded", w[:], A[n])
            for n, w in (("bq", bq), ("bk", bk), ("bv", bv), ("gmask", gmask), ("parity", parity)):
                load("att_small_loaded", w[:], A[n])
            load("att_small_loaded", bo[:], A["bo"].partition_broadcast(P))
            load("att_small_loaded", lam[:], A["lam"].partition_broadcast(P))
            load("l1_small_loaded", l1_small[:], A["l1_small"])
            load("phi_loaded", phi[:], A["phi"])
            load("phib_loaded", phib[:], A["phi_b"].partition_broadcast(P))
            eb = A["expert_b"].rearrange("(s j) h -> j s h", j=4)
            for j in range(4):
                load("expert_b_loaded", yt[32 * j:32 * j + 32], eb[j].partition_broadcast(32))
            sp.wait_ge(sig("att_ready"), G)
            for s in range(ST):
                if s == 1:
                    sp.wait_ge(sig("att_out_psum"), NT)
                    load("w_in_loaded", w_in, A["w_in"])
                if s >= 4:
                    sp.wait_ge(sig("y_psum"), s - 3)
                load(f"experts_loaded{s % 4}", ew[:, s % 4], A["expert_w"][s])
            sp.wait_ge(sig("l_psum"), CH * NT)
            load("w_lam_loaded", w_lam, A["w_lam"])
            load("w_v_loaded", w_v, A["w_v"])
            sp.wait_ge(sig("l_read"), CH * NT)
            load("w_out_loaded", w_out, A["w_out"])
            for n, w in (("wg", wg), ("b1c", b1c), ("gconst", gconst)):
                load("gate_small_loaded", w[:], A[n])

            def load_expert(e):
                ring = w_ff[:, e % 4]
                sp.dma_start(ring[:, 0:KD * FF], A["w1"][e]).then_inc(sig(f"ff_loaded{e % 4}"), 16)
                sp.dma_start(ring[:, KD * FF:2 * KD * FF], A["w2"][e]).then_inc(sig(f"ff_loaded{e % 4}"), 16)

            sp.wait_ge(sig("moe_psum"), NT)
            load("slot_iota_loaded", slot_iota, A["slot_iota"].partition_broadcast(P))
            load("order_loaded", order, A["order"])
            for e in range(4):
                load_expert(e)
            sp.wait_ge(sig("side_psum"), 21)
            load("b2_loaded", b2w, A["b2"].partition_broadcast(P))
            for e in range(4, E1):
                sp.wait_ge(sig("ff_y_psum"), e - 3)
                load_expert(e)
            for t in range(NT):
                sp.wait_ge(sig("h_final"), t + 1)
                sp.dma_start(out[t * P:t * P + ROWS[t], :], h[0:ROWS[t], t, :]).then_inc(sig("out_stored"), 16)
            sp.wait_ge(sig("out_stored"), 16 * NT)

        @block.vector
        def _(dve):
            steps = [0]

            def link(ins):
                steps[0] += 1
                ins.then_inc(sig("dve_step"), 1)
                dve.wait_ge(sig("dve_step"), steps[0])

            def mark(ins):
                steps[0] += 1
                ins.then_inc(sig("dve_step"), 1)
                return steps[0]

            def after(value):
                dve.wait_ge(sig("dve_step"), value)

            def row_stats(t, rows, parts, done):
                for i, part in enumerate(parts):
                    ins = dve.bn_stats(stats[0:rows, t, i, :], part)
                link(ins)
                n = len(parts)
                dve.bn_aggr(mv[0:rows, t, :], stats[0:rows, t, 0:n, :].rearrange("p a b -> p (a b)"))\
                    .then_inc(sig(done), 1)

            def ln_stats(t):
                row_stats(t, ROWS[t], [h[0:ROWS[t], t, :]], "ln_var")

            def ln_norm(k, t):
                r = ROWS[t]
                dve.wait_ge(sig("ln_rstd"), NT * (k - 1) + t + 1)
                dve.tensor_scalar(xn[0:r, t, :], h[0:r, t, :], mv[0:r, t, 0:1], rstd[0:r, t:t + 1],
                                  ALU.subtract, ALU.mult).then_inc(sig("ln_xn"), 1)

            def finish_tile(k, t, finish):
                link(finish(t))
                ln_stats(t)
                if t:
                    ln_norm(k, t - 1)

            def finish_tiles(k, finish):
                for t in range(NT):
                    finish_tile(k, t, finish)
                ln_norm(k, NT - 1)

            dve.memset(neg_half[:], -0.5).then_inc(sig("neg_half_set"), 1)
            dve.memset(ones[:], 1.0).then_inc(sig("ones_set"), 1)
            link(dve.memset(patch[0:CLS, 0, :], 0.0))

            def normalise_patch(t):
                r = ROWS[t]
                dve.wait_ge(sig("patch_rstd"), t + 1)
                dve.tensor_scalar(patch[0:r, t, :], patch[0:r, t, :], mv[0:r, t, 0:1], rstd[0:r, t:t + 1],
                                  ALU.subtract, ALU.mult).then_inc(sig("patch_xhat"), 1)

            def patchT_copy(t):
                r = ROWS[t]
                dve.wait_ge(sig("patchT_psum"), 2 * t + 2)
                dve.tensor_copy(patchT[:, 3:6, t * P:t * P + r],
                                ps[:, (2 * t + 1) % 6, 0:3 * r].rearrange("p (k n) -> p k n", k=3))\
                    .then_inc(sig("patchT_b"), 1)

            def z_stats(t):
                r = ROWS[t]
                z = ps[0:r, 7 - t % 2, 0:D]
                dve.wait_ge(sig("z_psum"), t + 1)
                row_stats(t, r, [z], "z_var")
                dve.wait_ge(sig("z_var"), t + 1)
                dve.scalar_tensor_tensor(h[0:r, t, :], z, mv[0:r, t, 0:1], ln2g[0:r], ALU.subtract, ALU.mult)\
                    .then_inc(sig("z_read"), 1)

            def z_finish(t):
                r = ROWS[t]
                dve.wait_ge(sig("z_read"), t + 1)
                dve.wait_ge(sig("z_rstd"), t + 1)
                dve.wait_ge(sig("pe2_done"), t + 1)
                ins = dve.scalar_tensor_tensor(h[0:r, t, :], h[0:r, t, :], rstd[0:r, t:t + 1], pe2[0:r, t],
                                               ALU.mult, ALU.add)
                if t == 0:
                    link(ins)
                    dve.wait_ge(sig("cls_loaded"), 32)
                    ins = dve.tensor_tensor(h[0:CLS, 0, :], clsA[0:CLS], clsB[0:CLS], ALU.add)
                return ins

            for t in range(NT):
                dve.wait_ge(sig(f"patch_loaded{t}"), 16)
                r = ROWS[t]
                row_stats(t, r, [patch[0:r, t, 0:384], patch[0:r, t, 384:768]], "patch_var")
                if t == 0:
                    normalise_patch(0)
                if t >= 2:
                    normalise_patch(t - 1)
                if t == 2:
                    dve.wait_ge(sig("brow_psum"), 1)
                    dve.wait_ge(sig("rows_loaded"), 48)
                    dve.tensor_tensor(brow, ps[:, 6, 0:D], tok_bias, ALU.add).then_inc(sig("brow_done"), 1)
                if t >= 2:
                    patchT_copy(t - 2)
                if t >= 3:
                    z_stats(t - 3)
            normalise_patch(NT - 1)
            patchT_copy(NT - 2)
            z_stats(2)
            patchT_copy(NT - 1)

            for t in range(NT):
                link(z_finish(t))
                ln_stats(t)
                if t + 3 < NT:
                    z_stats(t + 3)
                if t:
                    ln_norm(1, t - 1)
            ln_norm(1, NT - 1)

            dve.wait_ge(sig("att_small_loaded"), 16 * 7)
            dve.tensor_scalar(gmask[:], gmask[:], lam[:, 0:1], None, ALU.mult)
            for n in range(2):
                for m in range(KD):
                    i = 2 * m + n
                    dve.wait_ge(sig("k_psum"), KD * n + m + 1)
                    for e in range(2):
                        ins = dve.tensor_scalar(kbd[:, m, :, e, n * HT:(n + 1) * HT].rearrange("p b s -> p s b"),
                                                ps[:, 4 + i, 0:HN].rearrange("p (s b) -> p s b", b=B),
                                                bk[:, m:m + 1], parity[:, e:e + 1], ALU.add, ALU.mult)
                    ins.then_inc(sig("k_ready"), 1)

            dve.wait_ge(sig("q_ready"), 4)
            dve.memset(ps[32:64, 0:4, 0:4 * T], 0.0).then_inc(sig("score_pad"), 1)

            def scores(g):
                s = g % 2
                dve.wait_ge(sig("s_psum"), g + 1)
                if g >= 2:
                    dve.wait_ge(sig("exp_done"), g - 1)
                dve.tensor_tensor(soft[0:PR, s].rearrange("p (f r e) k -> p r f (e k)", f=KD, e=2),
                                  ps[0:PR, 0:4, 0:4 * T].rearrange("p r (f x) -> p r f x", f=KD),
                                  bc(bc(gmask[0:PR].rearrange("p e k -> p (e k)"), 1, KD), 1, 4), ALU.add)\
                    .then_inc(sig("s_read"), 1)
                dve.wait_ge(sig("s_read"), g + 1)
                link(dve.tensor_reduce(smax[0:PR, s], soft[0:PR, s], AX.X, ALU.max))
                dve.tensor_tensor(soft[0:PR, s], soft[0:PR, s], bc(smax[0:PR, s], 2, T), ALU.subtract)\
                    .then_inc(sig("s_shifted"), 1)

            def normalise(g):
                s = g % 2
                dve.wait_ge(sig("exp_done"), g + 1)
                link(dve.tensor_reduce(ssum[0:PR, s], prob[0:PR, s, :, 0:T], AX.X, ALU.add))
                link(dve.reciprocal(ssum[0:PR, s], ssum[0:PR, s]))
                dve.tensor_tensor(prob[0:PR, s, :, 0:T], prob[0:PR, s, :, 0:T], bc(ssum[0:PR, s], 2, T),
                                  ALU.mult).then_inc(sig("p_ready"), 1)

            for g in range(G):
                scores(g)
                if g >= 1:
                    normalise(g - 1)
            normalise(G - 1)

            def attention_out(t):
                r = ROWS[t]
                dve.wait_ge(sig("att_out_psum"), t + 1)
                return dve.tensor_tensor(h[0:r, t, :], ps[0:r, t, 0:D], hb[0:r, t, :], ALU.add)

            dve.wait_ge(sig("hb_done"), NT)
            finish_tiles(2, attention_out)

            def unit(u):
                c, t, q = u // NT, u % NT, u % 2
                r = ROWS[t]
                if u < CH * NT:
                    kept = logit[0:r, t, c * CS:(c + 1) * CS]
                    by_expert = kept.rearrange("p (n s) -> p n s", s=SL)
                    dve.wait_ge(sig("l_psum"), u + 1)
                    dve.tensor_tensor(kept, ps[0:r, LOGIT_BANKS[u % 4], :], phib[0:r, c * CS:(c + 1) * CS], ALU.add)\
                        .then_inc(sig("l_read"), 1)
                slot_variance(slot_tile(u - 2))
                if u >= 1:
                    pc, pt = (u - 1) // NT, (u - 1) % NT
                    pr = ROWS[pt]
                    e = disp[0:pr, pc % 2, pt].rearrange("p (n s) -> p n s", s=SL)
                    dve.wait_ge(sig("d_exp"), u)
                    summed = mark(dve.tensor_reduce(dsum[0:pr, 1 - q], e, AX.X, ALU.add))
                if u < CH * NT:
                    dve.wait_ge(sig("l_read"), u + 1)
                    top = mark(dve.tensor_reduce(dmax[0:r, q], by_expert, AX.X, ALU.max))
                slot_scale(slot_tile(u - 2))
                expert_outputs(slot_tile(u - 3))
                if u >= 1:
                    after(summed)
                    inverse = mark(dve.reciprocal(dsum[0:pr, 1 - q], dsum[0:pr, 1 - q]))
                if u < CH * NT:
                    after(top)
                    if c >= 2:
                        dve.wait_ge(sig("x_psum"), 4 * (c - 1))
                    dve.tensor_tensor(disp[0:r, c % 2, t].rearrange("p (n s) -> p n s", s=SL), by_expert,
                                      bc(dmax[0:r, q], 2, SL), ALU.subtract).then_inc(sig("d_shifted"), 1)
                    slot_clip(slot_tile(u - 1))
                if u >= 1:
                    after(inverse)
                    dve.tensor_tensor(e, e, bc(dsum[0:pr, 1 - q], 2, SL), ALU.mult).then_inc(sig("d_ready"), 1)
                if u < CH * NT:
                    slot_stats(slot_tile(u - 1))

            def slot_clip(s):
                if s is None:
                    return
                q = s % 2
                dve.wait_ge(sig("x_psum"), s + 1)
                if s >= 2:
                    dve.wait_ge(sig("xT_psum"), s - 1)
                dve.tensor_scalar(xt[:, q], ps[:, 2 + q, 0:D], -33000.0, 65000.0, ALU.max, ALU.min)\
                    .then_inc(sig("x_read"), 1)

            def slot_stats(s):
                if s is None:
                    return
                dve.wait_ge(sig("x_read"), s + 1)
                dve.bn_stats(xstats[:, s % 2], xt[:, s % 2]).then_inc(sig("x_stats"), 1)

            def slot_variance(s):
                if s is None:
                    return
                dve.wait_ge(sig("x_stats"), s + 1)
                dve.bn_aggr(xmv[:, s % 2, 0:2], xstats[:, s % 2]).then_inc(sig("x_var"), 1)

            def slot_inputs(s):
                slot_clip(s)
                slot_stats(s)
                slot_variance(s)

            def slot_scale(s):
                if s is None:
                    return
                q = s % 2
                dve.wait_ge(sig("x_rstd"), s + 1)
                dve.scalar_tensor_tensor(xmv[:, q, 3:4], xmv[:, q, 0:1], -1.0, xmv[:, q, 2:3], ALU.mult, ALU.mult)\
                    .then_inc(sig("x_scale"), 1)

            def expert_outputs(s):
                if s is None:
                    return
                dve.wait_ge(sig("y_psum"), s + 1)
                dve.tensor_tensor(yt[:, s], ps[:, 5, 0:D], yt[:, s], ALU.add).then_inc(sig("y_read"), 1)

            def combine_views(t):
                r = ROWS[t]
                return (logit[0:r, t].rearrange("p (n s) -> p s n", s=SL),
                        logit[0:r, t].rearrange("p (n s) -> p n s", s=SL))

            def combine_max(t):
                by_place, _ = combine_views(t)
                dve.tensor_reduce(cmax[0:ROWS[t], t], by_place, AX.X, ALU.max).then_inc(sig("c_max"), 1)

            def combine_shift(t):
                _, by_expert = combine_views(t)
                dve.wait_ge(sig("c_max"), t + 1)
                dve.tensor_tensor(by_expert, by_expert, bc(cmax[0:ROWS[t], t], 1, NE0), ALU.subtract)\
                    .then_inc(sig("c_shifted"), 1)

            def combine_sum(t):
                r = ROWS[t]
                by_place, _ = combine_views(t)
                dve.wait_ge(sig("c_exp"), t + 1)
                link(dve.tensor_reduce(csum[0:r, t], by_place, AX.X, ALU.add))
                dve.reciprocal(csum[0:r, t], csum[0:r, t]).then_inc(sig("c_inverse"), 1)

            def combine_divide(t):
                _, by_expert = combine_views(t)
                dve.wait_ge(sig("c_inverse"), t + 1)
                dve.tensor_tensor(by_expert, by_expert, bc(csum[0:ROWS[t], t], 1, NE0), ALU.mult)\
                    .then_inc(sig("c_ready"), 1)

            dve.wait_ge(sig("phib_loaded"), 16)
            dve.wait_ge(sig("expert_b_loaded"), 64)
            for u in range(CH * NT + 1):
                unit(u)
            s = ST - 4
            combine_max(0)
            combine_shift(0)
            expert_outputs(s - 1)
            slot_inputs(s)
            combine_max(1)
            slot_scale(s)
            slot_inputs(s + 1)
            combine_shift(1)
            slot_scale(s + 1)
            expert_outputs(s)
            slot_inputs(s + 2)
            combine_sum(0)
            slot_scale(s + 2)
            slot_inputs(s + 3)
            expert_outputs(s + 1)
            combine_divide(0)
            slot_scale(s + 3)
            expert_outputs(s + 2)
            combine_max(2)
            expert_outputs(s + 3)
            combine_shift(2)
            for t in range(1, NT):
                combine_sum(t)
                combine_divide(t)
                if t + 2 < NT:
                    combine_max(t + 2)
                    combine_shift(t + 2)

            def moe_out(t):
                r = ROWS[t]
                dve.wait_ge(sig("moe_psum"), t + 1)
                return dve.tensor_tensor(h[0:r, t, :], ps[0:r, t, 0:D], h[0:r, t, :], ALU.add)

            finish_tiles(3, moe_out)

            def part(n, m, whole):
                return whole[:, REC[n]:REC[n + 1], m, :]

            def times(bank, n):
                return ps[:, bank, 0:B * (REC[n + 1] - REC[n])].rearrange("p (s b) -> p s b", b=B)

            absneg, e, lnw, wm1, inv, sp_out = (sp_t[:, i] for i in range(6))
            dve.wait_ge(sig("l1_small_loaded"), 16)
            link(dve.tensor_scalar(absneg, omega, -1.0, None, ALU.mult))
            dve.tensor_tensor(absneg, absneg, omega, ALU.min).then_inc(sig("sp_abs"), 1)
            dve.wait_ge(sig("sp_exp"), 1)
            dve.tensor_scalar(wm1, e, 1.0, None, ALU.add).then_inc(sig("sp_w"), 1)
            dve.wait_ge(sig("sp_ln"), 1)
            link(dve.tensor_scalar(wm1, wm1, -1.0, None, ALU.add))
            link(dve.tensor_scalar(inv, wm1, 1e-30, None, ALU.max))
            link(dve.reciprocal(inv, inv))
            link(dve.tensor_tensor(lnw, lnw, inv, ALU.mult))
            link(dve.tensor_tensor(lnw, lnw, e, ALU.mult))
            link(dve.tensor_scalar(inv, wm1, 0.0, None, ALU.is_equal))
            link(dve.tensor_tensor(inv, inv, e, ALU.mult))
            link(dve.tensor_scalar(wm1, wm1, 0.0, None, ALU.is_gt))
            link(dve.tensor_tensor(lnw, lnw, wm1, ALU.mult))
            link(dve.tensor_tensor(lnw, lnw, inv, ALU.add))
            link(dve.tensor_scalar(sp_out, omega, 0.0, None, ALU.max))
            link(dve.tensor_tensor(sp_out, sp_out, lnw, ALU.add))
            dve.tensor_scalar(bl_half[:], bl, 0.5, None, ALU.mult)
            dve.tensor_scalar(sp_out, sp_out, -4.0, None, ALU.mult).then_inc(sig("decay_ready"), 1)
            for i in range(1, 8, 2):
                dve.wait_ge(sig("xi_psum"), i + 1)
                dve.tensor_copy(xi[:, (i // KI) * HT:(i // KI + 1) * HT, i % KI],
                                ps[:, i, 0:HN].rearrange("p (s b) -> p s b", b=B)).then_inc(sig("xi_odd"), 1)

            def flat(a):
                return a.rearrange("p s k b -> p s (k b)")

            def coefficients(piece, i):
                t0 = 4 * piece + 1
                t1 = t0 + 4 if piece < PIECES - 1 else T
                n = int(t0 >= REC[1]) + int(t0 >= REC[2])
                if i == 0:
                    dve.wait_ge(sig("vv_psum"), n + 1)
                    lo = B * (t0 - REC[n])
                    ins = dve.reciprocal(inv_vv[:, B * t0:B * t1], ps[:, VV_BANKS[n], lo:lo + B * (t1 - t0)])
                if i == 1:
                    dve.wait_ge(sig("lam_ready"), KI * (n + 1))
                    ins = dve.scalar_tensor_tensor(flat(kk[:, t0:t1]), flat(va[:, t0:t1, 0]), -2.0,
                                                   flat(va[:, t0:t1, 1]), ALU.mult, ALU.mult)
                if i == 2:
                    dve.wait_ge(sig("coefficients_done"), 4 * piece + 2)
                    ins = dve.tensor_tensor(kk[:, t0:t1], kk[:, t0:t1],
                                            bc(inv_vv[:, B * t0:B * t1].rearrange("p (s b) -> p s b", b=B), 2, KI),
                                            ALU.mult)
                if i == 3:
                    ins = dve.scalar_tensor_tensor(flat(xi[:, t0:t1]), flat(va[:, t0:t1, 1]), -1.0,
                                                   flat(xi[:, t0:t1]), ALU.add, ALU.mult)
                ins.then_inc(sig("coefficients_done"), 1)

            def gate_states(t):
                s0, s1 = 8 * t, min(8 * t + 8, T)
                dve.wait_ge(sig("silu_read"), 8)
                zt = zs[:, :, B * s0:B * s1].rearrange("p k (s b) -> p k s b", b=B)
                dve.tensor_tensor(zt, zt, hist[:, s0:s1].rearrange("p s k b -> p k s b"), ALU.mult)\
                    .then_inc(sig("gated"), 1)

            def recurrence_out(t):
                r = ROWS[t]
                dve.wait_ge(sig("rnn_out_psum"), t + 1)
                return dve.tensor_tensor(h[0:r, t, :], ps[0:r, SIDE_BANKS[21 + t], 0:D], h[0:r, t, :], ALU.add)

            def beside(t):
                if t <= 4 * (PIECES - 1):
                    coefficients((t + 3) // 4, (t - 1) % 4)
                if t in (27, 29, 31, 33):
                    gate_states((27, 29, 31, 33).index(t))
                if t in (T - 4, T - 2):
                    recurrence_out((t - (T - 4)) // 2).then_inc(sig("rnn_out_read"), 1)
                if t in (T - 3, T - 1):
                    dve.wait_ge(sig("rnn_out_read"), (t - (T - 3)) // 2 + 1)
                    ln_stats((t - (T - 3)) // 2)

            dve.wait_ge(sig("xi_even"), 4)
            for i in range(4):
                coefficients(0, i)
            dve.tensor_copy(hist[:, 0], xi[:, 0]).then_inc(sig("rnn_state"), 1)
            for t in range(1, T):
                dve.wait_ge(sig("rnn_state"), t)
                dve.tensor_tensor(prodg[:], va[:, t], bc(hist[:, t - 1], 1, 2), ALU.mult)\
                    .then_inc(sig("rnn_prod"), 1)
                dve.wait_ge(sig("rnn_prod"), t)
                dve.tensor_reduce(dot[:], prodg[:, 0].rearrange("p k b -> p b k"), AX.X, ALU.add)\
                    .then_inc(sig("rnn_dot"), 1)
                if t % 4 == 1:
                    dve.wait_ge(sig("coefficients_done"), 4 * min((t + 3) // 4, PIECES))
                dve.tensor_tensor(prodg[:, 1], prodg[:, 1], xi[:, t], ALU.subtract).then_inc(sig("rnn_decayed"), 1)
                beside(t)
                dve.wait_ge(sig("rnn_sum"), t)
                dve.tensor_tensor(hk[:], kk[:, t], bc(ps[:, 0, 0:B], 1, KI), ALU.mult).then_inc(sig("rnn_turned"), 1)
                dve.wait_ge(sig("rnn_turned"), t)
                dve.tensor_tensor(hist[:, t], hk[:], prodg[:, 1], ALU.add).then_inc(sig("rnn_state"), 1)
            dve.wait_ge(sig("rnn_state"), T)
            gate_states(NT - 1)
            ln_norm(4, 0)
            for t in range(2, NT):
                finish_tile(4, t, recurrence_out)
            ln_norm(4, NT - 1)

            lg, _, key, oh, picked, eg = (gate[:, i] for i in range(6))
            top, kmax, sumexp, cw, rank, sid, slot_base, slot_of = (tok[:, i] for i in range(8))
            dve.wait_ge(sig("gate_psum"), 1)
            dve.wait_ge(sig("gate_small_loaded"), 48)
            logits = ps[:, 1, 0:NT * E1].rearrange("p (t e) -> p t e", e=E1)
            link(dve.tensor_reduce(top, logits, AX.X, ALU.max))
            dve.tensor_tensor(lg, logits, bc(top, 2, E1), ALU.subtract).then_inc(sig("gate_shifted"), 1)
            dve.wait_ge(sig("gate_shifted"), 1)
            link(dve.scalar_tensor_tensor(key, lg, 0.0, bc(gconst[:, 0], 1, NT), ALU.is_equal, ALU.mult))
            link(dve.tensor_reduce(kmax, key, AX.X, ALU.max))
            link(dve.tensor_tensor(oh, key, bc(kmax, 2, E1), ALU.is_equal))
            dve.tensor_copy(oh16[:], oh).then_inc(sig("one_hot"), 1)
            dve.tensor_scalar(slot_base, kmax, -float(CAP), float(E1 * CAP), ALU.mult, ALU.add)\
                .then_inc(sig("slot_base_done"), 1)
            dve.wait_ge(sig("rank_psum"), 1)
            link(dve.tensor_tensor(picked, oh, ps[:, 6, 0:NT * E1].rearrange("p (t e) -> p t e", e=E1), ALU.mult))
            link(dve.tensor_reduce(rank, picked, AX.X, ALU.add))
            dve.wait_ge(sig("slot_base_done"), 1)
            link(dve.tensor_tensor(slot_of, slot_base, rank, ALU.add))
            link(dve.scalar_tensor_tensor(sid, rank, float(CAP), slot_of, ALU.is_le, ALU.mult))
            dve.wait_ge(sig("slot_iota_loaded"), 16)
            for n in range(2):
                for t in range(NT):
                    dve.tensor_scalar(pick[:, t, n * 384:(n + 1) * 384], slot_iota[:, n * 384:(n + 1) * 384],
                                      sid[:, t:t + 1], None, ALU.is_equal).then_inc(sig("pick_ready"), 1)
            for t in range(NT):
                dve.tensor_scalar(diag[:, t], ident[:], sid[:, t:t + 1], None, ALU.mult)\
                    .then_inc(sig("diag_ready"), 1)
            dve.wait_ge(sig("gate_exp"), 1)
            link(dve.tensor_reduce(sumexp, eg, AX.X, ALU.add))
            dve.reciprocal(cw, sumexp)
            for i in (2, 3):
                dve.wait_ge(sig("slots_psum"), i + 1)
                dve.tensor_copy(slotT[:, i % 2, 384:768], ps[:, i, 0:384]).then_inc(sig("slots_late"), 1)
            dve.wait_ge(sig("sid_row_ready"), 2)
            for e in range(E1):
                dve.tensor_scalar(pickT(e), sid_row[0:CAP], gconst[0:CAP, 1, e:e + 1], None, ALU.is_equal)\
                    .then_inc(sig("pickT_ready"), 1)
            dve.wait_ge(sig("b2_loaded"), 16)
            for e in range(E1):
                dve.wait_ge(sig("ff_y_psum"), e + 1)
                if e >= 2:
                    dve.wait_ge(sig("ff_added"), e - 1)
                dve.tensor_tensor(ysb[0:CAP, e % 2], ps[0:CAP, 7, 0:D], b2w[0:CAP, e], ALU.add)\
                    .then_inc(sig("ff_y_ready"), 1)
            for t in range(NT):
                r = ROWS[t]
                dve.wait_ge(sig("ff_out_psum"), t + 1)
                dve.scalar_tensor_tensor(h[0:r, t], ps[0:r, t, 0:D], cw[0:r, t:t + 1], h[0:r, t],
                                         ALU.mult, ALU.add).then_inc(sig("h_final"), 1)

        @block.gpsimd
        def _(pool):
            steps = [0]

            def link(ins):
                steps[0] += 1
                ins.then_inc(sig("pool_step"), 1)
                pool.wait_ge(sig("pool_step"), steps[0])

            def inv_sqrt(t, rows, ready, done, base=0):
                pool.wait_ge(sig(ready), base + t + 1)
                link(pool.tensor_scalar(veps[0:rows, t:t + 1], mv[0:rows, t, 1:2], EPS, None, ALU.add))
                pool.tensor_tensor(rstd[0:rows, t:t + 1], veps[0:rows, t:t + 1], neg_half[0:rows, t:t + 1],
                                   ALU.pow).then_inc(sig(done), 1)

            pool.wait_ge(sig("neg_half_set"), 1)
            for t in range(NT):
                inv_sqrt(t, ROWS[t], "patch_var", "patch_rstd")
            def add_beta(t):
                pool.tensor_tensor(pe2[:, t], pe2[:, t], ln2b, ALU.add).then_inc(sig("pe2_done"), 1)

            pool.wait_ge(sig("pe_loaded"), 16)
            pool.wait_ge(sig("rows_loaded"), 48)
            for t in range(3):
                inv_sqrt(t, ROWS[t], "z_var", "z_rstd")
                add_beta(t)
            for t in range(NT):
                inv_sqrt(t, ROWS[t], "ln_var", "ln_rstd", 0 * NT)
                if t + 3 < NT:
                    inv_sqrt(t + 3, ROWS[t + 3], "z_var", "z_rstd")
                    add_beta(t + 3)
            pool.memset(prob, 0.0)
            pool.memset(vbd, 0.0).then_inc(sig("att_pads"), 1)
            pool.wait_ge(sig("att_small_loaded"), 16 * 7)
            for t in range(NT):
                pool.tensor_tensor(hb[0:ROWS[t], t, :], h[0:ROWS[t], t, :], bo[0:ROWS[t]], ALU.add)\
                    .then_inc(sig("hb_done"), 1)

            for t in range(NT):
                inv_sqrt(t, ROWS[t], "ln_var", "ln_rstd", 1 * NT)

            for s in range(ST):
                q = s % 2
                pool.wait_ge(sig("x_var"), s + 1)
                link(pool.tensor_scalar(veps[:, q:q + 1], xmv[:, q, 1:2], EPS, None, ALU.add))
                pool.tensor_tensor(xmv[:, q, 2:3], veps[:, q:q + 1], neg_half[:, 0:1], ALU.pow)\
                    .then_inc(sig("x_rstd"), 1)

            for t in range(NT):
                inv_sqrt(t, ROWS[t], "ln_var", "ln_rstd", 2 * NT)

            for t in range(NT):
                inv_sqrt(t, ROWS[t], "ln_var", "ln_rstd", 3 * NT)

        @block.scalar
        def _(act):
            steps = [0]

            def link(ins):
                steps[0] += 1
                ins.then_inc(sig("act_step"), 1)
                act.wait_ge(sig("act_step"), steps[0])

            def transposed_copies(k):
                for t in range(NT):
                    act.wait_ge(sig("ln_T_psum"), NT * (k - 1) + t + 1)
                    act.activation(xnT[:, :, t * P:t * P + ROWS[t]],
                                   ps[:, LN_BANKS[k][t], 0:KD * ROWS[t]].rearrange("p (k n) -> p k n", k=KD), ACT.Copy)\
                        .then_inc(sig("ln_xnT"), 1)

            act.wait_ge(sig("ln1_loaded"), 32)
            act.activation(lnb_w, bc(lnb, 2, P), ACT.Copy).then_inc(sig("lnb_wide"), 1)
            act.wait_ge(sig("tokw_loaded"), 16)
            for k in range(KP):
                ins = act.activation(tokWg[:, k, :], tokW[:, k, :], ACT.Copy, scale=lng[:, k:k + 1])
            ins.then_inc(sig("tokwg_done"), 1)
            for t in range(NT):
                r = ROWS[t]
                act.wait_ge(sig("patchT_psum"), 2 * t + 1)
                act.activation(patchT[:, 0:3, t * P:t * P + r],
                               ps[:, (2 * t) % 6, 0:3 * r].rearrange("p (k n) -> p k n", k=3), ACT.Copy)\
                    .then_inc(sig("patchT_a"), 1)

            act.wait_ge(sig("att_small_loaded"), 16 * 7)
            link(act.activation(bq[:], bq[:], ACT.Copy, scale=HD ** -0.5))
            transposed_copies(1)
            for n in range(2):
                for m in range(KD):
                    i = 2 * m + n
                    act.wait_ge(sig("q_psum"), KD * n + m + 1)
                    act.activation(qb[:, m, :, n * HT:(n + 1) * HT].rearrange("p b s -> p s b"),
                                   ps[:, i, 0:HN].rearrange("p (s b) -> p s b", b=B),
                                   ACT.Identity, bias=bq[:, m:m + 1], scale=HD ** -0.5)\
                        .then_inc(sig("q_ready"), 1)
            act.wait_ge(sig("att_pads"), 1)

            def values(g):
                s = g % 2
                act.wait_ge(sig("v_psum"), g + 1)
                if g >= 2:
                    act.wait_ge(sig("o_psum"), g - 1)
                for e in range(2):
                    ins = act.activation(
                        vbd[64 * e:64 * e + T, s, :, :, e, :],
                        ps[64 * e:64 * e + T, 4, 0:D].rearrange("p (i j d) -> p i j d", i=2, d=HD), ACT.Copy)
                ins.then_inc(sig("v_ready"), 1)

            def exponent(g):
                s = g % 2
                act.wait_ge(sig("s_shifted"), g + 1)
                if g >= 2:
                    act.wait_ge(sig("pT_psum"), 2 * g - 2)
                act.activation(prob[0:PR, s, :, 0:T], soft[0:PR, s], ACT.Exp).then_inc(sig("exp_done"), 1)

            def probs(g):
                s = g % 2
                for f in range(2):
                    act.wait_ge(sig("pT_psum"), 2 * g + f + 1)
                    if g >= 2:
                        act.wait_ge(sig("o_psum"), g - 1)
                    act.activation(probT[:, s, 4 * f:4 * f + 4, :],
                                   ps[:, 5 + f, :].rearrange("p (j q) -> p j q", q=P)[:, :, 0:PR], ACT.Copy)\
                        .then_inc(sig("pT_ready"), 1)

            def heads_out(g):
                act.wait_ge(sig("o_psum"), g + 1)
                for f in range(KD):
                    ins = act.activation(
                        attT[:, f, :].rearrange("p (s b) -> p b s", b=B)[:, 2 * g:2 * g + 2, :],
                        ps[:, 7, 2 * T * f:2 * T * (f + 1)].rearrange("p (i s) -> p i s", i=2),
                        ACT.Identity, bias=bv[:, f:f + 1])
                ins.then_inc(sig("att_ready"), 1)

            values(0)
            exponent(0)
            for g in range(G):
                if g + 1 < G:
                    exponent(g + 1)
                probs(g)
                if g + 1 < G:
                    values(g + 1)
                heads_out(g)

            transposed_copies(2)

            def exp_dispatch(u):
                c, t = u // NT, u % NT
                r = ROWS[t]
                act.wait_ge(sig("d_shifted"), u + 1)
                act.activation(disp[0:r, c % 2, t], disp[0:r, c % 2, t], ACT.Exp).then_inc(sig("d_exp"), 1)

            def slot_tanh(s):
                if s is None:
                    return
                q = s % 2
                act.wait_ge(sig("x_scale"), s + 1)
                act.activation(xt[:, q], xt[:, q], ACT.Tanh, bias=xmv[:, q, 3:4], scale=xmv[:, q, 2:3])\
                    .then_inc(sig("x_hat"), 1)

            def slot_copy(s):
                if s is None:
                    return
                q = s % 2
                act.wait_ge(sig("xT_psum"), s + 1)
                if s >= 2:
                    act.wait_ge(sig("y_psum"), s - 1)
                act.activation(xtT[:, q], ps[:, 4, 0:KD * P].rearrange("p (k n) -> p k n", k=KD), ACT.Copy)\
                    .then_inc(sig("xT_ready"), 1)

            def exp_combine(t):
                r = ROWS[t]
                act.wait_ge(sig("c_shifted"), t + 1)
                act.activation(logit[0:r, t], logit[0:r, t], ACT.Exp).then_inc(sig("c_exp"), 1)

            def combine_copies(t):
                r = ROWS[t]
                for f in range(4):
                    act.wait_ge(sig("cT_psum"), 4 * t + f + 1)
                    act.activation(combT[:, 4 * f:4 * f + 4, t * P:t * P + r],
                                   ps[:, 6 + f % 2, 0:4 * r].rearrange("p (s n) -> p s n", n=r), ACT.Copy)\
                        .then_inc(sig("cT_ready"), 1)

            for u in range(CH * NT):
                slot_tanh(slot_tile(u - 2))
                slot_copy(slot_tile(u - 2))
                exp_dispatch(u)
            s = ST - 4
            slot_tanh(s - 1)
            slot_copy(s - 1)
            exp_combine(0)
            slot_tanh(s)
            slot_copy(s)
            slot_tanh(s + 1)
            exp_combine(1)
            slot_copy(s + 1)
            slot_tanh(s + 2)
            slot_copy(s + 2)
            slot_tanh(s + 3)
            slot_copy(s + 3)
            combine_copies(0)
            for t in range(1, NT):
                if t + 1 < NT:
                    exp_combine(t + 1)
                combine_copies(t)
            transposed_copies(3)

            def part(n, m, whole):
                return whole[:, REC[n]:REC[n + 1], m, :]

            def times(bank, n):
                return ps[:, bank, 0:B * (REC[n + 1] - REC[n])].rearrange("p (s b) -> p s b", b=B)

            def v_read(m, n, bank, name, read):
                act.activation(part(n, m, va[:, :, 0]), times(bank, n), ACT.Identity, bias=bv1[:, m:m + 1])\
                    .then_inc(sig(name), 1)
                act.wait_ge(sig(name), read)
                act.activation(part(n, m, hist), part(n, m, va[:, :, 0]), ACT.Square).then_inc(sig("v_squared"), 1)

            def lam_read(m, n, bank, name, read):
                act.activation(part(n, m, va[:, :, 1]), times(bank, n), ACT.Tanh, bias=bl_half[:, m:m + 1],
                               scale=0.5).then_inc(sig(name), 1)
                act.wait_ge(sig(name), read)
                act.activation(part(n, m, va[:, :, 1]), part(n, m, va[:, :, 1]), ACT.Exp,
                               scale=sp_t[:, 5, m:m + 1], bias=sp_t[:, 5, m:m + 1]).then_inc(sig("lam_ready"), 1)

            act.wait_ge(sig("sp_abs"), 1)
            act.activation(sp_t[:, 1], sp_t[:, 0], ACT.Exp).then_inc(sig("sp_exp"), 1)
            act.wait_ge(sig("sp_w"), 1)
            act.activation(sp_t[:, 2], sp_t[:, 3], ACT.Ln).then_inc(sig("sp_ln"), 1)
            for i in range(0, 8, 2):
                act.wait_ge(sig("xi_psum"), i + 1)
                act.activation(xi[:, (i // KI) * HT:(i // KI + 1) * HT, i % KI],
                               ps[:, i, 0:HN].rearrange("p (s b) -> p s b", b=B), ACT.Copy)\
                    .then_inc(sig("xi_even"), 1)
            for m in range(KI):
                act.wait_ge(sig("v0_psum"), m + 1)
                v_read(m, 0, m, "v0_read", m + 1)
            act.wait_ge(sig("decay_ready"), 1)
            for m in range(KI):
                act.wait_ge(sig("lam0_psum"), m + 1)
                lam_read(m, 0, 4 + m, "lam0_read", m + 1)
            def z_read(i, bank):
                m, n = i // 2, i % 2
                act.activation(zs[:, m, n * HN:(n + 1) * HN], ps[:, bank, 0:HN], ACT.Silu)\
                    .then_inc(sig("silu_read"), 1)

            for i in range(3):
                act.wait_ge(sig("silu_psum"), i + 1)
                z_read(i, Z_BANKS[i])
            for q in range(21):
                act.wait_ge(sig("side_psum"), q + 1)
                n, m = q // (2 * KI) + 1, q % KI
                if q >= 4 * KI:
                    z_read(3 + q - 4 * KI, SIDE_BANKS[q])
                elif q % (2 * KI) < KI:
                    v_read(m, n, SIDE_BANKS[q], "side_read", q + 1)
                else:
                    lam_read(m, n, SIDE_BANKS[q], "side_read", q + 1)

            transposed_copies(4)

            act.wait_ge(sig("gate_shifted"), 1)
            act.activation(gate[:, 5], gate[:, 0], ACT.Exp).then_inc(sig("gate_exp"), 1)
            for i in (0, 1):
                act.wait_ge(sig("slots_psum"), i + 1)
                act.activation(slotT[:, i, 0:384], ps[:, i, 0:384], ACT.Copy).then_inc(sig("slots_early"), 1)
            for i, (at, n) in enumerate(((0, 4 * P), (4 * P, N - 4 * P))):
                act.wait_ge(sig("sid_psum"), i + 1)
                act.activation(sid_row[:, at:at + n], ps[:, 4 + i, 0:n], ACT.Copy).then_inc(sig("sid_row_ready"), 1)
            for e in range(E1):
                if e >= 2:
                    act.wait_ge(sig("ff_y_psum"), e - 1)
                for f in range(KF):
                    if f % 4 == 0:
                        act.wait_ge(sig("ff_h_psum"), 2 * e + f // 4 + 1)
                    ins = act.activation(hid[:, e % 2, f], ps[:, 5 + f // 4, (f % 4) * CAP:(f % 4 + 1) * CAP],
                                         ACT.Gelu, bias=b1c[:, e, f:f + 1])
                    if f % 4 == 3:
                        ins.then_inc(sig("ff_h_ready"), 1)

        @block.tensor
        def _(pe):
            def keep_warm(n, bank):
                for _ in range(n):
                    pe.matmul(ps[:, bank, 0:P], ident[:], ident[:], start=True, stop=True)

            def transpose_tile(k, t):
                r = ROWS[t]
                pe.wait_ge(sig("ln_xn"), NT * (k - 1) + t + 1)
                bank = LN_BANKS[k][t]
                if bank in LN_BANKS[k][:t]:
                    pe.wait_ge(sig("ln_xnT"), NT * (k - 1) + t - LN_BANKS[k][:t][::-1].index(bank))
                for c in range(KD):
                    ins = pe.transpose(ps[:, bank, c * r:(c + 1) * r], xn[0:r, t, c * P:(c + 1) * P],
                                       ident[0:r, 0:r])
                ins.then_inc(sig("ln_T_psum"), 1)

            pe.wait_ge(sig("ident_loaded"), 16)

            def beta_row():
                pe.wait_ge(sig("lnb_wide"), 1)
                pe.wait_ge(sig("tokw_loaded"), 16)
                for k in range(KP):
                    ins = pe.matmul(ps[:, 6, 0:D], lnb_w[:, k, :], tokW[:, k, :], start=(k == 0), stop=(k == KP - 1))
                ins.then_inc(sig("brow_psum"), 1)

            def patch_product(t):
                r = ROWS[t]
                pe.wait_ge(sig("patchT_a"), t + 1)
                pe.wait_ge(sig("patchT_b"), t + 1)
                if t == 0:
                    pe.wait_ge(sig("tokwg_done"), 1)
                    pe.wait_ge(sig("brow_done"), 1)
                if t >= 2:
                    pe.wait_ge(sig("z_read"), t - 1)
                for k in range(KP):
                    pe.matmul(ps[0:r, 7 - t % 2, 0:D], patchT[:, k, t * P:t * P + r], tokWg[:, k, :],
                              start=(k == 0), stop=False)
                ins = pe.matmul(ps[0:r, 7 - t % 2, 0:D], ones[0:1, 0:r], brow[0:1], start=False, stop=True)
                ins.then_inc(sig("z_psum"), 1)

            for t in range(NT):
                r = ROWS[t]
                pe.wait_ge(sig("patch_xhat"), t + 1)
                for f in range(2):
                    if t >= 3:
                        pe.wait_ge(sig("patchT_b" if f else "patchT_a"), t - 2)
                    for k in range(3):
                        ins = pe.transpose(ps[:, (2 * t + f) % 6, k * r:(k + 1) * r],
                                           patch[0:r, t, (3 * f + k) * P:(3 * f + k + 1) * P], ident[0:r, 0:r])
                    ins.then_inc(sig("patchT_psum"), 1)
                if t == 0:
                    beta_row()
                    keep_warm(WARM_START, 7)
                if t >= 1:
                    patch_product(t - 1)
            patch_product(NT - 1)
            def attention_inputs(w, name, base, n):
                pe.wait_ge(sig(f"w{name}_loaded"), 16)
                for m in range(KD):
                    for k in range(KD):
                        ins = pe.matmul(ps[:, base + 2 * m + n, 0:HN], w[:, k, m * P:(m + 1) * P],
                                        xnT[:, k, n * HN:(n + 1) * HN], start=(k == 0), stop=(k == KD - 1))
                    ins.then_inc(sig(f"{name}_psum"), 1)

            for t in range(NT - 1):
                keep_warm(WARM_NORM1, 4)
                transpose_tile(1, t)
            pe.wait_ge(sig("ln_xnT"), 3)
            attention_inputs(wq, "q", 0, 0)
            attention_inputs(wk, "k", 4, 0)
            transpose_tile(1, NT - 1)
            pe.wait_ge(sig("ln_xnT"), NT)

            attention_inputs(wq, "q", 0, 1)
            attention_inputs(wk, "k", 4, 1)

            def image(ap, b):
                return ap.rearrange("p (s b) -> p b s", b=B)[:, b, :]

            def scores(g):
                if g >= 1:
                    pe.wait_ge(sig("s_read"), g)
                for f in range(KD):
                    for i in range(2):
                        for r in range(4):
                            ins = pe.matmul(ps[64 * i:64 * i + T, r, 2 * T * f:2 * T * (f + 1)],
                                            qb[32 * r:32 * r + 32, f, 2 * g + i, :],
                                            kbd[32 * r:32 * r + 32, f, 2 * g + i].rearrange("p e k -> p (e k)"),
                                            start=True, stop=True)
                ins.then_inc(sig("s_psum"), 1)

            def values(g):
                if g >= 1:
                    pe.wait_ge(sig("v_ready"), g)
                for i in range(2):
                    for k in range(KD):
                        for e in range(2):
                            ins = pe.matmul(
                                ps[64 * e:64 * e + T, 4, i * P:(i + 1) * P],
                                image(xnT[:, k, :], 2 * g + i),
                                wv[:, k, :].rearrange("p (j e d) -> p e j d", e=2, d=HD)[:, e],
                                start=(k == 0), stop=(k == KD - 1))
                ins.then_inc(sig("v_psum"), 1)

            def prob_transposes(g):
                s = g % 2
                keep_warm(WARM_SOFTMAX if g < G - 1 else WARM_LAST, 5)
                pe.wait_ge(sig("p_ready"), g + 1)
                for f in range(2):
                    if g >= 1:
                        pe.wait_ge(sig("pT_ready"), 2 * g - 1 + f)
                    for j in range(4):
                        hh = 2 * (4 * f + j)
                        ins = pe.transpose(ps[:, 5 + f, j * P:(j + 1) * P],
                                           prob[:, s, hh:hh + 2, :].rearrange("p a k -> p (a k)"), ident[:])
                    ins.then_inc(sig("pT_psum"), 1)

            def heads(g):
                s = g % 2
                pe.wait_ge(sig("v_ready"), g + 1)
                if g >= 1:
                    pe.wait_ge(sig("att_ready"), g)
                pe.wait_ge(sig("pT_ready"), 2 * g + 2)
                for f in range(2):
                    for i in range(2):
                        for j in range(4):
                            ins = pe.matmul(
                                ps[32 * j:32 * j + 32, 7, (2 * f + i) * T:(2 * f + i + 1) * T],
                                vbd[0:PR, s, i, 4 * f + j].rearrange("p e d -> p (e d)"),
                                probT[0:PR, s, 4 * f + j, 64 * i:64 * i + T], start=True, stop=True)
                ins.then_inc(sig("o_psum"), 1)

            pe.wait_ge(sig("k_ready"), 1)
            pe.wait_ge(sig("wv_loaded"), 16)
            values(0)
            pe.wait_ge(sig("k_ready"), 4)
            pe.wait_ge(sig("score_pad"), 1)
            keep_warm(WARM_SCORES, 5)
            scores(0)
            keep_warm(WARM_SCORES, 5)
            scores(1)
            for g in range(G):
                if g + 2 < G:
                    scores(g + 2)
                prob_transposes(g)
                if g + 1 < G:
                    values(g + 1)
                heads(g)
            pe.wait_ge(sig("att_ready"), G)
            pe.wait_ge(sig("wo_loaded"), 16)

            def project(t):
                r = ROWS[t]
                for k in range(KD):
                    ins = pe.matmul(ps[0:r, t, 0:D], attT[:, k, t * P:t * P + r], wo[:, k, :],
                                    start=(k == 0), stop=(k == KD - 1))
                ins.then_inc(sig("att_out_psum"), 1)

            for t in range(NT):
                project(t)
                if t >= 2:
                    transpose_tile(2, t - 2)
            keep_warm(WARM_NORM2, 5)
            transpose_tile(2, NT - 2)

            def logits(u):
                c, t, q = u // NT, u % NT, LOGIT_BANKS[u % 4]
                r = ROWS[t]
                if u < NT:
                    pe.wait_ge(sig("ln_xnT"), NT + u + 1)
                if u >= 4:
                    pe.wait_ge(sig("l_read"), u - 3)
                for k in range(KD):
                    ins = pe.matmul(ps[0:r, q, :], xnT[:, k, t * P:t * P + r], phi[:, k, c * CS:(c + 1) * CS],
                                    start=(k == 0), stop=(k == KD - 1))
                ins.then_inc(sig("l_psum"), 1)

            def slot_inputs(s):
                if s is None:
                    return
                c, i = s // 4, s % 4
                pe.wait_ge(sig("d_ready"), NT * (c + 1))
                if s >= 2:
                    pe.wait_ge(sig("x_read"), s - 1)
                for t in range(NT):
                    r = ROWS[t]
                    ins = pe.matmul(ps[:, 2 + s % 2, 0:D], disp[0:r, c % 2, t, i * P:(i + 1) * P], xn[0:r, t, :],
                                    start=(t == 0), stop=(t == NT - 1))
                ins.then_inc(sig("x_psum"), 1)

            def slot_transposes(s):
                if s is None:
                    return
                pe.wait_ge(sig("x_hat"), s + 1)
                if s:
                    pe.wait_ge(sig("xT_ready"), s)
                for k in range(KD):
                    ins = pe.transpose(ps[:, 4, k * P:(k + 1) * P], xt[:, s % 2, k * P:(k + 1) * P], ident[:])
                ins.then_inc(sig("xT_psum"), 1)

            def experts(s):
                if s is None:
                    return
                pe.wait_ge(sig("xT_ready"), s + 1)
                pe.wait_ge(sig(f"experts_loaded{s % 4}"), 16 * (s // 4 + 1))
                if s:
                    pe.wait_ge(sig("y_read"), s)
                for k in range(KD):
                    for j in range(4):
                        ins = pe.matmul(ps[32 * j:32 * j + 32, 5, 0:D], xtT[:, s % 2, k, 32 * j:32 * j + 32],
                                        ew[:, s % 4, j, k, :], start=(k == 0), stop=(k == KD - 1))
                ins.then_inc(sig("y_psum"), 1)

            def combine_transposes(t):
                r = ROWS[t]
                pe.wait_ge(sig("c_ready"), t + 1)
                for f in range(4):
                    if 4 * t + f >= 2:
                        pe.wait_ge(sig("cT_ready"), 4 * t + f - 1)
                    for i in range(4):
                        s = 4 * f + i
                        ins = pe.transpose(ps[:, 6 + f % 2, i * r:(i + 1) * r],
                                           logit[0:r, t, s * P:(s + 1) * P], ident[0:r, 0:r])
                    ins.then_inc(sig("cT_psum"), 1)

            def combine(t):
                r = ROWS[t]
                for s in range(ST):
                    if s % 4 == 0:
                        pe.wait_ge(sig("cT_ready"), 4 * t + s // 4 + 1)
                    if t == NT - 1 and s == ST // 2:
                        for done in range(NT - 2):
                            transpose_tile(3, done)
                    ins = pe.matmul(ps[0:r, t, 0:D], combT[:, s, t * P:t * P + r], yt[:, s, :],
                                    start=(s == 0), stop=(s == ST - 1))
                ins.then_inc(sig("moe_psum"), 1)

            pe.wait_ge(sig("phi_loaded"), 16)
            logits(0)
            transpose_tile(2, NT - 1)
            logits(1)
            logits(2)
            for u in range(CH * NT):
                if u + 3 < CH * NT:
                    logits(u + 3)
                slot_transposes(slot_tile(u - 2))
                if u % NT:
                    slot_inputs(slot_tile(u))
                experts(slot_tile(u - 2))
                if u % NT == 0:
                    slot_inputs(slot_tile(u))
            s = ST - 4
            slot_transposes(s - 1)
            slot_inputs(s)
            experts(s - 1)
            slot_inputs(s + 1)
            slot_inputs(s + 2)
            for i in range(4):
                slot_transposes(s + i)
                experts(s + i)
                if i == 0:
                    slot_inputs(s + 3)
            pe.wait_ge(sig("y_read"), ST)

            for t in range(NT):
                combine_transposes(t)
                combine(t)
            transpose_tile(3, NT - 2)

            def cols(n):
                return B * (REC[n + 1] - REC[n])

            def x_product(m, n, bank, k):
                return pe.matmul(ps[:, bank, 0:HN], w_in[:, k, m * P:(m + 1) * P],
                                 xnT[:, k, n * HN:(n + 1) * HN], start=(k == 0), stop=(k == KD - 1))

            def xi_product(w, m, n, bank, k):
                return pe.matmul(ps[:, bank, 0:cols(n)], w[:, k, m * P:(m + 1) * P],
                                 xi[:, REC[n]:REC[n + 1], k, :], start=(k == 0), stop=(k == KI - 1))

            def vv_product(n, k):
                ins = pe.matmul(ps[:, VV_BANKS[n], 0:cols(n)], ones[:], hist[:, REC[n]:REC[n + 1], k, :],
                                start=(k == 0), stop=(k == KI - 1))
                if k == KI - 1:
                    ins.then_inc(sig("vv_psum"), 1)

            def z_product(m, n, bank, k):
                return pe.matmul(ps[:, bank, 0:HN], w_in[:, k, DI + m * P:DI + (m + 1) * P],
                                 xnT[:, k, n * HN:(n + 1) * HN], start=(k == 0), stop=(k == KD - 1))

            pe.wait_ge(sig("w_in_loaded"), 16)
            pe.wait_ge(sig("ln_xnT"), 2 * NT + 3)
            for i in range(8):
                if i == KI:
                    transpose_tile(3, NT - 1)
                    pe.wait_ge(sig("ln_xnT"), NT * 3)
                for k in range(KD):
                    ins = x_product(i % KI, i // KI, i, k)
                ins.then_inc(sig("xi_psum"), 1)
            pe.wait_ge(sig("xi_even"), 2)
            pe.wait_ge(sig("xi_odd"), 2)
            pe.wait_ge(sig("w_v_loaded"), 16)
            for m in range(KI):
                for k in range(KI):
                    ins = xi_product(w_v, m, 0, m, k)
                ins.then_inc(sig("v0_psum"), 1)
            pe.wait_ge(sig("xi_even"), 4)
            pe.wait_ge(sig("xi_odd"), 4)
            pe.wait_ge(sig("w_lam_loaded"), 16)
            for m in range(KI):
                if m == KI - 1:
                    pe.wait_ge(sig("v_squared"), KI)
                    for k in range(KI):
                        vv_product(0, k)
                for k in range(KI):
                    ins = xi_product(w_lam, m, 0, 4 + m, k)
                ins.then_inc(sig("lam0_psum"), 1)

            def side(i):
                if i < 18 * KI:
                    n, j = i // (9 * KI) + 1, i % (9 * KI)
                    if j >= 8 * KI:
                        if j == 8 * KI:
                            pe.wait_ge(sig("v_squared"), KI * (n + 1))
                        if n == 2 and j == 8 * KI:
                            pe.wait_ge(sig("coefficients_done"), 4 * 3 + 1)
                        vv_product(n, j - 8 * KI)
                        return
                    q, k, last = 2 * KI * (n - 1) + j // KI, j % KI, KI - 1
                else:
                    q, k, last = 4 * KI + (i - 18 * KI) // KD, (i - 18 * KI) % KD, KD - 1
                bank = SIDE_BANKS[q]
                if k == 0:
                    if q == 0:
                        pe.wait_ge(sig("v0_read"), KI)
                    elif q < 5:
                        pe.wait_ge(sig("lam0_read"), q)
                    elif q - 5 < 4 * KI:
                        pe.wait_ge(sig("side_read"), q - 4)
                    if q == 0:
                        pe.wait_ge(sig("silu_read"), 1)
                if q >= 4 * KI:
                    z = 3 + q - 4 * KI
                    ins = z_product(z // 2, z % 2, bank, k)
                else:
                    ins = xi_product(w_v if q % (2 * KI) < KI else w_lam, q % KI, n, bank, k)
                if k == last:
                    ins.then_inc(sig("side_psum"), 1)

            def recurrence_out(t, k):
                r = ROWS[t]
                if k == 0:
                    pe.wait_ge(sig("gated"), t + 1)
                    if t == 0:
                        pe.wait_ge(sig("w_out_loaded"), 16)
                        pe.wait_ge(sig("silu_read"), 8)
                ins = pe.matmul(ps[0:r, SIDE_BANKS[21 + t], 0:D], zs[:, k, t * P:t * P + r], w_out[:, k, :],
                                start=(k == 0), stop=(k == KI - 1))
                if k == KI - 1:
                    ins.then_inc(sig("rnn_out_psum"), 1)

            def gate_logits(t):
                r = ROWS[t]
                if t == 0:
                    pe.wait_ge(sig("gate_small_loaded"), 48)
                pe.wait_ge(sig("ln_xnT"), 3 * NT + t + 1)
                for k in range(KD):
                    ins = pe.matmul(ps[0:r, 1, t * E1:(t + 1) * E1], xnT[:, k, t * P:t * P + r], wg[:, k, :],
                                    start=(k == 0), stop=(k == KD - 1))
                if t == NT - 1:
                    ins.then_inc(sig("gate_psum"), 1)

            pe.wait_ge(sig("v0_read"), KI)
            for i in range(3):
                for k in range(KD):
                    ins = z_product(i // 2, i % 2, Z_BANKS[i], k)
                ins.then_inc(sig("silu_psum"), 1)
            pe.wait_ge(sig("silu_read"), 3)
            for t in range(1, T):
                pe.wait_ge(sig("rnn_dot"), t)
                pe.matmul(ps[:, 0, 0:B], ones[:], dot[:], start=True, stop=True).then_inc(sig("rnn_sum"), 1)
                if t <= 12:
                    for i in range(3 * t - 3, 3 * t):
                        side(i)
                elif t <= 21:
                    for i in range(4 * t - 16, 4 * t - 12):
                        side(i)
                elif t <= 26:
                    side(28 + 2 * t)
                    side(29 + 2 * t)
                elif t not in OUT_STEPS:
                    keep_warm(WARM_STEP, 2)
                if t in OUT_STEPS:
                    i = OUT_STEPS.index(t)
                    for k in (0, 1) if i % 2 == 0 else (2, 3):
                        recurrence_out(i // 2, k)
            for k in range(KI):
                recurrence_out(4, k)
            for t in range(NT):
                transpose_tile(4, t)
                if t:
                    gate_logits(t - 1)
            gate_logits(NT - 1)

            keep_warm(WARM_GATE, 7)
            pe.wait_ge(sig("one_hot"), 1)
            pe.wait_ge(sig("order_loaded"), 16)
            for t in range(NT):
                r = ROWS[t]
                for j in range(NT):
                    ins = pe.matmul(ps[0:r, 6, t * E1:(t + 1) * E1], order[0:ROWS[j], j, t * P:t * P + r],
                                    oh16[0:ROWS[j], j, :], start=(j == 0), stop=(j == NT - 1))
            ins.then_inc(sig("rank_psum"), 1)
            keep_warm(WARM_PICK, 7)
            for i in range(4):
                n, m = i // 2, i % 2
                for t in range(NT):
                    r = ROWS[t]
                    if m == 0:
                        pe.wait_ge(sig("pick_ready"), NT * n + t + 1)
                    ins = pe.matmul(ps[:, i, 0:384], xn[0:r, t, m * P:(m + 1) * P],
                                    pick[0:r, t, n * 384:(n + 1) * 384], start=(t == 0), stop=(t == NT - 1))
                ins.then_inc(sig("slots_psum"), 1)
            pe.wait_ge(sig("diag_ready"), NT)
            for t in range(NT):
                r = ROWS[t]
                ins = pe.matmul(ps[:, 4 + t // 4, (t % 4) * P:(t % 4) * P + r], ones[0:r, :], diag[0:r, t, 0:r],
                                start=True, stop=True)
                if t >= 3:
                    ins.then_inc(sig("sid_psum"), 1)

            def hidden(e):
                w1 = w_ff[:, e % 4, 0:KD * FF].rearrange("p (k f) -> p k f", k=KD)
                pe.wait_ge(sig(f"ff_loaded{e % 4}"), 32 * (e // 4 + 1))
                for f in range(KF):
                    if e and f % 4 == 0:
                        pe.wait_ge(sig("ff_h_ready"), 2 * e - 1 + f // 4)
                    for k in range(KD):
                        ins = pe.matmul(ps[:, 5 + f // 4, (f % 4) * CAP:(f % 4 + 1) * CAP], w1[:, k, f * P:(f + 1) * P],
                                        slotT[:, k, e * CAP:(e + 1) * CAP], start=(k == 0), stop=(k == KD - 1))
                    if f % 4 == 3:
                        ins.then_inc(sig("ff_h_psum"), 1)

            def outputs(e):
                w2 = w_ff[:, e % 4, KD * FF:].rearrange("p (k d) -> p k d", k=KF)
                pe.wait_ge(sig("ff_h_ready"), 2 * e + 2)
                if e:
                    pe.wait_ge(sig("ff_y_ready"), e)
                for f in range(KF):
                    ins = pe.matmul(ps[0:CAP, 7, 0:D], hid[:, e % 2, f], w2[:, f, :],
                                    start=(f == 0), stop=(f == KF - 1))
                ins.then_inc(sig("ff_y_psum"), 1)

            def add_back(e):
                pe.wait_ge(sig("ff_y_ready"), e + 1)
                for t in range(NT):
                    r = ROWS[t]
                    ins = pe.matmul(ps[0:r, t, 0:D], pickT(e)[:, t * P:t * P + r], ysb[0:CAP, e % 2],
                                    start=(e == 0), stop=(e == E1 - 1))
                    if e == E1 - 1:
                        ins.then_inc(sig("ff_out_psum"), 1)
                if e < E1 - 1:
                    ins.then_inc(sig("ff_added"), 1)

            pe.wait_ge(sig("slots_early"), 2)
            pe.wait_ge(sig("slots_late"), 2)
            pe.wait_ge(sig("sid_row_ready"), 2)
            hidden(0)
            pe.wait_ge(sig("pickT_ready"), E1)
            for e in range(E1):
                if e + 1 < E1:
                    hidden(e + 1)
                outputs(e)
                if e:
                    add_back(e - 1)
            add_back(E1 - 1)


def kernel(x, cls_tok, L0_tok_cls_token, L0_tok_cls_pos_embedding, L0_tok_ln1_g, L0_tok_ln1_b, L0_tok_W,
           L0_tok_bias, L0_tok_ln2_g, L0_tok_ln2_b, L0_attn_Wq, L0_attn_bq, L0_attn_Wk, L0_attn_bk, L0_attn_Wv,
           L0_attn_bv, L0_attn_Wo, L0_attn_bo, L0_attn_prior_lambda, L0_ffn_phi_w, L0_ffn_phi_b,
           L0_ffn_expert_w, L0_ffn_expert_b, L1_attn_omega, L1_attn_Win, L1_attn_Wl, L1_attn_bl, L1_attn_Wv,
           L1_attn_bv, L1_attn_Wout, L1_ffn_wg, L1_ffn_W1, L1_ffn_b1, L1_ffn_W2, L1_ffn_b2):
    import concourse.bacc as bacc
    from concourse.bass_utils import run_bass_kernel_spmd

    def arr(a):
        return np.asarray(a)

    def tiled(w):
        w = arr(w)
        return w.reshape(w.shape[0] // P, P, w.shape[1]).transpose(1, 0, 2)

    def col(v):
        return arr(v).reshape(-1, P).T

    patches = arr(x).reshape(B, 3, 6, 16, 6, 16).transpose(2, 4, 0, 1, 3, 5).reshape(B * NP, PD)

    def by_channel(w):
        return arr(w).reshape(16 * 16, 3, -1).transpose(1, 0, 2).reshape(PD, -1)

    omega = (1.0 / 10000.0 ** (np.arange(D // 4, dtype=np.float32) / (D // 4 - 1))).astype(np.float32)
    gy, gx = np.meshgrid(np.arange(6), np.arange(6), indexing="ij")
    ya = gy.reshape(-1)[:, None] * omega[None, :]
    xa = gx.reshape(-1)[:, None] * omega[None, :]
    pe = np.concatenate((np.sin(xa), np.cos(xa), np.sin(ya), np.cos(ya)), axis=1).astype(np.float32)
    pe_rows = np.zeros((NT * P, D), np.float32)
    pe_rows[CLS:N] = np.repeat(pe, B, axis=0)
    time = np.arange(T)
    delta = np.abs(time[:, None] - time[None, :]).astype(np.float32)
    gauss = np.zeros((T, T), np.float32)
    for period, weight, sigma in ((1.0, 0.8, 0.5), (30.0, 0.4, 2.0)):
        gauss = gauss + np.float32(weight) * np.exp(-(delta - np.float32(period)) ** 2 / np.float32(2.0 * sigma ** 2))
    gmask = np.zeros((P, 2, T), np.float32)
    gmask[0:T] = gauss[:, None]
    gmask[64:64 + T] = gauss[:, None]
    parity = (np.arange(P)[:, None] // HD % 2 == np.arange(2)[None, :]).astype(np.float32)

    ins = {
        "patches": patches,
        "ident": np.eye(P, dtype=np.float32),
        "ln1_g": by_channel(L0_tok_ln1_g)[:, 0].reshape(KP, P).T,
        "ln1_b": by_channel(L0_tok_ln1_b)[:, 0].reshape(KP, P).T,
        "tok_w": tiled(by_channel(L0_tok_W)),
        "tok_bias": arr(L0_tok_bias), "ln2_g": arr(L0_tok_ln2_g), "ln2_b": arr(L0_tok_ln2_b),
        "pe": pe_rows.reshape(NT, P, D).transpose(1, 0, 2),
        "cls_a": np.repeat(np.concatenate([arr(cls_tok)[0], arr(L0_tok_cls_token)[0]]), B, axis=0),
        "cls_b": np.repeat(np.concatenate([np.zeros((1, D), np.float32), arr(L0_tok_cls_pos_embedding)[0]]), B, axis=0),
        "wq": tiled(arr(L0_attn_Wq).T), "wk": tiled(arr(L0_attn_Wk).T),
        "wv": tiled(arr(L0_attn_Wv).T), "wo": tiled(arr(L0_attn_Wo).T),
        "bq": col(L0_attn_bq), "bk": col(L0_attn_bk), "bv": col(L0_attn_bv), "bo": arr(L0_attn_bo),
        "lam": arr(L0_attn_prior_lambda).reshape(1), "gmask": gmask, "parity": parity,
    }
    ew = arr(L0_ffn_expert_w).reshape(ST, 4, KD, P, D).transpose(0, 3, 1, 2, 4)
    ins |= {"phi": tiled(arr(L0_ffn_phi_w).T), "phi_b": arr(L0_ffn_phi_b), "expert_b": arr(L0_ffn_expert_b),
            "expert_w": ew,
            "l1_small": np.stack([col(arr(L1_attn_omega).reshape(-1)), col(L1_attn_bl), col(L1_attn_bv)], axis=1),
            "w_in": tiled(arr(L1_attn_Win).T), "w_lam": tiled(arr(L1_attn_Wl).T), "w_v": tiled(arr(L1_attn_Wv).T),
            "w_out": tiled(arr(L1_attn_Wout).T)}
    rank_of = (np.arange(B)[None, :] * T + time[:, None]).reshape(-1)
    before = np.zeros((NT * P, N), np.float32)
    before[:N] = rank_of[:, None] <= rank_of[None, :]
    e8 = np.arange(E1, dtype=np.float32)
    gconst = np.zeros((P, 2, E1), np.float32)
    gconst[:, 0] = E1 - e8
    gconst[:, 1] = 1 + np.arange(P, dtype=np.float32)[:, None] + CAP * e8
    ins |= {
        "wg": tiled(L1_ffn_wg), "gconst": gconst, "slot_iota": np.arange(1, E1 * CAP + 1, dtype=np.float32),
        "order": before.reshape(NT, P, N).transpose(1, 0, 2).astype(mybir.dt.np(BF16)),
        "w1": arr(L1_ffn_W1).reshape(E1, KD, P, FF).transpose(0, 2, 1, 3).reshape(E1, P, KD * FF),
        "w2": arr(L1_ffn_W2).reshape(E1, KF, P, D).transpose(0, 2, 1, 3).reshape(E1, P, KF * D),
        "b1c": arr(L1_ffn_b1).reshape(E1, KF, P).transpose(2, 0, 1), "b2": arr(L1_ffn_b2),
    }
    nc = bacc.Bacc("TRN2", target_bir_lowering=False, num_devices=1)
    arrays, A = {}, {}
    for name, a in ins.items():
        a = np.ascontiguousarray(a)
        arrays["in_" + name] = a
        A[name] = nc.dram_tensor("in_" + name, a.shape, mybir.dt.from_np(a.dtype), kind="ExternalInput").ap()
    out = nc.dram_tensor("out_rows", (N, D), F32, kind="ExternalOutput").ap()
    tower(nc, A, out)
    r = run_bass_kernel_spmd(nc, [arrays], core_ids=[0])
    rows = r.results[0]["out_rows"]
    return np.ascontiguousarray(rows.reshape(T, B, D).transpose(1, 0, 2))
```
